# Optimizing a Trainium2 kernel written in Bass

```python
import numpy as np
import jax
import jax.numpy as jnp

def _softmax(x, axis=-1):
    return jax.nn.softmax(x, axis=axis)

def _gelu(x):
    return jax.nn.gelu(x, approximate=True)

def _silu(x):
    return jax.nn.silu(x)

def _sigmoid(x):
    return jax.nn.sigmoid(x)

def _layernorm(x, axis=-1, eps=1e-05):
    m = jnp.mean(x, axis=axis, keepdims=True)
    v = jnp.var(x, axis=axis, keepdims=True)
    return (x - m) / jnp.sqrt(v + eps)

def _scatter_add(tgt, idx, src, axis=0):
    return tgt.at[idx].add(src)

def _segment_sum(src, seg, n):
    return jax.ops.segment_sum(src, seg, n)
kernel_name = 'mk_xattn_ffn_d2_seqx_r8_a788ac'

def setup_inputs(seed: int=0):
    np.random.seed(seed)
    _w = jnp.asarray

    def _rec_inputs():
        import jax
        import jax.numpy as jnp
        _rk = jax.random.key(seed)
        x = 7.22e-05 + 1 * jax.random.normal(jax.random.fold_in(_rk, 1), (32, 128, 128), jnp.float32)
        _lenS = 128 - jax.random.randint(jax.random.fold_in(_rk, 7), (32,), 0, max(1, 128 // 4) + 1, jnp.int32)
        _lenS2 = 128 - jax.random.randint(jax.random.fold_in(_rk, 8), (32,), 0, max(1, 128 // 4) + 1, jnp.int32)
        _ctx_768P = jax.random.normal(jax.random.fold_in(_rk, 11), (32, 16, 96), jnp.float32)
        _ctx_768c = jax.random.dirichlet(jax.random.fold_in(_rk, 511), 0.3 * jnp.ones((16,), jnp.float32), (32, 128))
        _ctx_768t = jnp.einsum('bsk,bkd->bsd', _ctx_768c, _ctx_768P)
        _ctx_768t = _ctx_768t * jax.lax.rsqrt(jnp.mean(jnp.square(_ctx_768t)) + 1e-12) * 0.953939
        ctx_768 = 2.09791e-05 + 1.00001 * (_ctx_768t + 0.3 * jax.random.normal(jax.random.fold_in(_rk, 611), (32, 128, 96), jnp.float32))
        _validS = jnp.arange(128)[None, :] < _lenS[:, None]
        _validS2 = jnp.arange(128)[None, :] < _lenS2[:, None]
        _causal = jnp.tril(jnp.ones((128, 128), dtype=bool))
        mask_BxS_bk0 = jnp.logical_not(jnp.broadcast_to(_validS[:, :], (32, 128)))
        return (x, ctx_768, mask_BxS_bk0)
    x, ctx_768, mask_BxS_bk0 = _rec_inputs()

    def _L0_xattn_setup():
        import jax, jax.numpy as jnp
        import numpy as np
        NUM_HEADS = 16
        key = jax.random.key(seed)
        k1, k2, k3, k4, k5 = jax.random.split(key, 5)
        B, N, C = (4, 256, 128)
        N2, Cy = (128, 96)
        x = jax.random.normal(k1, (B, N, C), dtype=jnp.float32)
        y = jax.random.normal(k2, (B, N2, Cy), dtype=jnp.float32)
        pad_mask = jax.random.randint(k3, (B, N), 0, 2).astype(jnp.bool_)
        Wq = jax.random.normal(k4, (C, C), dtype=jnp.float32) * C ** (-0.5)
        Wkv = jax.random.normal(k5, (2 * C, Cy), dtype=jnp.float32) * Cy ** (-0.5)
        return {'x': x, 'y': y, 'pad_mask': pad_mask, 'Wq': Wq, 'Wkv': Wkv}
    _L0_xattn_all = _L0_xattn_setup()
    _L0_xattn_in = {k: v for k, v in _L0_xattn_all.items() if k in ('Wq', 'Wkv')}
    del _L0_xattn_all

    def _L0_ffn_setup():
        import math
        import jax, jax.numpy as jnp
        import numpy as np
        E = 8
        K = 2
        CF = 1.25
        D = 128
        F = 256
        B, S = (4, 256)
        key = jax.random.key(seed)
        ks = jax.random.split(key, 8)
        sd = 1.0 / math.sqrt(D)
        sf = 1.0 / math.sqrt(F)
        return {'x': jax.random.normal(ks[0], (B, S, D), jnp.float32), 'router_w': jax.random.normal(ks[1], (D, E), jnp.float32) * sd, 'router_b': jnp.zeros((E,), jnp.float32), 'w1': jax.random.normal(ks[2], (E, D, F), jnp.float32) * sd, 'b1': jax.random.normal(ks[3], (E, F), jnp.float32) * 0.01, 'w2': jax.random.normal(ks[4], (E, F, D), jnp.float32) * sf, 'b2': jax.random.normal(ks[5], (E, D), jnp.float32) * 0.01}
    _L0_ffn_all = _L0_ffn_setup()
    _L0_ffn_in = {k: v for k, v in _L0_ffn_all.items() if k in ('router_w', 'router_b', 'w1', 'b1', 'w2', 'b2')}
    del _L0_ffn_all

    def _L1_xattn_setup():
        import jax, jax.numpy as jnp
        import numpy as np
        N_HEADS = 16
        D_HEAD = 64
        key = jax.random.key(seed)
        ks = jax.random.split(key, 7)
        B, SQ, SKV = (2, 256, 256)
        D_MODEL, D_COND, D_ATTN = (128, 96, N_HEADS * D_HEAD)
        return {'x': jax.random.normal(ks[0], (B, SQ, D_MODEL), jnp.float32), 'cond': jax.random.normal(ks[1], (B, SKV, D_COND), jnp.float32), 'w_q': jax.random.normal(ks[2], (D_MODEL, D_ATTN), jnp.float32) * D_MODEL ** (-0.5), 'w_k': jax.random.normal(ks[3], (D_COND, D_ATTN), jnp.float32) * D_COND ** (-0.5), 'w_v': jax.random.normal(ks[4], (D_COND, D_ATTN), jnp.float32) * D_COND ** (-0.5), 'w_out': jax.random.normal(ks[5], (D_ATTN, D_MODEL), jnp.float32) * D_ATTN ** (-0.5), 'b_out': jnp.zeros((D_MODEL,), jnp.float32)}
    _L1_xattn_all = _L1_xattn_setup()
    _L1_xattn_in = {k: v for k, v in _L1_xattn_all.items() if k in ('w_q', 'w_k', 'w_v', 'w_out', 'b_out')}
    del _L1_xattn_all

    def _L1_ffn_setup():
        import jax, jax.numpy as jnp
        import numpy as np
        E = 16
        H = 128
        F = 256
        TOP_K = 1
        B, S = (2, 128)
        key = jax.random.key(seed)
        ks = jax.random.split(key, 7)
        s = 0.02
        return {'hidden_states': jax.random.normal(ks[0], (B, S, H), jnp.float32), 'w_router': jax.random.normal(ks[1], (E, H), jnp.float32) * s, 'gate_up_proj': jax.random.normal(ks[2], (E, H, 2 * F), jnp.float32) * s, 'down_proj': jax.random.normal(ks[3], (E, F, H), jnp.float32) * s, 'w_gate': jax.random.normal(ks[4], (F, H), jnp.float32) * s, 'w_up': jax.random.normal(ks[5], (F, H), jnp.float32) * s, 'w_down': jax.random.normal(ks[6], (H, F), jnp.float32) * s}
    _L1_ffn_all = _L1_ffn_setup()
    _L1_ffn_in = {k: v for k, v in _L1_ffn_all.items() if k in ('w_router', 'gate_up_proj', 'down_proj', 'w_gate', 'w_up', 'w_down')}
    del _L1_ffn_all
    return {'x': x, 'ctx_768': ctx_768, 'mask_BxS_bk0': mask_BxS_bk0, 'L0_xattn_Wq': _L0_xattn_in['Wq'], 'L0_xattn_Wkv': _L0_xattn_in['Wkv'], 'L0_ffn_router_w': _L0_ffn_in['router_w'], 'L0_ffn_router_b': _L0_ffn_in['router_b'], 'L0_ffn_w1': _L0_ffn_in['w1'], 'L0_ffn_b1': _L0_ffn_in['b1'], 'L0_ffn_w2': _L0_ffn_in['w2'], 'L0_ffn_b2': _L0_ffn_in['b2'], 'L1_xattn_w_q': _L1_xattn_in['w_q'], 'L1_xattn_w_k': _L1_xattn_in['w_k'], 'L1_xattn_w_v': _L1_xattn_in['w_v'], 'L1_xattn_w_out': _L1_xattn_in['w_out'], 'L1_xattn_b_out': _L1_xattn_in['b_out'], 'L1_ffn_w_router': _L1_ffn_in['w_router'], 'L1_ffn_gate_up_proj': _L1_ffn_in['gate_up_proj'], 'L1_ffn_down_proj': _L1_ffn_in['down_proj'], 'L1_ffn_w_gate': _L1_ffn_in['w_gate'], 'L1_ffn_w_up': _L1_ffn_in['w_up'], 'L1_ffn_w_down': _L1_ffn_in['w_down']}

def reference(x, ctx_768, mask_BxS_bk0, L0_xattn_Wq, L0_xattn_Wkv, L0_ffn_router_w, L0_ffn_router_b, L0_ffn_w1, L0_ffn_b1, L0_ffn_w2, L0_ffn_b2, L1_xattn_w_q, L1_xattn_w_k, L1_xattn_w_v, L1_xattn_w_out, L1_xattn_b_out, L1_ffn_w_router, L1_ffn_gate_up_proj, L1_ffn_down_proj, L1_ffn_w_gate, L1_ffn_w_up, L1_ffn_w_down):
    import jax
    import jax.numpy as jnp

    def _L0_xattn_ref(x, y, pad_mask, Wq, Wkv):
        import jax, jax.numpy as jnp
        import numpy as np
        NUM_HEADS = 16
        B, N, C = x.shape
        N2 = y.shape[1]
        H = NUM_HEADS
        d = C // H
        scale = d ** (-0.5)
        q = (x @ Wq.T).reshape(B, N, H, d).transpose(0, 2, 1, 3)
        kv = (y @ Wkv.T).reshape(B, N2, 2, H, d).transpose(2, 0, 3, 1, 4)
        k, v = (kv[0], kv[1])
        attn = jnp.einsum('bhnd,bhmd->bhnm', q * scale, k)
        attn = jnp.where(pad_mask[:, None, :, None], attn, jnp.float32(-1000000000.0))
        attn = jax.nn.softmax(attn, axis=-1)
        out = jnp.einsum('bhnm,bhmd->bhnd', attn, v)
        return out.transpose(0, 2, 1, 3).reshape(B, N, C)

    def _L0_ffn_ref(x, router_w, router_b, w1, b1, w2, b2):
        import math
        import jax, jax.numpy as jnp
        import numpy as np
        E = 8
        K = 2
        CF = 1.25
        D = 128
        F = 256
        B, S = (4, 256)
        b, s, d = x.shape
        xf = x.reshape(-1, d)
        T = b * s
        A = T * K
        cap = max(1, int(math.ceil(CF * A / E)))
        logits = xf @ router_w + router_b
        probs = jax.nn.softmax(logits, axis=-1)
        topk_p, topk_i = jax.lax.top_k(probs, K)
        topk_p = topk_p / jnp.clip(topk_p.sum(-1, keepdims=True), 1e-09)
        a_tok = jnp.repeat(jnp.arange(T), K)
        a_exp = topk_i.reshape(-1)
        a_w = topk_p.reshape(-1)
        order = jnp.argsort(a_exp)
        se, st, sw = (a_exp[order], a_tok[order], a_w[order])
        counts = jnp.bincount(se, length=E)
        starts = jnp.cumsum(counts) - counts
        rank = jnp.arange(A) - starts[se]
        keep = rank < cap
        slot = jnp.where(keep, se * cap + rank, E * cap)
        buf = jnp.zeros((E * cap + 1, d), x.dtype).at[slot].set(xf[st])
        buf = buf[:-1].reshape(E, cap, d)
        h = jax.nn.gelu(jnp.einsum('ecd,edf->ecf', buf, w1) + b1[:, None, :], approximate=False)
        eo = jnp.einsum('ecf,efd->ecd', h, w2) + b2[:, None, :]
        eo_flat = jnp.concatenate([eo.reshape(E * cap, d), jnp.zeros((1, d), x.dtype)], axis=0)
        w = jnp.where(keep, sw, 0.0)[:, None]
        out = jnp.zeros_like(xf).at[st].add(eo_flat[slot] * w)
        return out.reshape(b, s, d)

    def _L1_xattn_ref(x, cond, w_q, w_k, w_v, w_out, b_out):
        import jax, jax.numpy as jnp
        import numpy as np
        N_HEADS = 16
        D_HEAD = 64
        B, SQ, _ = x.shape
        SKV = cond.shape[1]
        scale = D_HEAD ** (-0.5)
        q = (x @ w_q).reshape(B, SQ, N_HEADS, D_HEAD)
        k = (cond @ w_k).reshape(B, SKV, N_HEADS, D_HEAD)
        v = (cond @ w_v).reshape(B, SKV, N_HEADS, D_HEAD)
        attn = jnp.einsum('bqhd,bkhd->bhqk', q, k) * scale
        attn = jax.nn.softmax(attn, axis=-1)
        out = jnp.einsum('bhqk,bkhd->bqhd', attn, v).reshape(B, SQ, N_HEADS * D_HEAD)
        return out @ w_out + b_out

    def _L1_ffn_ref(hidden_states, w_router, gate_up_proj, down_proj, w_gate, w_up, w_down):
        import jax, jax.numpy as jnp
        import numpy as np
        E = 16
        H = 128
        F = 256
        TOP_K = 1
        B, S = (2, 128)
        b, s, h = hidden_states.shape
        x = hidden_states.reshape(-1, h)
        logits = x @ w_router.T
        _, top_idx = jax.lax.top_k(logits, TOP_K)
        mask = jax.nn.one_hot(top_idx, E, dtype=logits.dtype).sum(axis=1)
        scores = jax.nn.sigmoid(logits) * mask
        masked_inputs = scores.T[:, :, None] * x[None, :, :]
        gate_up = jnp.einsum('eth,ehf->etf', masked_inputs, gate_up_proj)
        gate, up = jnp.split(gate_up, 2, axis=-1)
        expert_out = jnp.einsum('etf,efh->eth', up * jax.nn.silu(gate), down_proj)
        shared = jax.nn.silu(x @ w_gate.T) * (x @ w_up.T) @ w_down.T
        out = shared + expert_out.sum(axis=0)
        return out.reshape(b, s, h)
    x = x + _L0_xattn_ref(_layernorm(x, axis=-1), ctx_768, mask_BxS_bk0, L0_xattn_Wq, L0_xattn_Wkv)
    x = x + _L0_ffn_ref(_layernorm(x, axis=-1), L0_ffn_router_w, L0_ffn_router_b, L0_ffn_w1, L0_ffn_b1, L0_ffn_w2, L0_ffn_b2)
    x = x + _L1_xattn_ref(_layernorm(x, axis=-1), ctx_768, L1_xattn_w_q, L1_xattn_w_k, L1_xattn_w_v, L1_xattn_w_out, L1_xattn_b_out)
    x = x + _L1_ffn_ref(_layernorm(x, axis=-1), L1_ffn_w_router, L1_ffn_gate_up_proj, L1_ffn_down_proj, L1_ffn_w_gate, L1_ffn_w_up, L1_ffn_w_down)
    return x

_drawn_inputs = setup_inputs


def setup_inputs(seed=0):
    import zlib

    import numpy as np

    out = dict(_drawn_inputs(seed))
    spreads = {'L0_ffn_router_b': (0.0, 0.1), 'L1_xattn_b_out': (0.0, 0.1)}
    factors = {'L0_ffn_b1': 8.0,
     'L0_ffn_b2': 8.0,
     'L1_ffn_w_router': 8.0,
     'L1_ffn_gate_up_proj': 8.0,
     'L1_ffn_down_proj': 8.0,
     'L1_ffn_w_gate': 8.0,
     'L1_ffn_w_up': 8.0,
     'L1_ffn_w_down': 8.0}
    for name, (base, spread) in spreads.items():
        noise = np.random.default_rng([zlib.crc32(name.encode()), seed]).standard_normal(out[name].shape)
        drawn = base * np.exp(spread * noise) if base else spread * noise
        out[name] = jnp.asarray(drawn.astype(out[name].dtype))
    for name, factor in factors.items():
        out[name] = (out[name] * factor).astype(out[name].dtype)
    return out
```

```python
import numpy as np
import concourse.bass as bass
from concourse import mybir
from contextlib import ExitStack

F32 = mybir.dt.float32
BF16 = mybir.dt.bfloat16
I32 = mybir.dt.int32
U8 = mybir.dt.uint8
ALU = mybir.AluOpType
ACT = mybir.ActivationFunctionType
AX = mybir.AxisListType

NB = 32
P = 128
DM = 128
DC = 96
NH = 16
QH = 4
NQ = NH // QH
D0, D1 = 8, 64
NCH = NH * D1 // P
E0, F0, CAP = 8, 256, 1280
E1, F1 = 16, 256
EPS = 1e-5
LAST = NB - 1


def need(eng, sem, value):
    if isinstance(value, int) and value <= 0:
        return
    eng.wait_ge(sem, value)


def over_batches(eng, body):
    for b in range(-1, 3):
        body((b + 1) // 2, b - 2 * ((b + 1) // 2))
    with eng.Fori(1, NB // 2 - 2) as i:
        body(i, 1)
        body(i, 2)
    for b in range(NB - 3, NB + 1):
        body((b - 1) // 2, 2 - b % 2)


def inside(b):
    return not isinstance(b, int) or 0 <= b <= LAST


FILLS0 = ("xT", "q", "k", "v")
FILLS1 = ("xT", "q0", "q1", "k0", "k1", "v0", "v1", "oT0", "oT1")


def fill0(i, off, name):
    n = FILLS0.index(name)
    return n % 2, 2 * (2 * i + off + 1) + n // 2


def fill1(i, off, name):
    n, b = FILLS1.index(name), 2 * i + off
    short = len(FILLS1) - 2
    if isinstance(b, int):
        if b < 1:
            f = short * (b + 1) + n
        else:
            f = 2 * short + len(FILLS1) * (min(b, LAST) - 1) + (2 * (b - LAST) + n - short if b >= LAST else n)
        return f % 2, f // 2
    f = 2 * short + len(FILLS1) * (off - 1) + n
    return f % 2, f // 2 + len(FILLS1) * i


NT0, PER = E0 * CAP // (2 * P), CAP // (2 * P)
NT1 = NB + E1
ZROW = E0 * CAP
RING = 8


def over_pairs(eng, body):
    for i in range(2):
        body(i, 0)
        body(i, 1)
    with eng.Fori(2, NB // 2) as i:
        body(i, 0)
        body(i, 1)
    body(NB // 2, 0)
    body(NB // 2, 1)


def over_tiles0(eng, body):
    for j in range(2 * PER):
        body(0, j)
    with eng.Fori(1, E0 // 2) as i:
        for j in range(2 * PER):
            body(i, j)
    body(E0 // 2, 0)
    body(E0 // 2, 1)


def over_tiles1(eng, body):
    for i in range(2):
        body(i, 0)
        body(i, 1)
    with eng.Fori(2, NT1 // 2) as i:
        body(i, 0)
        body(i, 1)
    body(NT1 // 2, 0)
    body(NT1 // 2, 1)


def within(t, n):
    return not isinstance(t, int) or 0 <= t < n


def build(nc, a, out, stage=9):
    ctx = ExitStack()
    with ctx:
        def sb(name, shape, dt=F32):
            return ctx.enter_context(nc.sbuf_tensor(name, shape, dt))

        def sem(name):
            return ctx.enter_context(nc.semaphore(name))

        x = sb("x", [P, NB, DM])
        ident = sb("ident", [P, P])
        identb = sb("identb", [P, P], BF16)
        sel = sb("sel", [2 * QH, QH, P], BF16)
        selw = sb("selw", [2 * QH, QH, P])
        hmask = sb("hmask", [P, NH])
        mask8 = sb("mask8", [P, NB], U8)
        mask = sb("mask", [P, NB])
        mhalf = sb("mhalf", [P, NB])
        stats = sb("stats", [P, NB, 6])
        mean = sb("mean", [P, NB])
        ln = [sb(f"ln{n}", [P, NB]) for n in range(4)]
        rstd = sb("rstd", [P, NB])
        wq0 = sb("wq0", [DM, DM])
        wk0 = sb("wk0", [DC, DM])
        wv0 = sb("wv0", [DC, DM])
        wq1 = sb("wq1", [DM, NH * D1])
        wk1 = sb("wk1", [DC, NH * D1])
        wv1 = sb("wv1", [DC, NH * D1])
        wo1 = sb("wo1", [P, NCH, DM])
        bo1 = sb("bo1", [P, DM])
        xn = [sb(f"xn{p}", [P, DM]) for p in range(2)]
        xnT = [sb(f"xnT{p}", [DM, P]) for p in range(2)]
        ctxT = [sb(f"ctxT{p}", [DC, P]) for p in range(2)]
        qpads = sb("qpads", [P, 2 * NH, P])
        qpad = [qpads[:, p * NH:(p + 1) * NH, :] for p in range(2)]
        kT = [sb(f"kT{p}", [P, NCH, P]) for p in range(2)]
        va0 = [sb(f"va0{p}", [P, NH, D0 + 1]) for p in range(2)]
        va1 = [sb(f"va1{p}", [P, NH, D1 + 1]) for p in range(2)]
        mx = [sb(f"mx{p}", [P, QH]) for p in range(2)]
        c8 = [sb(f"c8{p}", [P, 2 * QH], BF16) for p in range(2)]
        cT = [sb(f"cT{p}", [2 * QH, P], BF16) for p in range(2)]
        pT = [sb(f"pT{p}", [P, QH, P]) for p in range(2)]
        rden = sb("rden", [P, QH])
        o0 = sb("o0", [P, NH, D0])
        o1 = [sb(f"o1{p}", [P, NH, D1]) for p in range(2)]
        oT = sb("oT", [P, NCH, P])
        ysum = sb("ysum", [P, DM])

        xna = qpads
        tri = sb("tri", [P, P], BF16)
        ones = sb("ones", [P, P], BF16)
        triw = sb("triw", [P, P])
        rw = [sb("rw0", [DM, E0]), sb("rw1", [DM, E1])]
        rb0 = sb("rb0", [P, E0])
        rev = sb("rev", [P, E1])
        base0 = sb("base0", [P, E0])
        k128 = sb("k128", [P, NB])
        tiota = sb("tiota", [1, NT1])
        reset = sb("reset", [P, E1, NB])
        RT = [P, E1, NB]
        lg, pr, wk, oh1, oh2, rk = [sb(n, RT) for n in ("lg", "pr", "wk", "oh1", "oh2", "rk")]
        selb = sb("selb", RT, BF16)
        v1, v2, v3, v4 = [sb(n, [P, NB]) for n in ("v1", "v2", "v3", "v4")]
        wt = [sb(f"wt{k}", [P, NB]) for k in range(2)]
        slot = [sb(f"slot{k}", [P, NB], I32) for k in range(3)]
        ntile, tcum, base1 = [sb(n, [P, E1]) for n in ("ntile", "tcum", "base1")]
        pr2 = sb("pr2", [1, NT1, E1])
        tef = sb("tef", [1, NT1])
        tei = sb("tei", [1, NT1], I32)
        zero = sb("zero", [P, 8 * DM])
        w1s = [sb(f"w1s{p}", [DM, F0]) for p in range(2)]
        w2s = [sb(f"w2s{p}", [P, 2, DM]) for p in range(2)]
        b1s = [sb(f"b1s{p}", [P, 2]) for p in range(2)]
        b2s = [sb(f"b2s{p}", [P, DM]) for p in range(2)]
        xs = [sb(f"xs{p}", [P, 2, DM]) for p in range(2)]
        xsT = [sb(f"xsT{p}", [DM, 2, P]) for p in range(2)]
        hT = [sb(f"hT{p}", [P, 2, 2 * P]) for p in range(2)]
        sg = [sb(f"sg{p}", [P, 2, P]) for p in range(2)]
        ysb = [sb(f"ysb{p}", [P, 2, DM]) for p in range(2)]
        gb = [sb(f"gb{r}", [P, DM]) for r in range(RING)]
        gu = sb("gu", [DM, E1, 2 * F1])
        dn = sb("dn", [P, E1, 2, DM])
        gus = [sb(f"gus{p}", [DM, 2 * F1]) for p in range(2)]
        dns = [sb(f"dns{p}", [P, 2, DM]) for p in range(2)]
        wgu = sb("wgu", [DM, 2 * F1])
        wdn = sb("wdn", [P, 2, DM])

        buf0 = nc.dram_tensor("buf0", (ZROW, DM), F32, kind="Internal").ap()
        eo0 = nc.dram_tensor("eo0", (ZROW + P, DM), F32, kind="Internal").ap()
        buf1 = nc.dram_tensor("buf1", (NT1 * P, DM), F32, kind="Internal").ap()
        eo1 = nc.dram_tensor("eo1", (NT1 * P, DM), F32, kind="Internal").ap()

        bank = [ctx.enter_context(nc.psum_tensor(f"bank{n}", [P, 512], F32)) for n in range(7)]
        cbank = ctx.enter_context(nc.psum_tensor("cbank", [P, 1024], BF16))
        s_bank, st_bank, pj_bank, o_bank = bank[0:2], bank[2:4], bank[4:6], bank[6]

        loaded = sem("loaded")
        masked = sem("masked")
        stat_done = sem("stat_done")
        ln_step = sem("ln_step")
        rstd_done = sem("rstd_done")
        const_done = sem("const_done")
        stored = sem("stored")
        zeroed = sem("zeroed")
        zset = sem("zset")
        rt = sem("rt")
        exp_in, exp_out = sem("exp_in"), sem("exp_out")
        sel_ready, rank_ready = sem("sel_ready"), sem("rank_ready")
        slots_ready = sem("slots_ready")
        qpad_zero = sem("qpad_zero")
        g_in = [sem(f"g_in{r}") for r in range(RING)]
        g_used = sem("g_used")

        class Moe:
            def __init__(self, n):
                self.xr_ready = sem(f"xr_ready_{n}")
                self.xr_copied = sem(f"xr_copied_{n}")
                self.t_full = sem(f"t_full_{n}")
                self.t_evac = sem(f"t_evac_{n}")
                self.lg_done = sem(f"lg_done_{n}")
                self.scattered = sem(f"scattered_{n}")
                self.sg_done = sem(f"sg_done_{n}")
                self.sh_done = sem(f"sh_done_{n}")
                self.sy_full = sem(f"sy_full_{n}")
                self.sy_done = sem(f"sy_done_{n}")
                self.wcopied = sem(f"wcopied_{n}")
                self.xt_full = sem(f"xt_full_{n}")
                self.xt_evac = sem(f"xt_evac_{n}")
                self.h_full = sem(f"h_full_{n}")
                self.h_act = sem(f"h_act_{n}")
                self.h_done = sem(f"h_done_{n}")
                self.y_full = sem(f"y_full_{n}")
                self.y_evac = sem(f"y_evac_{n}")
                self.w_in = [sem(f"w_in{n}{p}") for p in range(2)]
                self.xs_in = [sem(f"xs_in{n}{p}") for p in range(2)]
                self.y_out = [sem(f"y_out{n}{p}") for p in range(2)]
        M0, M1 = Moe(0), Moe(1)

        class Layer:
            def __init__(self, n):
                self.ctx_in = [sem(f"ctx_in{n}{p}") for p in range(2)]
                self.xn_ready = sem(f"xn_ready{n}")
                self.pj_full = [sem(f"pj_full{n}{p}") for p in range(2)]
                self.pj_free = [sem(f"pj_free{n}{p}") for p in range(2)]
                self.s_full = sem(f"s_full{n}")
                self.max_done = sem(f"max_done{n}")
                self.hi_done = sem(f"hi_done{n}")
                self.shift_ready = sem(f"shift_ready{n}")
                self.c_full = sem(f"c_full{n}")
                self.c_free = sem(f"c_free{n}")
                self.st_full = sem(f"st_full{n}")
                self.exp_done = sem(f"exp_done{n}")
                self.pv_full = sem(f"pv_full{n}")
                self.rden_done = sem(f"rden_done{n}")
                self.pv_free = sem(f"pv_free{n}")
                self.y_full = sem(f"y_full{n}")
                self.y_free = sem(f"y_free{n}")
                self.x_done = sem(f"x_done{n}")
        L0, L1 = Layer(0), Layer(1)

        NZERO = -(-ZROW // (8 * P)) + -(-NT1 // 8) + 1

        with nc.Block() as block:
            NLOAD = 16 * 28

            @block.sync
            def _(sp):
                sp.dma_start(x[:, :, :], a["x"]).then_inc(loaded, 16)
                for dst, name in ((ident, "ident"), (selw, "sel"), (hmask, "hmask"), (mask8, "mask"),
                                  (mhalf, "mhalf"), (wq0, "wq0"), (wk0, "wk0"), (wv0, "wv0"),
                                  (wq1, "wq1"), (wk1, "wk1"), (wv1, "wv1"), (wo1, "wo1"), (bo1, "bo1"),
                                  (triw, "tri"), (rw[0], "rw0"), (rw[1], "rw1"), (rb0, "rb0"), (rev, "rev"),
                                  (base0, "base0"), (k128, "k128"), (tiota, "tiota"), (reset, "reset"),
                                  (gu, "gu"), (dn, "dn"), (wgu, "wgu"), (wdn, "wdn"), (zero, "zero")):
                    sp.dma_start(dst[:], a[name]).then_inc(loaded, 16)

                def attention(L, fill, lastv):
                    def body(i, off):
                        b = 2 * i + off
                        if not inside(b + 1):
                            return
                        at = (b + 1) * P
                        if not isinstance(at, int):
                            at = sp.snap(at)
                        if inside(b - 1):
                            bk, k = fill(i, off - 2, lastv)
                            need(sp, L.pj_full[bk], k + 1)
                        sp.dma_start(ctxT[(off + 1) % 2][:, :], a["ctxT"][:, bass.ds(at, P)])\
                            .then_inc(L.ctx_in[(off + 1) % 2], 16)
                    over_batches(sp, body)
                sp.wait_ge(loaded, NLOAD)
                nz = 0
                for buf, rows in ((buf0, ZROW), (buf1, NT1 * P)):
                    for r in range(0, rows, 8 * P):
                        m = min(8 * P, rows - r) // P
                        sp.dma_start(buf[r:r + m * P, :].rearrange("(p m) d -> p (m d)", p=P), zero[:, 0:m * DM])\
                            .then_inc(zeroed, 16)
                        nz += 1
                sp.dma_start(eo0[ZROW:ZROW + P, :], zero[:, 0:DM]).then_inc(zeroed, 16)
                assert nz + 1 == NZERO
                attention(L0, fill0, "v")
                if stage >= 1:
                    sp.wait_ge(M0.scattered, 16 * 2 * NB)
                    tiles0 = range(2)

                    def body(i, j):
                        u, q, t = j // PER % 2, j % 2, 2 * PER * i + j
                        if j % PER == 0 and within(t, NT0):
                            need(sp, M0.y_evac, t - PER)
                            e = 2 * i + u
                            for dst, name in ((w1s, "w1"), (w2s, "w2"), (b1s, "b1"), (b2s, "b2")):
                                src = a[name][e] if isinstance(e, int) else a[name][bass.ds(e, 1)]
                                if not isinstance(e, int):
                                    src = src.squeeze(0)
                                sp.dma_start(dst[u][:], src).then_inc(M0.w_in[u], 16)
                        if within(t, NT0):
                            need(sp, M0.xt_full, t - 1)
                            sp.dma_start(xs[q][:, :, :], buf0[bass.ds(t * 2 * P, 2 * P), :]
                                         .rearrange("(h p) d -> p h d", p=P)).then_inc(M0.xs_in[q], 16)
                        if within(t - 2, NT0):
                            sp.wait_ge(M0.y_evac, t - 1)
                            sp.dma_start(eo0[bass.ds((t - 2) * 2 * P, 2 * P), :].rearrange("(h p) d -> p h d", p=P),
                                         ysb[q][:, :, :]).then_inc(M0.y_out[q], 16)
                    over_tiles0(sp, body)
                if stage >= 2:
                    attention(L1, fill1, "v1")
                if stage >= 3:
                    sp.wait_ge(M1.scattered, 16 * NB)

                    def body(i, u):
                        t = 2 * i + u
                        if within(t, NT1):
                            need(sp, M1.xt_full, t - 1)
                            sp.dma_start(xs[u][:, 0, :], buf1[bass.ds(t * P, P), :]).then_inc(M1.xs_in[u], 16)
                        if within(t - 2, NT1):
                            sp.wait_ge(M1.y_evac, t - 1)
                            sp.dma_start(eo1[bass.ds((t - 2) * P, P), :], ysb[u][:, 0, :]).then_inc(M1.y_out[u], 16)
                    over_tiles1(sp, body)
                if stage == 0:
                    sp.wait_ge(L0.x_done, NB)
                elif stage == 1:
                    sp.wait_ge(g_used, 2 * NB)
                elif stage == 2:
                    sp.wait_ge(L1.x_done, NB)
                else:
                    sp.wait_ge(g_used, 3 * NB)
                sp.dma_start(out, x[:, :, :]).then_inc(stored, 16)
                sp.wait_ge(stored, 16)

            @block.gpsimd
            def _(pool):
                for p in range(2):
                    nc.gpsimd.memset(va0[p][:, :, D0:D0 + 1], 1.0).then_inc(const_done, 1)
                    nc.gpsimd.memset(va1[p][:, :, D1:D1 + 1], 1.0).then_inc(const_done, 1)
                pool.wait_ge(loaded, NLOAD)
                nc.gpsimd.tensor_copy(identb[:, :], ident[:, :]).then_inc(const_done, 1)
                nc.gpsimd.tensor_copy(sel[:, :, :], selw[:, :, :]).then_inc(const_done, 1)
                nc.gpsimd.tensor_copy(tri[:, :], triw[:, :]).then_inc(const_done, 1)
                nc.gpsimd.memset(ones[:, :], 1.0).then_inc(const_done, 1)
                nc.gpsimd.tensor_copy(mask[:, :], mask8[:, :]).then_inc(masked, 1)

                def norm(n):
                    even, odd = 1, 4
                    steps = [0]

                    def step(ins):
                        steps[0] += 1
                        ins.then_inc(ln_step, 1)
                        pool.wait_ge(ln_step, 9 * (n - 1) + steps[0])
                    tt, ts = nc.gpsimd.tensor_tensor, nc.gpsimd.tensor_scalar
                    pool.wait_ge(stat_done, NB * n)
                    step(tt(ln[0][:, :], stats[:, :, even], stats[:, :, odd], ALU.add))
                    step(ts(mean[:, :], ln[0][:, :], 0.5, None, ALU.mult))
                    step(tt(ln[1][:, :], stats[:, :, even], stats[:, :, odd], ALU.subtract))
                    step(tt(ln[2][:, :], ln[1][:, :], ln[1][:, :], ALU.mult))
                    step(ts(ln[3][:, :], ln[2][:, :], 0.25, EPS, ALU.mult, ALU.add))
                    step(tt(ln[0][:, :], stats[:, :, even + 1], stats[:, :, odd + 1], ALU.add))
                    step(ts(ln[1][:, :], ln[0][:, :], 1.0 / DM, None, ALU.mult))
                    step(tt(ln[2][:, :], ln[1][:, :], ln[3][:, :], ALU.add))
                    ins = tt(rstd[:, :], ln[2][:, :], mhalf[:, :], ALU.pow)
                    step(ins)
                    nc.gpsimd.sem_inc(rstd_done, 1)
                norm(1)

                def keep_tokens(M):
                    def body(i, u):
                        b = 2 * i + u
                        if within(b, NB):
                            pool.wait_ge(M.xr_ready, b + 1)
                            nc.gpsimd.tensor_copy(xna[:, b, :], xn[u][:, :]).then_inc(M.xr_copied, 1)
                    over_pairs(pool, body)

                def scatter(M, ks, buf, bound):
                    for b in range(NB):
                        for k in ks:
                            nc.gpsimd.indirect_dma_start(
                                out=buf[:, :], out_offset=bass.IndirectOffsetOnAxis(ap=slot[k][:, b:b + 1], axis=0),
                                in_=xna[:, b, :], in_offset=None, bounds_check=bound, oob_is_err=False)\
                                .then_inc(M.scattered, 16)

                def gather(n0, ks, src):
                    n = n0
                    for b in range(NB):
                        for k in ks:
                            if n >= RING:
                                pool.wait_ge(g_used, n - RING + 1)
                            nc.gpsimd.indirect_dma_start(
                                out=gb[n % RING][:, :], out_offset=None, in_=src[:, :],
                                in_offset=bass.IndirectOffsetOnAxis(ap=slot[k][:, b:b + 1], axis=0))\
                                .then_inc(g_in[n % RING], 16)
                            n += 1
                if stage >= 1:
                    norm(2)
                    keep_tokens(M0)
                    pool.wait_ge(slots_ready, 2)
                    pool.wait_ge(zeroed, 16 * NZERO)
                    pool.wait_ge(M0.xr_copied, NB)
                    scatter(M0, (0, 1), buf0, ZROW - 1)
                    for q in range(2):
                        pool.wait_ge(M0.y_out[q], 16 * NT0 // 2)
                    gather(0, (0, 1), eo0)
                if stage >= 2:
                    pool.wait_ge(L0.st_full, NB * NQ)
                    for p in range(2):
                        nc.gpsimd.memset(qpad[p][:, :, :], 0.0).then_inc(qpad_zero, 1)
                    norm(3)
                if stage >= 3:
                    norm(4)
                    pool.wait_ge(slots_ready, 3)
                    pool.wait_ge(M1.xr_copied, NB)
                    scatter(M1, (2,), buf1, NT1 * P - 1)

                    def body(i, u):
                        t = 2 * i + u
                        if not within(t, NT1):
                            return
                        e = nc.gpsimd.value_load(tei[0:1, bass.ds(t, 1)], min_val=0, max_val=E1 - 1)
                        need(pool, M1.y_full, t - 1)
                        nc.gpsimd.tensor_copy(gus[u][:, :], gu[:, bass.ds(e, 1), :].squeeze(1))
                        nc.gpsimd.tensor_copy(dns[u][:, :, :], dn[:, bass.ds(e, 1), :, :].squeeze(1)).then_inc(M1.wcopied, 1)
                    over_tiles1(pool, body)
                    for u in range(2):
                        pool.wait_ge(M1.y_out[u], 16 * NT1 // 2)
                    gather(2 * NB, (2,), eo1)

            def proj(L, fill, i, off, name):
                bk, k = fill(i, off, name)
                need(nc.tensor, L.pj_free[bk], k)
                return bk, pj_bank[bk]

            @block.tensor
            def _(pe):
                pe.wait_ge(loaded, NLOAD)
                pe.wait_ge(const_done, 8)

                def shifted(Q, g, j, last):
                    return nc.tensor.matmul(st_bank[g % 2][:, j * P:(j + 1) * P], sel[:, j, :], cT[g % 2][:, :],
                                            start=False, stop=last)

                def attention(L, fill, layer):
                    D = (D0, D1)[layer]
                    va = (va0, va1)[layer]

                    def body(i, off):
                        b = 2 * i + off
                        p, pn = off % 2, (off + 1) % 2
                        for g in range(NQ):
                            Q = NQ * b + g
                            if g == 0 and inside(b + 1):
                                bk, ps = proj(L, fill, i, off, "xT")
                                need(pe, L.xn_ready, b + 2)
                                nc.tensor.transpose(ps[:, 0:P], xn[pn][:, :], ident[:, :]).then_inc(L.pj_full[bk], 1)

                            bs, gs = b + (g + 2) // NQ, (g + 2) % NQ
                            ps_ = p if g < 2 else pn
                            if inside(bs):
                                if gs == 0:
                                    for nm in (("q", "k") if layer == 0 else ("q1", "k1")):
                                        bk, k = fill(i, off, nm)
                                        need(pe, L.pj_free[bk], k + 1)
                                need(pe, L.max_done, Q + 1)
                                for j in range(QH):
                                    h = QH * gs + j
                                    last = nc.tensor.matmul(s_bank[g % 2][:, j * P:(j + 1) * P], qpad[ps_][:, h, :],
                                                            kT[ps_][:, h // 2 if layer else 0, :], start=True, stop=True)
                                last.then_inc(L.s_full, 1)

                            if inside(b + (g + 1) // NQ):
                                need(pe, L.shift_ready, Q + 2)
                                need(pe, L.c_free, Q + 1)
                                nc.tensor.transpose(cbank[0:2 * QH, 0:P], c8[(g + 1) % 2][:, :], identb[:, :])\
                                    .then_inc(L.c_full, 1)

                            if inside(b):
                                need(pe, L.exp_done, Q - 1)
                                st = st_bank[g % 2]
                                if layer == 0:
                                    nc.tensor.matmul(st[:, :], kT[p][:, 0, :], qpad[p][:, QH * g:QH * (g + 1), :],
                                                     start=True, stop=False)
                                    pe.wait_ge(L.c_free, Q + 1)
                                    for j in range(QH):
                                        last = shifted(Q, g, j, j == QH - 1)
                                else:
                                    for c in range(2):
                                        nc.tensor.matmul(st[:, 2 * c * P:2 * (c + 1) * P], kT[p][:, 2 * g + c, :],
                                                         qpad[p][:, QH * g + 2 * c:QH * g + 2 * c + 2, :],
                                                         start=True, stop=False)
                                        if c == 0:
                                            pe.wait_ge(L.c_free, Q + 1)
                                        for j in (2 * c, 2 * c + 1):
                                            last = shifted(Q, g, j, j % 2 == 1)
                                last.then_inc(L.st_full, 1)

                            if layer == 0 and inside(b + 1):
                                if g == 0:
                                    bk, ps = proj(L, fill, i, off, "q")
                                    bx, kx = fill(i, off, "xT")
                                    need(pe, L.pj_free[bx], kx + 1)
                                    nc.tensor.matmul(ps[:, 0:P], wq0[:, :], xnT[pn][:, :], start=True, stop=True)\
                                        .then_inc(L.pj_full[bk], 1)
                                    bk, ps = proj(L, fill, i, off, "k")
                                    pe.wait_ge(L.ctx_in[pn], 16 * (i + 1 + (off + 1) // 2))
                                    nc.tensor.matmul(ps[:, 0:P], wk0[:, :], ctxT[pn][:, :], start=True, stop=True)\
                                        .then_inc(L.pj_full[bk], 1)
                                if g == 1:
                                    bk, ps = proj(L, fill, i, off, "v")
                                    nc.tensor.matmul(ps[:, 0:P], ctxT[pn][:, :], wv0[:, :], start=True, stop=True)\
                                        .then_inc(L.pj_full[bk], 1)
                            if layer == 1 and inside(b + 1):
                                if g == 0:
                                    bx, kx = fill(i, off, "xT")
                                    for nm in ("q0", "q1"):
                                        bk, ps = proj(L, fill, i, off, nm)
                                        if nm == "q0":
                                            need(pe, L.pj_free[bx], kx + 1)
                                        for c in range(4):
                                            n = 4 * (nm == "q1") + c
                                            last = nc.tensor.matmul(ps[:, c * P:(c + 1) * P], wq1[:, n * P:(n + 1) * P],
                                                                    xnT[pn][:, :], start=True, stop=True)
                                        last.then_inc(L.pj_full[bk], 1)
                                for nm in {0: ("k0",), 1: ("k1",)}.get(g, ()):
                                    bk, ps = proj(L, fill, i, off, nm)
                                    if nm == "k0":
                                        pe.wait_ge(L.ctx_in[pn], 16 * (i + 1 + (off + 1) // 2))
                                    for c in range(4):
                                        n = 4 * (nm == "k1") + c
                                        last = nc.tensor.matmul(ps[:, c * P:(c + 1) * P], wk1[:, n * P:(n + 1) * P],
                                                                ctxT[pn][:, :], start=True, stop=True)
                                    last.then_inc(L.pj_full[bk], 1)
                                for nm in {1: ("v0",), 2: ("v1",)}.get(g, ()):
                                    bk, ps = proj(L, fill, i, off, nm)
                                    n = int(nm == "v1")
                                    nc.tensor.matmul(ps[:, :], ctxT[pn][:, :], wv1[:, 512 * n:512 * (n + 1)],
                                                     start=True, stop=True).then_inc(L.pj_full[bk], 1)
                            if layer == 1 and inside(b - 1):
                                if g == 2:
                                    pe.wait_ge(L.pv_free, NQ * b)
                                    for nm in ("oT0", "oT1"):
                                        bk, ps = proj(L, fill, i, off, nm)
                                        for c in range(4):
                                            n = 4 * (nm == "oT1") + c
                                            last = nc.tensor.transpose(ps[:, c * P:(c + 1) * P],
                                                                       o1[pn][:, 2 * n:2 * n + 2, :], ident[:, :])
                                        last.then_inc(L.pj_full[bk], 1)
                                if g == 3:
                                    for nm in ("oT0", "oT1"):
                                        bk, k = fill(i, off, nm)
                                        pe.wait_ge(L.pj_free[bk], k + 1)
                                    need(pe, L.pv_free, Q - 1 if inside(b) else NQ * b)
                                    for c in range(NCH):
                                        last = nc.tensor.matmul(o_bank[:, 0:DM], oT[:, c, :], wo1[:, c, :],
                                                                start=(c == 0), stop=(c == NCH - 1))
                                    last.then_inc(L.y_full, 1)

                            bo, go = b + (g - 1) // NQ, (g - 1) % NQ
                            po = p if g else pn
                            if inside(bo):
                                pe.wait_ge(L.exp_done, Q)
                                if go == 0:
                                    bk, k = fill(i, off - 1, "v" if layer == 0 else "v1")
                                    need(pe, L.pj_free[bk], k + 1)
                                need(pe, L.pv_free, Q - 1)
                                if layer == 1 and g == 3:
                                    need(pe, L.y_free, b)
                                for j in range(QH):
                                    last = nc.tensor.matmul(o_bank[:, j * (D + 1):(j + 1) * (D + 1)], pT[go % 2][:, j, :],
                                                            va[po][:, QH * go + j, :], start=True, stop=True)
                                last.then_inc(L.pv_full, 1)
                    over_batches(pe, body)
                attention(L0, fill0, 0)

                def route(M, n):
                    E = (E0, E1)[n]

                    def transposed(b, u):
                        pe.wait_ge(M.xr_ready, b + 1)
                        need(pe, M.t_evac, b - 1)
                        nc.tensor.transpose(pj_bank[u][:, 0:P], xn[u][:, :], ident[:, :]).then_inc(M.t_full, 1)

                    def logits(b, u):
                        pe.wait_ge(M.t_evac, b + 1)
                        if n == 1:
                            need(pe, M.sh_done, b - 1)
                            for c in range(4):
                                nc.tensor.matmul(s_bank[u][:, c * P:(c + 1) * P], wgu[:, c * P:(c + 1) * P],
                                                 xnT[u][:, :], start=True, stop=True)
                        nc.tensor.matmul(o_bank[:, bass.ds(b * E, E)], xnT[u][:, :], rw[n][:, :],
                                         start=True, stop=True).then_inc(M.lg_done, 1)

                    def shared(b, u):
                        pe.wait_ge(M.sh_done, b + 1)
                        need(pe, M.sy_done, b - 1)
                        for c in range(2):
                            last = nc.tensor.matmul(st_bank[u][:, 0:DM], hT[u][:, c, 0:P], wdn[:, c, :],
                                                    start=(c == 0), stop=(c == 1))
                        last.then_inc(M.sy_full, 1)

                    def body(i, u):
                        b = 2 * i + u
                        if within(b, NB):
                            transposed(b, u)
                        if within(b - 1, NB):
                            logits(b - 1, 1 - u)
                        if n == 1 and within(b - 2, NB):
                            shared(b - 2, u)
                    over_pairs(pe, body)

                def ranks(n):
                    cols = (E0, E1)[n] * NB
                    flat = selb[:, 0:(E0, E1)[n], :].rearrange("p e b -> p (e b)")
                    pe.wait_ge(sel_ready, n + 1)
                    nc.tensor.matmul(s_bank[0][:, 0:cols], tri[:, :], flat, start=True, stop=True)
                    nc.tensor.matmul(s_bank[1][:, 0:cols], ones[:, :], flat, start=True, stop=True)\
                        .then_inc(rank_ready, 1)

                if stage >= 1:
                    route(M0, 0)
                    ranks(0)

                    def body(i, j):
                        q, t = j % 2, 2 * PER * i + j
                        if within(t, NT0):
                            pe.wait_ge(M0.xs_in[q], 16 * (PER * i + j // 2 + 1))
                            need(pe, M0.xt_evac, t - 1)
                            for h in range(2):
                                last = nc.tensor.transpose(pj_bank[q][:, h * P:(h + 1) * P], xs[q][:, h, :], ident[:, :])
                            last.then_inc(M0.xt_full, 1)
                        if within(t - 1, NT0):
                            jj, ii = (j - 1) % (2 * PER), i if j else i - 1
                            u = jj // PER
                            pe.wait_ge(M0.w_in[u], 64 * (ii + 1))
                            pe.wait_ge(M0.xt_evac, t)
                            need(pe, M0.h_done, t - 2)
                            for f in range(2):
                                last = nc.tensor.matmul(s_bank[1 - q][:, 2 * f * P:2 * (f + 1) * P],
                                                        w1s[u][:, f * P:(f + 1) * P], xsT[1 - q][:, :, :],
                                                        start=True, stop=True)
                            last.then_inc(M0.h_full, 1)
                        if within(t - 2, NT0):
                            u = (j - 2) % (2 * PER) // PER
                            pe.wait_ge(M0.h_done, t - 1)
                            need(pe, M0.y_evac, t - 3)
                            for h in range(2):
                                for f in range(2):
                                    last = nc.tensor.matmul(st_bank[q][:, h * DM:(h + 1) * DM],
                                                            hT[q][:, f, h * P:(h + 1) * P], w2s[u][:, f, :],
                                                            start=(f == 0), stop=(f == 1))
                            last.then_inc(M0.y_full, 1)
                    over_tiles0(pe, body)
                if stage >= 2:
                    pe.wait_ge(qpad_zero, 2)
                    attention(L1, fill1, 1)
                if stage >= 3:
                    route(M1, 1)
                    ranks(1)

                    def body(i, q):
                        t = 2 * i + q
                        if within(t, NT1):
                            pe.wait_ge(M1.xs_in[q], 16 * (i + 1))
                            need(pe, M1.xt_evac, t - 1)
                            nc.tensor.transpose(pj_bank[q][:, 0:P], xs[q][:, 0, :], ident[:, :]).then_inc(M1.xt_full, 1)
                        if within(t - 1, NT1):
                            pe.wait_ge(M1.wcopied, t)
                            pe.wait_ge(M1.xt_evac, t)
                            need(pe, M1.h_done, t - 2)
                            for f in range(4):
                                last = nc.tensor.matmul(s_bank[1 - q][:, f * P:(f + 1) * P],
                                                        gus[1 - q][:, f * P:(f + 1) * P], xsT[1 - q][:, 0, :],
                                                        start=True, stop=True)
                            last.then_inc(M1.h_full, 1)
                        if within(t - 2, NT1):
                            pe.wait_ge(M1.h_done, t - 1)
                            need(pe, M1.y_evac, t - 3)
                            for f in range(2):
                                last = nc.tensor.matmul(st_bank[q][:, 0:DM], hT[q][:, f, 0:P], dns[q][:, f, :],
                                                        start=(f == 0), stop=(f == 1))
                            last.then_inc(M1.y_full, 1)
                    over_tiles1(pe, body)

            @block.scalar
            def _(act):
                def attention(L, fill, layer):
                    D = (D0, D1)[layer]

                    def take(i, off, name):
                        bk, k = fill(i, off, name)
                        act.wait_ge(L.pj_full[bk], k + 1)
                        return bk, pj_bank[bk]

                    def body(i, off):
                        b = 2 * i + off
                        p, pn = off % 2, (off + 1) % 2
                        for g in range(NQ):
                            Q = NQ * b + g
                            if g == 0 and inside(b + 1):
                                bk, ps = take(i, off, "xT")
                                if inside(b - 1):
                                    bq, kq = fill(i, off - 2, "q" if layer == 0 else "q1")
                                    need(act, L.pj_full[bq], kq + 1)
                                nc.scalar.copy(xnT[pn][:, :], ps[:, 0:P]).then_inc(L.pj_free[bk], 1)
                            if inside(b + (g + 1) // NQ):
                                act.wait_ge(L.c_full, Q + 2)
                                need(act, L.st_full, Q)
                                nc.scalar.copy(cT[(g + 1) % 2][:, :], cbank[0:2 * QH, 0:P]).then_inc(L.c_free, 1)
                            if inside(b):
                                act.wait_ge(L.st_full, Q + 1)
                                need(act, L.pv_full, Q - 1)
                                nc.scalar.activation(pT[g % 2][:, :, :], st_bank[g % 2][:, :], ACT.Exp, scale=D ** -0.5)\
                                    .then_inc(L.exp_done, 1)
                            if layer == 0 and inside(b + 1):
                                if g == 0:
                                    bk, ps = take(i, off, "k")
                                    need(act, L.st_full, NQ * b)
                                    nc.scalar.copy(kT[pn][:, 0, :], ps[:, 0:P]).then_inc(L.pj_free[bk], 1)
                                if g == 1:
                                    bk, ps = take(i, off, "v")
                                    need(act, L.pv_full, NQ * b)
                                    nc.scalar.copy(va0[pn][:, :, 0:D0], ps[:, 0:P].rearrange("p (h d) -> p h d", d=D0))\
                                        .then_inc(L.pj_free[bk], 1)
                            if layer == 1 and inside(b + 1):
                                for nm in {0: ("q0", "q1", "k0"), 1: ("k1", "v0"), 2: ("v1",)}.get(g, ()):
                                    bk, ps = take(i, off, nm)
                                    half = int(nm[1])
                                    need(act, L.pv_full if nm[0] == "v" else L.st_full, NQ * b)
                                    if nm[0] == "q":
                                        for r in range(2):
                                            rows = slice(D1 * r, D1 * (r + 1))
                                            dst = qpad[pn][rows, :, :].rearrange("p (c r) n -> p c r n", r=2)
                                            last = nc.scalar.copy(dst[:, 4 * half:4 * half + 4, r, :],
                                                                  ps[rows, :].rearrange("p (c n) -> p c n", c=4))
                                        last.then_inc(L.pj_free[bk], 1)
                                    elif nm[0] == "k":
                                        nc.scalar.copy(kT[pn][:, 4 * half:4 * half + 4, :], ps[:, :])\
                                            .then_inc(L.pj_free[bk], 1)
                                    else:
                                        nc.scalar.copy(va1[pn][:, 8 * half:8 * half + 8, 0:D1],
                                                       ps[:, :].rearrange("p (h d) -> p h d", d=D1))\
                                            .then_inc(L.pj_free[bk], 1)
                            if layer == 1 and inside(b - 1) and g == 2:
                                need(act, L.y_full, b - 1)
                                for nm in ("oT0", "oT1"):
                                    bk, ps = take(i, off, nm)
                                    half = int(nm[2])
                                    nc.scalar.copy(oT[:, 4 * half:4 * half + 4, :], ps[:, :]).then_inc(L.pj_free[bk], 1)
                    over_batches(act, body)
                attention(L0, fill0, 0)

                def route(M, n):
                    def body(i, u):
                        b = 2 * i + u
                        if within(b, NB):
                            act.wait_ge(M.t_full, b + 1)
                            need(act, M.lg_done, b - 1)
                            nc.scalar.copy(xnT[u][:, :], pj_bank[u][:, 0:P]).then_inc(M.t_evac, 1)
                        if n == 1 and within(b - 1, NB):
                            act.wait_ge(M.lg_done, b)
                            need(act, M.sh_done, b - 2)
                            nc.scalar.activation(sg[1 - u][:, :, :], s_bank[1 - u][:, 0:2 * P], ACT.Silu)\
                                .then_inc(M.sg_done, 1)
                    over_pairs(act, body)

                if stage >= 1:
                    route(M0, 0)
                    act.wait_ge(exp_in, 1)
                    nc.scalar.activation(pr[:, 0:E0, :], wk[:, 0:E0, :], ACT.Exp).then_inc(exp_out, 1)

                    def body(i, j):
                        q, t = j % 2, 2 * PER * i + j
                        if within(t, NT0):
                            act.wait_ge(M0.xt_full, t + 1)
                            need(act, M0.h_full, t - 1)
                            nc.scalar.copy(xsT[q][:, :, :], pj_bank[q][:, 0:2 * P]).then_inc(M0.xt_evac, 1)
                        if within(t - 1, NT0):
                            u = (j - 1) % (2 * PER) // PER
                            act.wait_ge(M0.h_full, t)
                            need(act, M0.y_full, t - 2)
                            for f in range(2):
                                last = nc.scalar.activation(hT[1 - q][:, f, :], s_bank[1 - q][:, 2 * f * P:2 * (f + 1) * P],
                                                            ACT.Gelu, bias=b1s[u][:, f:f + 1])
                            last.then_inc(M0.h_done, 1)
                    over_tiles0(act, body)
                if stage >= 2:
                    act.wait_ge(qpad_zero, 2)
                    attention(L1, fill1, 1)
                if stage >= 3:
                    route(M1, 1)
                    act.wait_ge(exp_in, 2)
                    nc.scalar.activation(v2[:, :], v1[:, :], ACT.Exp, scale=-1.0).then_inc(exp_out, 1)

                    def body(i, q):
                        t = 2 * i + q
                        if within(t, NT1):
                            act.wait_ge(M1.xt_full, t + 1)
                            need(act, M1.h_full, t - 1)
                            nc.scalar.copy(xsT[q][:, 0, :], pj_bank[q][:, 0:P]).then_inc(M1.xt_evac, 1)
                        if within(t - 1, NT1):
                            act.wait_ge(M1.h_full, t)
                            need(act, M1.h_done, t - 2)
                            nc.scalar.activation(sg[1 - q][:, :, :], s_bank[1 - q][:, 0:2 * P], ACT.Silu)\
                                .then_inc(M1.h_act, 1)
                    over_tiles1(act, body)

            @block.vector
            def _(dve):
                dve.wait_ge(loaded, NLOAD)

                def stat(b):
                    nc.vector.bn_stats(stats[:, b, :], x[:, b, :]).then_inc(stat_done, 1)
                with dve.Fori(0, NB) as b:
                    stat(b)
                dve.wait_ge(rstd_done, 1)
                dve.wait_ge(masked, 1)
                nc.vector.tensor_tensor(rstd[:, :], rstd[:, :], mask[:, :], ALU.mult).then_inc(masked, 1)
                dve.wait_ge(masked, 2)

                def attention(L, fill, layer):
                    D = (D0, D1)[layer]

                    def normed(b, p):
                        nc.vector.tensor_scalar(xn[p][:, :], x[:, b, :], mean[:, bass.ds(b, 1)], rstd[:, bass.ds(b, 1)],
                                                ALU.subtract, ALU.mult).then_inc(L.xn_ready, 1)
                    normed(0, 0)

                    def body(i, off):
                        b = 2 * i + off
                        p, pn = off % 2, (off + 1) % 2
                        for g in range(NQ):
                            Q = NQ * b + g
                            if inside(b + (g + 2) // NQ):
                                dve.wait_ge(L.s_full, Q + 3)
                                m, c = mx[g % 2], c8[g % 2]
                                nc.vector.reduce_max(m[:, :], s_bank[g % 2][:, :].rearrange("p (h k) -> p h k", h=QH), AX.X)\
                                    .then_inc(L.max_done, 1)
                                dve.wait_ge(L.max_done, Q + 3)
                                need(dve, L.c_full, Q + 1)
                                nc.vector.tensor_copy(c[:, 0:QH], m[:, :]).then_inc(L.hi_done, 1)
                                dve.wait_ge(L.hi_done, Q + 3)
                                nc.vector.tensor_tensor(c[:, QH:2 * QH], m[:, :], c[:, 0:QH], ALU.subtract)\
                                    .then_inc(L.shift_ready, 1)
                            if g == 0 and layer == 0 and inside(b + 1):
                                bk, k = fill(i, off, "q")
                                dve.wait_ge(L.pj_full[bk], k + 1)
                                need(dve, L.st_full, NQ * b)
                                nc.vector.tensor_tensor(
                                    qpad[pn][:, :, :],
                                    pj_bank[bk][:, 0:P].unsqueeze(1).broadcast_to([P, NH, P]),
                                    hmask[:, :].unsqueeze(2).broadcast_to([P, NH, P]), ALU.mult)\
                                    .then_inc(L.pj_free[bk], 1)
                            if g == 1 and inside(b + 2):
                                if inside(b):
                                    bx, kx = fill(i, off - 1, "xT")
                                    need(dve, L.pj_full[bx], kx + 1)
                                normed(b + 2, p)
                            if layer == 1 and g == 3 and inside(b - 1):
                                dve.wait_ge(L.y_full, b)
                                nc.vector.tensor_tensor(ysum[:, :], o_bank[:, 0:DM], bo1[:, :], ALU.add)\
                                    .then_inc(L.y_free, 1)
                                dve.wait_ge(L.y_free, b)
                                nc.vector.tensor_tensor(x[:, b - 1, :], x[:, b - 1, :], ysum[:, :], ALU.add)\
                                    .then_inc(L.x_done, 1)
                                dve.wait_ge(L.x_done, b)
                                stat(b - 1)
                            bo, go = b + (g - 1) // NQ, (g - 1) % NQ
                            po = p if g else pn
                            if inside(bo):
                                dve.wait_ge(L.pv_full, Q)
                                ov = o_bank[:, 0:QH * (D + 1)].rearrange("p (h d) -> p h d", d=D + 1)
                                nc.vector.reciprocal(rden[:, :], ov[:, :, D]).then_inc(L.rden_done, 1)
                                dve.wait_ge(L.rden_done, Q)
                                o = o0 if layer == 0 else o1[po]
                                nc.vector.tensor_tensor(o[:, QH * go:QH * (go + 1), :], ov[:, :, 0:D],
                                                        rden[:, :].unsqueeze(2).broadcast_to([P, QH, D]), ALU.mult)\
                                    .then_inc(L.pv_free, 1)
                                if layer == 0 and go == NQ - 1:
                                    dve.wait_ge(L.pv_free, Q)
                                    nc.vector.tensor_tensor(x[:, bo, :], x[:, bo, :], o0[:, :, :].rearrange("p h d -> p (h d)"), ALU.add)\
                                        .then_inc(L.x_done, 1)
                                    dve.wait_ge(L.x_done, bo + 1)
                                    stat(bo)
                    over_batches(dve, body)
                attention(L0, fill0, 0)

                chain = [0]

                def link(ins):
                    chain[0] += 1
                    ins.then_inc(rt, 1)
                    dve.wait_ge(rt, chain[0])

                def route(M, n, base):
                    dve.wait_ge(rstd_done, base)

                    def body(i, u):
                        b = 2 * i + u
                        if within(b, NB):
                            need(dve, M.t_full, b - 1)
                            need(dve, M.xr_copied, b - 1)
                            nc.vector.tensor_scalar(xn[u][:, :], x[:, b, :], mean[:, bass.ds(b, 1)],
                                                    rstd[:, bass.ds(b, 1)], ALU.subtract, ALU.mult)\
                                .then_inc(M.xr_ready, 1)
                            if n == 1:
                                nc.vector.tensor_scalar(xna[:, b, :], x[:, b, :], mean[:, bass.ds(b, 1)],
                                                        rstd[:, bass.ds(b, 1)], ALU.subtract, ALU.mult)\
                                    .then_inc(M.xr_copied, 1)
                        if n == 1 and within(b - 1, NB):
                            dve.wait_ge(M.sg_done, b)
                            need(dve, M.sy_full, b - 2)
                            nc.vector.tensor_tensor(hT[1 - u][:, :, 0:P], sg[1 - u][:, :, :],
                                                    s_bank[1 - u][:, 2 * P:4 * P].rearrange("p (c n) -> p c n", c=2),
                                                    ALU.mult).then_inc(M.sh_done, 1)
                        if n == 1 and within(b - 2, NB):
                            dve.wait_ge(M.sy_full, b - 1)
                            nc.vector.tensor_tensor(x[:, b - 2, :], x[:, b - 2, :], st_bank[u][:, 0:DM], ALU.add)\
                                .then_inc(M.sy_done, 1)
                    over_pairs(dve, body)

                def top(E, src, oh, best):
                    tt = nc.vector.tensor_tensor
                    by_token = "p e b -> p b e"
                    link(nc.vector.reduce_max(best[:, :], src[:, 0:E, :].rearrange(by_token), AX.X))
                    link(tt(wk[:, 0:E, :], src[:, 0:E, :], best[:, :].unsqueeze(1).broadcast_to([P, E, NB]), ALU.is_equal))
                    link(tt(wk[:, 0:E, :], wk[:, 0:E, :], rev[:, 0:E].unsqueeze(2).broadcast_to([P, E, NB]), ALU.mult))
                    link(nc.vector.reduce_max(v3[:, :], wk[:, 0:E, :].rearrange(by_token), AX.X))
                    link(tt(oh[:, 0:E, :], rev[:, 0:E].unsqueeze(2).broadcast_to([P, E, NB]),
                            v3[:, :].unsqueeze(1).broadcast_to([P, E, NB]), ALU.is_equal))

                def rank(n, E):
                    tt = nc.vector.tensor_tensor
                    dve.wait_ge(rank_ready, n + 1)
                    fl = "p e b -> p (e b)"
                    cols = E * NB
                    link(nc.vector.tensor_tensor_scan(wk[:, 0:E, :].rearrange(fl), reset[:, 0:E, :].rearrange(fl),
                                                      s_bank[1][:, 0:cols], 0.0, ALU.mult, ALU.add))
                    link(tt(rk[:, 0:E, :].rearrange(fl), wk[:, 0:E, :].rearrange(fl), s_bank[1][:, 0:cols], ALU.subtract))
                    link(tt(rk[:, 0:E, :].rearrange(fl), rk[:, 0:E, :].rearrange(fl), s_bank[0][:, 0:cols], ALU.add))

                def to_slot(E, oh, k, add):
                    link(nc.vector.tensor_tensor(wk[:, 0:E, :], oh[:, 0:E, :], rk[:, 0:E, :], ALU.mult))
                    link(nc.vector.reduce_sum(v4[:, :], wk[:, 0:E, :].rearrange("p e b -> p b e"), AX.X))
                    nc.vector.tensor_scalar(slot[k][:, :], v4[:, :], float(add), None, ALU.add).then_inc(slots_ready, 1)

                def add_gathered(n0, ks, weights, stats_too):
                    n = n0
                    for b in range(NB):
                        for k in ks:
                            dve.wait_ge(g_in[n % RING], 16 * (n // RING + 1))
                            g = gb[n % RING]
                            if weights:
                                nc.vector.scalar_tensor_tensor(x[:, b, :], g[:, :], wt[k][:, b:b + 1], x[:, b, :],
                                                               ALU.mult, ALU.add).then_inc(g_used, 1)
                            else:
                                nc.vector.tensor_tensor(x[:, b, :], x[:, b, :], g[:, :], ALU.add).then_inc(g_used, 1)
                            n += 1
                            dve.wait_ge(g_used, n)
                        if stats_too:
                            stat(b)

                tt, ts = nc.vector.tensor_tensor, nc.vector.tensor_scalar
                if stage >= 1:
                    route(M0, 0, 2)
                    dve.wait_ge(M0.lg_done, NB)
                    E = E0
                    r = slice(0, E)
                    link(tt(lg[:, r, :], o_bank[:, 0:E * NB].rearrange("p (b e) -> p e b", e=E),
                            rb0[:, :].unsqueeze(2).broadcast_to([P, E, NB]), ALU.add))
                    link(nc.vector.reduce_max(v1[:, :], lg[:, r, :].rearrange("p e b -> p b e"), AX.X))
                    tt(wk[:, r, :], lg[:, r, :], v1[:, :].unsqueeze(1).broadcast_to([P, E, NB]), ALU.subtract)\
                        .then_inc(exp_in, 1)
                    dve.wait_ge(exp_out, 1)
                    link(nc.vector.reduce_sum(v2[:, :], pr[:, r, :].rearrange("p e b -> p b e"), AX.X))
                    link(nc.vector.reciprocal(v3[:, :], v2[:, :]))
                    link(tt(pr[:, r, :], pr[:, r, :], v3[:, :].unsqueeze(1).broadcast_to([P, E, NB]), ALU.mult))
                    top(E, pr, oh1, v1)
                    link(nc.vector.scalar_tensor_tensor(pr[:, r, :], oh1[:, r, :], -2.0, pr[:, r, :], ALU.mult, ALU.add))
                    top(E, pr, oh2, v2)
                    tt(selb[:, r, :], oh1[:, r, :], oh2[:, r, :], ALU.add).then_inc(sel_ready, 1)
                    link(tt(v3[:, :], v1[:, :], v2[:, :], ALU.add))
                    link(ts(v4[:, :], v3[:, :], 1e-9, None, ALU.max))
                    link(nc.vector.reciprocal(v3[:, :], v4[:, :]))
                    link(tt(wt[0][:, :], v1[:, :], v3[:, :], ALU.mult))
                    link(tt(wt[1][:, :], v2[:, :], v3[:, :], ALU.mult))
                    rank(0, E)
                    link(ts(wk[:, r, :], rk[:, r, :], float(CAP), None, ALU.is_lt))
                    link(tt(rk[:, r, :], rk[:, r, :], base0[:, :].unsqueeze(2).broadcast_to([P, E, NB]), ALU.add))
                    link(tt(rk[:, r, :], rk[:, r, :], wk[:, r, :], ALU.mult))
                    to_slot(E, oh1, 0, ZROW)
                    to_slot(E, oh2, 1, ZROW)

                    def body(i, j):
                        q, t = j % 2, 2 * PER * i + j
                        if within(t - 2, NT0):
                            u = (j - 2) % (2 * PER) // PER
                            dve.wait_ge(M0.y_full, t - 1)
                            if within(t - 4, NT0):
                                dve.wait_ge(M0.y_out[q], 16 * (PER * i + j // 2 - 1))
                            nc.vector.tensor_tensor(ysb[q][:, :, :], st_bank[q][:, 0:2 * DM].rearrange("p (h d) -> p h d", h=2),
                                                    b2s[u][:, :].unsqueeze(1).broadcast_to([P, 2, DM]), ALU.add)\
                                .then_inc(M0.y_evac, 1)
                    over_tiles0(dve, body)
                    add_gathered(0, (0, 1), True, stage >= 2)
                if stage >= 2:
                    dve.wait_ge(rstd_done, 3)
                    attention(L1, fill1, 1)
                if stage >= 3:
                    route(M1, 1, 4)
                    E = E1
                    link(tt(lg[:, :, :], o_bank[:, 0:E * NB].rearrange("p (b e) -> p e b", e=E),
                            reset[:, :, 1:2].broadcast_to([P, E, NB]), ALU.mult))
                    top(E, lg, oh1, v1)
                    link(ts(selb[:, :, :], oh1[:, :, :], 1.0, None, ALU.mult))
                    nc.vector.sem_inc(sel_ready, 1)
                    nc.vector.sem_inc(exp_in, 1)
                    dve.wait_ge(exp_out, 2)
                    link(ts(v3[:, :], v2[:, :], 1.0, None, ALU.add))
                    link(nc.vector.reciprocal(v4[:, :], v3[:, :]))
                    link(tt(xna[:, :, :], xna[:, :, :], v4[:, :].unsqueeze(2).broadcast_to([P, NB, DM]), ALU.mult))
                    rank(1, E)
                    link(tt(oh2[:, :, :], wk[:, :, NB - 1:NB].broadcast_to([P, E, NB]),
                            k128[:, :].unsqueeze(1).broadcast_to([P, E, NB]), ALU.is_gt))
                    link(nc.vector.reduce_sum(ntile[:, :], oh2[:, :, :], AX.X))
                    link(nc.vector.tensor_tensor_scan(tcum[:, :], reset[:, :, 1:2].rearrange("p e b -> p (e b)"),
                                                      ntile[:, :], 0.0, ALU.mult, ALU.add))
                    link(tt(base1[:, :], tcum[:, :], ntile[:, :], ALU.subtract))
                    link(ts(base1[:, :], base1[:, :], float(P), None, ALU.mult))
                    link(tt(rk[:, :, :], rk[:, :, :], base1[:, :].unsqueeze(2).broadcast_to([P, E, NB]), ALU.add))
                    tw = pr2[0:1, :, :]
                    link(tt(tw, tiota[:, :].unsqueeze(2).broadcast_to([1, NT1, E]),
                            tcum[0:1, :].unsqueeze(1).broadcast_to([1, NT1, E]), ALU.is_ge))
                    link(nc.vector.reduce_sum(tef[:, :], tw, AX.X))
                    link(ts(tei[:, :], tef[:, :], float(E - 1), None, ALU.min))
                    to_slot(E, oh1, 2, 0)

                    def body(i, q):
                        t = 2 * i + q
                        if within(t - 1, NT1):
                            dve.wait_ge(M1.h_act, t)
                            need(dve, M1.y_full, t - 3 + 1)
                            nc.vector.tensor_tensor(hT[1 - q][:, :, 0:P], sg[1 - q][:, :, :],
                                                    s_bank[1 - q][:, 2 * P:4 * P].rearrange("p (c n) -> p c n", c=2),
                                                    ALU.mult).then_inc(M1.h_done, 1)
                        if within(t - 2, NT1):
                            dve.wait_ge(M1.y_full, t - 1)
                            if within(t - 4, NT1):
                                dve.wait_ge(M1.y_out[q], 16 * (i - 1))
                            nc.vector.tensor_copy(ysb[q][:, 0, :], st_bank[q][:, 0:DM]).then_inc(M1.y_evac, 1)
                    over_tiles1(dve, body)
                    add_gathered(2 * NB, (2,), False, False)


def kernel(x, ctx_768, mask_BxS_bk0, L0_xattn_Wq, L0_xattn_Wkv, L0_ffn_router_w, L0_ffn_router_b, L0_ffn_w1,
           L0_ffn_b1, L0_ffn_w2, L0_ffn_b2, L1_xattn_w_q, L1_xattn_w_k, L1_xattn_w_v, L1_xattn_w_out,
           L1_xattn_b_out, L1_ffn_w_router, L1_ffn_gate_up_proj, L1_ffn_down_proj, L1_ffn_w_gate, L1_ffn_w_up,
           L1_ffn_w_down):
    import concourse.bacc as bacc
    from concourse.bass_utils import run_bass_kernel_spmd as run

    def lay(v):
        return np.ascontiguousarray(v)

    x = np.asarray(x)
    head = np.zeros((2 * QH, QH, P), np.float32)
    for j in range(QH):
        head[j, j] = head[QH + j, j] = -1.0
    hm = np.zeros((P, NH), np.float32)
    for h in range(NH):
        hm[D0 * h:D0 * (h + 1), h] = 1.0
    arrays = {
        "x": lay(x.transpose(1, 0, 2)),
        "ctxT": lay(np.asarray(ctx_768).transpose(2, 0, 1).reshape(DC, NB * P)),
        "mask": lay(np.asarray(mask_BxS_bk0).T),
        "wq0": lay(np.asarray(L0_xattn_Wq).T),
        "wk0": lay(np.asarray(L0_xattn_Wkv)[:DM].T),
        "wv0": lay(np.asarray(L0_xattn_Wkv)[DM:].T),
        "wq1": lay(np.asarray(L1_xattn_w_q)),
        "wk1": lay(np.asarray(L1_xattn_w_k)),
        "wv1": lay(np.asarray(L1_xattn_w_v)),
        "wo1": lay(np.asarray(L1_xattn_w_out).reshape(NCH, P, DM).transpose(1, 0, 2)),
        "bo1": lay(np.broadcast_to(np.asarray(L1_xattn_b_out), (P, DM))),
        "ident": np.eye(P, dtype=np.float32),
        "sel": head,
        "hmask": hm,
        "mhalf": np.full((P, NB), -0.5, np.float32),
        "tri": np.triu(np.ones((P, P), np.float32), 1),
        "rw0": lay(np.asarray(L0_ffn_router_w)),
        "rw1": lay(np.asarray(L1_ffn_w_router).T),
        "rb0": lay(np.broadcast_to(np.asarray(L0_ffn_router_b), (P, E0))),
        "rev": lay(np.broadcast_to(E1 - np.arange(E1, dtype=np.float32), (P, E1))),
        "base0": lay(np.broadcast_to(CAP * np.arange(E0, dtype=np.float32) - ZROW, (P, E0))),
        "k128": lay(np.broadcast_to(P * np.arange(NB, dtype=np.float32), (P, NB))),
        "tiota": np.arange(NT1, dtype=np.float32)[None],
        "reset": lay(np.broadcast_to((np.arange(NB) > 0).astype(np.float32), (P, E1, NB))),
        "gu": lay(np.asarray(L1_ffn_gate_up_proj).transpose(1, 0, 2)),
        "dn": lay(np.asarray(L1_ffn_down_proj).reshape(E1, 2, P, DM).transpose(2, 0, 1, 3)),
        "wgu": lay(np.concatenate([np.asarray(L1_ffn_w_gate).T, np.asarray(L1_ffn_w_up).T], 1)),
        "wdn": lay(np.asarray(L1_ffn_w_down).T.reshape(2, P, DM).transpose(1, 0, 2)),
        "zero": np.zeros((P, 8 * DM), np.float32),
        "w1": lay(np.asarray(L0_ffn_w1)),
        "w2": lay(np.asarray(L0_ffn_w2).reshape(E0, 2, P, DM).transpose(0, 2, 1, 3)),
        "b1": lay(np.asarray(L0_ffn_b1).reshape(E0, 2, P).transpose(0, 2, 1)),
        "b2": lay(np.broadcast_to(np.asarray(L0_ffn_b2)[:, None], (E0, P, DM))),
    }
    nc = bacc.Bacc("TRN2", target_bir_lowering=False, num_devices=1)
    a = {n: nc.dram_tensor(f"in_{n}", v.shape, mybir.dt.from_np(v.dtype), kind="ExternalInput").ap()
         for n, v in arrays.items()}
    out = nc.dram_tensor("out", (P, NB, DM), F32, kind="ExternalOutput").ap()
    build(nc, a, out)
    r = run(nc, [{f"in_{n}": v for n, v in arrays.items()}], core_ids=[0])
    return r.results[0]["out"].transpose(1, 0, 2)
```

```python
import numpy as np
import concourse.bass as bass
from concourse import mybir
from contextlib import ExitStack

F32 = mybir.dt.float32
BF16 = mybir.dt.bfloat16
I32 = mybir.dt.int32
U8 = mybir.dt.uint8
ALU = mybir.AluOpType
ACT = mybir.ActivationFunctionType
AX = mybir.AxisListType

NB = 32
P = 128
DM = 128
DC = 96
NH = 16
QH = 4
NQ = NH // QH
D0, D1 = 8, 64
NCH = NH * D1 // P
E0, F0, CAP = 8, 256, 1280
E1, F1 = 16, 256
EPS = 1e-5
LAST = NB - 1


def need(eng, sem, value):
    if isinstance(value, int) and value <= 0:
        return
    eng.wait_ge(sem, value)


def over_batches(eng, body):
    for b in range(-2, 3):
        body((b + 1) // 2, b - 2 * ((b + 1) // 2))
    with eng.Fori(1, NB // 2 - 2) as i:
        body(i, 1)
        body(i, 2)
    for b in range(NB - 3, NB + 2):
        body((b - 1) // 2, 2 - b % 2)


def inside(b):
    return not isinstance(b, int) or 0 <= b <= LAST


FILLS = (
    ((("k", 1),), (("v", 1),), (("xT", 2),), (("q", 2),)),
    ((("q0", 1), ("k0", 1)), (("q1", 1), ("k1", 1)), (("v0", 1), ("oT0", -1)), (("v1", 1), ("oT1", -1), ("xT", 2))),
)


def number_fills(layer):
    numbers = {}
    for b in range(-2, NB + 2):
        for step in FILLS[layer]:
            for name, ahead in step:
                if 0 <= b + ahead <= LAST:
                    numbers[b, name] = len(numbers)
    return numbers


NUMBERS = (number_fills(0), number_fills(1))


def fill_of(layer, i, off, name):
    if isinstance(i, int):
        f = NUMBERS[layer][2 * i + off, name]
        return f % 2, f // 2
    per = sum(len(step) for step in FILLS[layer])
    f = NUMBERS[layer][2 + off, name]
    return f % 2, f // 2 + per * (i - 1)


def fill0(i, off, name):
    return fill_of(0, i, off, name)


def fill1(i, off, name):
    return fill_of(1, i, off, name)


NT0, PER = E0 * CAP // (2 * P), CAP // (2 * P)
NT1 = NB + E1
ZROW = E0 * CAP
RING = 8
ZR = 4
R0, R1 = 5, 4
LAG0, LAG1 = R0 + 3, R1 + 3


def over_pairs(eng, body):
    for i in range(2):
        body(i, 0)
        body(i, 1)
    with eng.Fori(2, NB // 2) as i:
        body(i, 0)
        body(i, 1)
    body(NB // 2, 0)
    body(NB // 2, 1)


def over_tiles0(eng, body, drain=2):
    for j in range(2 * PER):
        body(0, j)
    with eng.Fori(1, E0 // 2) as i:
        for j in range(2 * PER):
            body(i, j)
    for j in range(drain):
        body(E0 // 2, j)


def over_tiles1(eng, body, drain=2):
    for i in range(2):
        for u in range(R1):
            body(i, u)
    with eng.Fori(2, NT1 // R1) as i:
        for u in range(R1):
            body(i, u)
    for u in range(drain):
        body(NT1 // R1 + u // R1, u % R1)


def within(t, n):
    return not isinstance(t, int) or 0 <= t < n


def build(nc, a, out, stage=9):
    ctx = ExitStack()
    with ctx:
        def sb(name, shape, dt=F32):
            return ctx.enter_context(nc.sbuf_tensor(name, shape, dt))

        def sem(name):
            return ctx.enter_context(nc.semaphore(name))

        x = sb("x", [P, NB, DM])
        ident = sb("ident", [P, P])
        identb = sb("identb", [P, P], BF16)
        sel = sb("sel", [QH, QH, P], BF16)
        hmask = sb("hmask", [P, NH])
        mask8 = sb("mask8", [P, NB], U8)
        mask = sb("mask", [P, NB])
        mhalf = sb("mhalf", [P, NB])
        stats = sb("stats", [P, NB, 6])
        mean = sb("mean", [P, NB])
        ln = [sb(f"ln{n}", [P, NB]) for n in range(4)]
        rstd = sb("rstd", [P, NB])
        wq0 = sb("wq0", [DM, DM])
        wk0 = sb("wk0", [DC, DM])
        wv0 = sb("wv0", [DC, DM])
        wq1 = sb("wq1", [DM, NH * D1])
        wk1 = sb("wk1", [DC, NH * D1])
        wv1 = sb("wv1", [DC, NH * D1])
        wo1 = sb("wo1", [P, NCH, DM])
        bo1 = sb("bo1", [P, DM])
        xn = [sb(f"xn{p}", [P, DM]) for p in range(2)]
        xnT = [sb(f"xnT{p}", [DM, P]) for p in range(2)]
        ctxT = [sb(f"ctxT{p}", [DC, P]) for p in range(2)]
        qpads = sb("qpads", [P, 2 * NH, P])
        qpad = [qpads[:, p * NH:(p + 1) * NH, :] for p in range(2)]
        kTs = sb("kTs", [P, 2 * NCH, P])
        kT = [kTs[:, p * NCH:(p + 1) * NCH, :] for p in range(2)]
        qT = [sb(f"qT{p}", [P, P]) for p in range(2)]
        qpadb = [sb(f"qpadb{p}", [P, NH, P], BF16) for p in range(2)]
        kTb = [sb(f"kTb{p}", [P, NCH, P], BF16) for p in range(2)]
        va0 = [[sb(f"va0{p}{n}", [P, NH, D0 + 1], BF16) for n in "hl"] for p in range(2)]
        va1 = [[sb(f"va1{p}{n}", [P, NH, D1 + 1], BF16) for n in "hl"] for p in range(2)]
        cm = [sb(f"cm{p}", [P, QH], BF16) for p in range(2)]
        cT = [sb(f"cT{p}", [QH, P], BF16) for p in range(2)]
        pT = [sb(f"pT{p}", [P, QH, P]) for p in range(2)]
        ph = [sb(f"ph{g}", [P, QH, P], BF16) for g in range(NQ)]
        pl = [sb(f"pl{g}", [P, QH, P], BF16) for g in range(NQ)]
        rden = sb("rden", [P, QH])
        oraw = sb("oraw", [P, NH, D0 + 1])
        rden0 = sb("rden0", [P, NH])
        o0 = sb("o0", [P, NH, D0])
        o1s = sb("o1s", [P, 2 * NH, D1])
        o1 = [o1s[:, p * NH:(p + 1) * NH, :] for p in range(2)]
        oT = sb("oT", [P, NCH, P])
        ysum = sb("ysum", [P, DM])

        xna = qpads
        tri = sb("tri", [P, P], BF16)
        ones = sb("ones", [P, P], BF16)
        rw = [sb("rw0", [DM, E0]), sb("rw1", [DM, E1])]
        rb0 = sb("rb0", [P, E0])
        rev = sb("rev", [P, E1])
        base0 = sb("base0", [P, E0])
        k128 = sb("k128", [P, NB])
        tiota = sb("tiota", [1, NT1])
        reset = sb("reset", [P, E1, NB])
        RT = [P, E1, NB]
        lg, pr, wk, oh1, oh2, rk = [sb(n, RT) for n in ("lg", "pr", "wk", "oh1", "oh2", "rk")]
        selb = sb("selb", RT, BF16)
        triw = wk[:, 0:P // NB, :].rearrange("p e b -> p (e b)")
        selw = rk[0:QH, :, :].rearrange("p e b -> p (e b)").rearrange("p (h n) -> p h n", h=QH)
        v1, v2, v3, v4 = [sb(n, [P, NB]) for n in ("v1", "v2", "v3", "v4")]
        wt = [sb(f"wt{k}", [P, NB]) for k in range(2)]
        slot = [sb(f"slot{k}", [P, NB], I32) for k in range(3)]
        ntile, tcum, base1 = [sb(n, [P, E1]) for n in ("ntile", "tcum", "base1")]
        tile_past = qpadb[0][0:1, :, :].rearrange("p h n -> p (h n)").bitcast(F32)[:, 0:NT1 * E1]\
            .rearrange("p (t e) -> p t e", e=E1)
        tef = sb("tef", [1, NT1])
        tei = sb("tei", [1, NT1], I32)
        zero = sb("zero", [P, ZR * DM])
        w1s = [sb(f"w1s{p}", [DM, F0]) for p in range(2)]
        w2s = [sb(f"w2s{p}", [P, 2, DM]) for p in range(2)]
        b1s = [sb(f"b1s{p}", [P, 2]) for p in range(2)]
        b2s = [sb(f"b2s{p}", [P, DM]) for p in range(2)]
        xs = [qpads[:, 2 * r:2 * r + 2, :] for r in range(R0)]
        xsT = [sb(f"xsT{p}", [DM, 2, P]) for p in range(2)]
        hT = [sb(f"hT{p}", [P, 2, 2 * P]) for p in range(2)]
        sg = [sb(f"sg{p}", [P, 2, P]) for p in range(2)]
        ysb = [qpads[:, 2 * (R0 + r):2 * (R0 + r) + 2, :] for r in range(R0)]
        gb = [sb(f"gb{r}", [P, DM]) for r in range(RING)]
        gu = sb("gu", [DM, E1, 2 * F1])
        dn = sb("dn", [P, E1, 2, DM])
        hid = [sb(f"hid{p}", [P, F1]) for p in range(2)]
        wgu = sb("wgu", [DM, 2 * F1])
        wdn = sb("wdn", [P, 2, DM])

        buf0 = nc.dram_tensor("buf0", (ZROW, DM), F32, kind="Internal").ap()
        eo0 = nc.dram_tensor("eo0", (ZROW + P, DM), F32, kind="Internal").ap()
        buf1 = nc.dram_tensor("buf1", (NT1 * P, DM), F32, kind="Internal").ap()
        eo1 = nc.dram_tensor("eo1", (NT1 * P, DM), F32, kind="Internal").ap()

        bank = [ctx.enter_context(nc.psum_tensor(f"bank{n}", [P, 512], F32)) for n in range(7)]
        cbank = ctx.enter_context(nc.psum_tensor("cbank", [P, 1024], BF16))
        s_bank, st_bank, pj_bank, o_bank = bank[0:2], bank[2:4], bank[4:6], bank[6]

        loaded = sem("loaded")
        masked = sem("masked")
        stat_done = sem("stat_done")
        ln_step = sem("ln_step")
        rstd_done = sem("rstd_done")
        const_done = sem("const_done")
        stored = sem("stored")
        zeroed = sem("zeroed")
        zset = sem("zset")
        rt = sem("rt")
        exp_in, exp_out = sem("exp_in"), sem("exp_out")
        sel_ready, rank_ready = sem("sel_ready"), sem("rank_ready")
        slots_ready = sem("slots_ready")
        qpad_zero = sem("qpad_zero")
        g_in = [sem(f"g_in{r}") for r in range(RING)]
        g_used = sem("g_used")

        class Moe:
            def __init__(self, n):
                self.xr_ready = sem(f"xr_ready_{n}")
                self.xr_copied = sem(f"xr_copied_{n}")
                self.t_full = sem(f"t_full_{n}")
                self.t_evac = sem(f"t_evac_{n}")
                self.lg_done = sem(f"lg_done_{n}")
                self.scattered = sem(f"scattered_{n}")
                self.sg_done = sem(f"sg_done_{n}")
                self.sh_done = sem(f"sh_done_{n}")
                self.sy_full = sem(f"sy_full_{n}")
                self.sy_done = sem(f"sy_done_{n}")
                self.ht_full = sem(f"ht_full_{n}")
                self.ht_evac = sem(f"ht_evac_{n}")
                self.xt_full = sem(f"xt_full_{n}")
                self.xt_evac = sem(f"xt_evac_{n}")
                self.h_full = sem(f"h_full_{n}")
                self.h_act = sem(f"h_act_{n}")
                self.h_done = sem(f"h_done_{n}")
                self.y_full = sem(f"y_full_{n}")
                self.y_evac = sem(f"y_evac_{n}")
                self.w_in = [sem(f"w_in{n}{p}") for p in range(2)]
                self.xs_in = [sem(f"xs_in{n}{p}") for p in range(R0)]
                self.y_out = [sem(f"y_out{n}{p}") for p in range(R0)]
        M0, M1 = Moe(0), Moe(1)

        class Layer:
            def __init__(self, n):
                self.ctx_in = [sem(f"ctx_in{n}{p}") for p in range(2)]
                self.xn_ready = sem(f"xn_ready{n}")
                self.pj_full = [sem(f"pj_full{n}{p}") for p in range(2)]
                self.pj_free = [sem(f"pj_free{n}{p}") for p in range(2)]
                self.s_full = sem(f"s_full{n}")
                self.max_done = sem(f"max_done{n}")
                self.qT_done = sem(f"qT_done{n}")
                self.qpad_done = sem(f"qpad_done{n}")
                self.cast_done = sem(f"cast_done{n}")
                self.vh_done = sem(f"vh_done{n}")
                self.ph_done = sem(f"ph_done{n}")
                self.pl_done = sem(f"pl_done{n}")
                self.c_full = sem(f"c_full{n}")
                self.c_free = sem(f"c_free{n}")
                self.st_full = sem(f"st_full{n}")
                self.exp_done = sem(f"exp_done{n}")
                self.pv_full = sem(f"pv_full{n}")
                self.rden_done = sem(f"rden_done{n}")
                self.o_done = sem(f"o_done{n}")
                self.pv_free = sem(f"pv_free{n}")
                self.y_full = sem(f"y_full{n}")
                self.y_free = sem(f"y_free{n}")
                self.x_done = sem(f"x_done{n}")
        L0, L1 = Layer(0), Layer(1)

        NZERO = -(-ZROW // (ZR * P)) + -(-NT1 // ZR) + 1

        with nc.Block() as block:
            NLOAD = 16 * 28

            @block.sync
            def _(sp):
                sp.dma_start(x[:, :, :], a["x"]).then_inc(loaded, 16)
                for dst, name in ((ident, "ident"), (selw, "sel"), (hmask, "hmask"), (mask8, "mask"),
                                  (mhalf, "mhalf"), (wq0, "wq0"), (wk0, "wk0"), (wv0, "wv0"),
                                  (wq1, "wq1"), (wk1, "wk1"), (wv1, "wv1"), (wo1, "wo1"), (bo1, "bo1"),
                                  (triw, "tri"), (rw[0], "rw0"), (rw[1], "rw1"), (rb0, "rb0"), (rev, "rev"),
                                  (base0, "base0"), (k128, "k128"), (tiota, "tiota"), (reset, "reset"),
                                  (gu, "gu"), (dn, "dn"), (wgu, "wgu"), (wdn, "wdn"), (zero, "zero")):
                    sp.dma_start(dst[(slice(None),) * len(dst.shape)], a[name]).then_inc(loaded, 16)

                def attention(L, fill, lastv):
                    def body(i, off):
                        b = 2 * i + off
                        if isinstance(b, int) and b < -1 or not inside(b + 1):
                            return
                        at = (b + 1) * P
                        if not isinstance(at, int):
                            at = sp.snap(at)
                        if inside(b - 1):
                            bk, k = fill(i, off - 2, lastv)
                            need(sp, L.pj_full[bk], k + 1)
                        sp.dma_start(ctxT[(off + 1) % 2][:, :], a["ctxT"][:, bass.ds(at, P)])\
                            .then_inc(L.ctx_in[(off + 1) % 2], 16)
                    over_batches(sp, body)
                sp.wait_ge(loaded, NLOAD)
                nz = 0
                for buf, rows in ((buf0, ZROW), (buf1, NT1 * P)):
                    for r in range(0, rows, ZR * P):
                        m = min(ZR * P, rows - r) // P
                        sp.dma_start(buf[r:r + m * P, :].rearrange("(p m) d -> p (m d)", p=P), zero[:, 0:m * DM])\
                            .then_inc(zeroed, 16)
                        nz += 1
                sp.dma_start(eo0[ZROW:ZROW + P, :], zero[:, 0:DM]).then_inc(zeroed, 16)
                assert nz + 1 == NZERO
                attention(L0, fill0, "v")
                if stage >= 1:
                    sp.wait_ge(M0.scattered, 16 * 2 * NB)
                    tiles0 = range(2)

                    def body(i, j):
                        u, q, t = j // PER % 2, j % 2, 2 * PER * i + j
                        if j % PER == 0 and within(t, NT0):
                            need(sp, M0.y_evac, t - PER)
                            e = 2 * i + u
                            for dst, name in ((w1s, "w1"), (w2s, "w2"), (b1s, "b1"), (b2s, "b2")):
                                src = a[name][e] if isinstance(e, int) else a[name][bass.ds(e, 1)]
                                if not isinstance(e, int):
                                    src = src.squeeze(0)
                                sp.dma_start(dst[u][:], src).then_inc(M0.w_in[u], 16)
                        r, rs = j % R0, (j - LAG0) % R0
                        if within(t, NT0):
                            need(sp, M0.xt_full, t - R0 + 1)
                            sp.dma_start(xs[r][:, :, :], buf0[bass.ds(t * 2 * P, 2 * P), :]
                                         .rearrange("(h p) d -> p h d", p=P)).then_inc(M0.xs_in[r], 16)
                        if within(t - LAG0, NT0):
                            sp.wait_ge(M0.y_evac, t - LAG0 + 1)
                            sp.dma_start(eo0[bass.ds((t - LAG0) * 2 * P, 2 * P), :].rearrange("(h p) d -> p h d", p=P),
                                         ysb[rs][:, :, :]).then_inc(M0.y_out[rs], 16)
                    over_tiles0(sp, body, LAG0)
                if stage >= 2:
                    attention(L1, fill1, "v1")
                if stage >= 3:
                    sp.wait_ge(M1.scattered, 16 * NB)

                    def body(i, u):
                        t, us = R1 * i + u, (u - LAG1) % R1
                        if within(t, NT1):
                            need(sp, M1.xt_full, t - R1 + 1)
                            sp.dma_start(xs[u][:, 0, :], buf1[bass.ds(t * P, P), :]).then_inc(M1.xs_in[u], 16)
                        if within(t - LAG1, NT1):
                            sp.wait_ge(M1.y_evac, t - LAG1 + 1)
                            sp.dma_start(eo1[bass.ds((t - LAG1) * P, P), :], ysb[us][:, 0, :]).then_inc(M1.y_out[us], 16)
                    over_tiles1(sp, body, LAG1)
                if stage == 0:
                    sp.wait_ge(L0.x_done, NB)
                elif stage == 1:
                    sp.wait_ge(g_used, 2 * NB)
                elif stage == 2:
                    sp.wait_ge(L1.x_done, NB)
                else:
                    sp.wait_ge(g_used, 3 * NB)
                sp.dma_start(out, x[:, :, :]).then_inc(stored, 16)
                sp.wait_ge(stored, 16)

            @block.gpsimd
            def _(pool):
                for p in range(2):
                    for part in range(2):
                        nc.gpsimd.memset(va0[p][part][:, :, D0:D0 + 1], 1.0 - part).then_inc(const_done, 1)
                        nc.gpsimd.memset(va1[p][part][:, :, D1:D1 + 1], 1.0 - part).then_inc(const_done, 1)
                pool.wait_ge(loaded, NLOAD)
                nc.gpsimd.tensor_copy(identb[:, :], ident[:, :]).then_inc(const_done, 1)
                nc.gpsimd.tensor_copy(sel[:, :, :], selw[:, :, :]).then_inc(const_done, 1)
                nc.gpsimd.tensor_copy(tri[:, :], triw[:, :]).then_inc(const_done, 1)
                nc.gpsimd.memset(ones[:, :], 1.0).then_inc(const_done, 1)
                nc.gpsimd.tensor_copy(mask[:, :], mask8[:, :]).then_inc(masked, 1)

                def norm(n):
                    even, odd = 1, 4
                    steps = [0]

                    def step(ins):
                        steps[0] += 1
                        ins.then_inc(ln_step, 1)
                        pool.wait_ge(ln_step, 9 * (n - 1) + steps[0])
                    tt, ts = nc.gpsimd.tensor_tensor, nc.gpsimd.tensor_scalar
                    pool.wait_ge(stat_done, NB * n)
                    step(tt(ln[0][:, :], stats[:, :, even], stats[:, :, odd], ALU.add))
                    step(ts(mean[:, :], ln[0][:, :], 0.5, None, ALU.mult))
                    step(tt(ln[1][:, :], stats[:, :, even], stats[:, :, odd], ALU.subtract))
                    step(tt(ln[2][:, :], ln[1][:, :], ln[1][:, :], ALU.mult))
                    step(ts(ln[3][:, :], ln[2][:, :], 0.25, EPS, ALU.mult, ALU.add))
                    step(tt(ln[0][:, :], stats[:, :, even + 1], stats[:, :, odd + 1], ALU.add))
                    step(ts(ln[1][:, :], ln[0][:, :], 1.0 / DM, None, ALU.mult))
                    step(tt(ln[2][:, :], ln[1][:, :], ln[3][:, :], ALU.add))
                    ins = tt(rstd[:, :], ln[2][:, :], mhalf[:, :], ALU.pow)
                    step(ins)
                    nc.gpsimd.sem_inc(rstd_done, 1)
                norm(1)

                def attention(L, fill, layer):
                    def body(i, off):
                        b = 2 * i + off
                        for g in range(NQ):
                            Q = NQ * b + g
                            if inside(b):
                                pool.wait_ge(L.exp_done, Q + 1)
                                pool.wait_ge(L.ph_done, Q + 1)
                                need(pool, L.pv_full, Q - 3)
                                nc.gpsimd.tensor_tensor(pl[g][:, :, :], pT[g % 2][:, :, :], ph[g][:, :, :],
                                                        ALU.subtract).then_inc(L.pl_done, 1)
                    over_batches(pool, body)
                attention(L0, fill0, 0)

                def keep_tokens(M):
                    def body(i, u):
                        b = 2 * i + u
                        if within(b, NB):
                            pool.wait_ge(M.xr_ready, b + 1)
                            nc.gpsimd.tensor_copy(xna[:, b, :], xn[u][:, :]).then_inc(M.xr_copied, 1)
                    over_pairs(pool, body)

                def scatter(M, ks, buf, bound):
                    for b in range(NB):
                        for k in ks:
                            nc.gpsimd.indirect_dma_start(
                                out=buf[:, :], out_offset=bass.IndirectOffsetOnAxis(ap=slot[k][:, b:b + 1], axis=0),
                                in_=xna[:, b, :], in_offset=None, bounds_check=bound, oob_is_err=False)\
                                .then_inc(M.scattered, 16)

                def gather(n0, ks, src):
                    n = n0
                    for b in range(NB):
                        for k in ks:
                            if n >= RING:
                                pool.wait_ge(g_used, n - RING + 1)
                            nc.gpsimd.indirect_dma_start(
                                out=gb[n % RING][:, :], out_offset=None, in_=src[:, :],
                                in_offset=bass.IndirectOffsetOnAxis(ap=slot[k][:, b:b + 1], axis=0))\
                                .then_inc(g_in[n % RING], 16)
                            n += 1
                if stage >= 1:
                    norm(2)
                    keep_tokens(M0)
                    pool.wait_ge(slots_ready, 2)
                    pool.wait_ge(zeroed, 16 * NZERO)
                    pool.wait_ge(M0.xr_copied, NB)
                    scatter(M0, (0, 1), buf0, ZROW - 1)
                    for r in range(R0):
                        pool.wait_ge(M0.y_out[r], 16 * NT0 // R0)
                    gather(0, (0, 1), eo0)
                if stage >= 2:
                    pool.wait_ge(L0.st_full, NB * NQ)
                    for p in range(2):
                        nc.gpsimd.memset(qpad[p][:, :, :], 0.0).then_inc(qpad_zero, 1)
                    norm(3)
                if stage >= 2:
                    attention(L1, fill1, 1)
                if stage >= 3:
                    norm(4)
                    pool.wait_ge(slots_ready, 3)
                    pool.wait_ge(M1.xr_copied, NB)
                    scatter(M1, (2,), buf1, NT1 * P - 1)
                    for u in range(R1):
                        pool.wait_ge(M1.y_out[u], 16 * NT1 // R1)
                    gather(2 * NB, (2,), eo1)

            @block.tensor
            def _(pe):
                pe.wait_ge(loaded, NLOAD)
                pe.wait_ge(const_done, 12)

                def shifted(Q, g, j, last):
                    return nc.tensor.matmul(st_bank[g % 2][:, j * P:(j + 1) * P], sel[:, j, :], cT[g % 2][:, :],
                                            start=False, stop=last)

                def attention(L, fill, layer):
                    D = (D0, D1)[layer]
                    va = (va0, va1)[layer]

                    def evacuated(i, off, name):
                        bk, k = fill(i, off, name)
                        pe.wait_ge(L.pj_free[bk], k + 1)

                    def project(i, off, name, ahead):
                        b, p = 2 * i + off + ahead, (off + ahead) % 2
                        if not inside(b):
                            return
                        bk, k = fill(i, off, name)
                        need(pe, L.pj_free[bk], k)
                        ps = pj_bank[bk]
                        what, half = name[0], int(name[-1] == "1")
                        if name == "xT":
                            pe.wait_ge(L.xn_ready, b + 1)
                            last = nc.tensor.transpose(ps[:, 0:P], xn[p][:, :], ident[:, :])
                        elif what == "o":
                            pe.wait_ge(L.pv_free, NQ * b + 2 * half + 2)
                            for c in range(4):
                                last = nc.tensor.transpose(ps[:, c * P:(c + 1) * P],
                                                           o1[p][:, 8 * half + 2 * c:8 * half + 2 * c + 2, :], ident[:, :])
                        else:
                            if name in ("q", "q0"):
                                evacuated(i, off - layer, "xT")
                            if name in ("k", "k0"):
                                pe.wait_ge(L.ctx_in[p], 16 * (i + (off + 1) // 2 + 1))
                            if layer == 0 and what == "v":
                                last = nc.tensor.matmul(ps[:, 0:P], ctxT[p][:, :], wv0[:, :], start=True, stop=True)
                            elif what == "v":
                                last = nc.tensor.matmul(ps[:, :], ctxT[p][:, :], wv1[:, 512 * half:512 * (half + 1)],
                                                        start=True, stop=True)
                            else:
                                w = ((wq0, wk0), (wq1, wk1))[layer][what == "k"]
                                rhs = xnT[p] if what == "q" else ctxT[p]
                                for c in range(4 if layer else 1):
                                    n = 4 * half + c
                                    last = nc.tensor.matmul(ps[:, c * P:(c + 1) * P], w[:, n * P:(n + 1) * P],
                                                            rhs[:, :], start=True, stop=True)
                        last.then_inc(L.pj_full[bk], 1)

                    def body(i, off):
                        b = 2 * i + off
                        p, pn = off % 2, (off + 1) % 2
                        for g in range(NQ):
                            Q = NQ * b + g
                            fills = FILLS[layer][g]
                            for name, ahead in fills[:layer]:
                                project(i, off, name, ahead)

                            st = st_bank[g % 2]
                            if inside(b):
                                need(pe, L.exp_done, Q - 1)
                                if layer == 0:
                                    need(pe, L.ph_done, Q - 1)
                                    nc.tensor.matmul(st[:, :], kT[p][:, 0, :], qpad[p][:, QH * g:QH * (g + 1), :],
                                                     start=True, stop=False)
                                else:
                                    for c in range(2):
                                        nc.tensor.matmul(st[:, 2 * c * P:2 * (c + 1) * P], kT[p][:, 2 * g + c, :],
                                                         qpad[p][:, QH * g + 2 * c:QH * g + 2 * c + 2, :],
                                                         start=(c == 0), stop=False)

                            if inside(b + (g + 1) // NQ):
                                pe.wait_ge(L.max_done, Q + 2)
                                need(pe, L.c_free, Q + 1)
                                nc.tensor.transpose(cbank[0:QH, 0:P], cm[(g + 1) % 2][:, :], identb[:, :])\
                                    .then_inc(L.c_full, 1)

                            if inside(b):
                                pe.wait_ge(L.c_free, Q + 1)
                                for j in range(QH):
                                    last = nc.tensor.matmul(st[:, j * P:(j + 1) * P], sel[:, j, :], cT[g % 2][:, :],
                                                            start=False, stop=(j == QH - 1))
                                last.then_inc(L.st_full, 1)

                            bs, gs = b + (g + 2) // NQ, (g + 2) % NQ
                            ps_ = p if g < 2 else pn
                            if inside(bs):
                                if layer == 0:
                                    pe.wait_ge(L.cast_done, NQ * bs + gs + 1)
                                    if gs == 0:
                                        evacuated(i, off, "k")
                                elif gs % 2 == 0:
                                    pe.wait_ge(L.cast_done, 4 * bs + gs + 2)
                                need(pe, L.max_done, Q + 1)
                                for j in range(QH):
                                    h = QH * gs + j
                                    last = nc.tensor.matmul(s_bank[g % 2][:, j * P:(j + 1) * P], qpadb[ps_][:, h, :],
                                                            kTb[ps_][:, h // 2 if layer else 0, :], start=True, stop=True)
                                last.then_inc(L.s_full, 1)

                            for name, ahead in fills[layer:]:
                                project(i, off, name, ahead)

                            if layer == 1 and g == 0 and inside(b - 2):
                                evacuated(i, off - 1, "oT1")
                                pe.wait_ge(L.pv_free, NQ * (b - 1) + (2 if inside(b - 1) else 0))
                                for c in range(NCH):
                                    last = nc.tensor.matmul(o_bank[:, 0:DM], oT[:, c, :], wo1[:, c, :],
                                                            start=(c == 0), stop=(c == NCH - 1))
                                last.then_inc(L.y_full, 1)

                            bo, go = b + (g - 2) // NQ, (g - 2) % NQ
                            po = p if g > 1 else pn
                            if inside(bo):
                                pe.wait_ge(L.pl_done, Q - 1)
                                if go == 0:
                                    evacuated(i, off - 1, "v" if layer == 0 else "v1")
                                need(pe, L.pv_free, Q - 2)
                                if layer == 1 and g == 0:
                                    need(pe, L.y_free, b - 1)
                                for j in range(QH):
                                    for n, (pp, part) in enumerate(((ph, 0), (ph, 1), (pl, 0), (pl, 1))):
                                        last = nc.tensor.matmul(o_bank[:, j * (D + 1):(j + 1) * (D + 1)],
                                                                pp[go][:, j, :], va[po][part][:, QH * go + j, :],
                                                                start=(n == 0), stop=(n == 3))
                                last.then_inc(L.pv_full, 1)
                    over_batches(pe, body)
                attention(L0, fill0, 0)

                def route(M, n):
                    E = (E0, E1)[n]

                    def transposed(b, u):
                        pe.wait_ge(M.xr_ready, b + 1)
                        need(pe, M.t_evac, b - 1)
                        nc.tensor.transpose(pj_bank[u][:, 0:P], xn[u][:, :], ident[:, :]).then_inc(M.t_full, 1)

                    def logits(b, u):
                        pe.wait_ge(M.t_evac, b + 1)
                        if n == 1:
                            need(pe, M.sh_done, b - 1)
                            for c in range(4):
                                nc.tensor.matmul(s_bank[u][:, c * P:(c + 1) * P], wgu[:, c * P:(c + 1) * P],
                                                 xnT[u][:, :], start=True, stop=True)
                        nc.tensor.matmul(o_bank[:, bass.ds(b * E, E)], xnT[u][:, :], rw[n][:, :],
                                         start=True, stop=True).then_inc(M.lg_done, 1)

                    def shared(b, u):
                        pe.wait_ge(M.sh_done, b + 1)
                        need(pe, M.sy_done, b - 1)
                        for c in range(2):
                            last = nc.tensor.matmul(st_bank[u][:, 0:DM], hT[u][:, c, 0:P], wdn[:, c, :],
                                                    start=(c == 0), stop=(c == 1))
                        last.then_inc(M.sy_full, 1)

                    def body(i, u):
                        b = 2 * i + u
                        if within(b, NB):
                            transposed(b, u)
                        if within(b - 1, NB):
                            logits(b - 1, 1 - u)
                        if n == 1 and within(b - 2, NB):
                            shared(b - 2, u)
                    over_pairs(pe, body)

                def ranks(n):
                    cols = (E0, E1)[n] * NB
                    flat = selb[:, 0:(E0, E1)[n], :].rearrange("p e b -> p (e b)")
                    pe.wait_ge(sel_ready, n + 1)
                    nc.tensor.matmul(s_bank[0][:, 0:cols], tri[:, :], flat, start=True, stop=True)
                    nc.tensor.matmul(s_bank[1][:, 0:cols], ones[:, :], flat, start=True, stop=True)\
                        .then_inc(rank_ready, 1)

                if stage >= 1:
                    route(M0, 0)
                    ranks(0)

                    def body(i, j):
                        q, t = j % 2, 2 * PER * i + j
                        if within(t, NT0):
                            r = j % R0
                            pe.wait_ge(M0.xs_in[r], 16 * (2 * PER // R0 * i + j // R0 + 1))
                            need(pe, M0.xt_evac, t - 1)
                            for h in range(2):
                                last = nc.tensor.transpose(pj_bank[q][:, h * P:(h + 1) * P], xs[r][:, h, :], ident[:, :])
                            last.then_inc(M0.xt_full, 1)
                        if within(t - 1, NT0):
                            jj, ii = (j - 1) % (2 * PER), i if j else i - 1
                            u = jj // PER
                            pe.wait_ge(M0.w_in[u], 64 * (ii + 1))
                            pe.wait_ge(M0.xt_evac, t)
                            need(pe, M0.h_done, t - 2)
                            for f in range(2):
                                last = nc.tensor.matmul(s_bank[1 - q][:, 2 * f * P:2 * (f + 1) * P],
                                                        w1s[u][:, f * P:(f + 1) * P], xsT[1 - q][:, :, :],
                                                        start=True, stop=True)
                            last.then_inc(M0.h_full, 1)
                        if within(t - 2, NT0):
                            u = (j - 2) % (2 * PER) // PER
                            pe.wait_ge(M0.h_done, t - 1)
                            need(pe, M0.y_evac, t - 3)
                            for h in range(2):
                                for f in range(2):
                                    last = nc.tensor.matmul(st_bank[q][:, h * DM:(h + 1) * DM],
                                                            hT[q][:, f, h * P:(h + 1) * P], w2s[u][:, f, :],
                                                            start=(f == 0), stop=(f == 1))
                            last.then_inc(M0.y_full, 1)
                    over_tiles0(pe, body)
                if stage >= 2:
                    pe.wait_ge(qpad_zero, 2)
                    attention(L1, fill1, 1)
                if stage >= 3:
                    route(M1, 1)
                    ranks(1)
                    pe.wait_ge(slots_ready, 3)

                    now = [pe.alloc_register(f"expert{u}") for u in range(R1)]
                    before = [pe.alloc_register(f"expert_before{u}") for u in range(R1)]

                    def expert_of(u):
                        return pe.snap((now[u] if u >= 0 else before[u + R1]), min_val=0, max_val=E1 - 1)

                    def body(i, u):
                        t, q = R1 * i + u, u % 2
                        if u == 0:
                            if within(t - 1, NT1):
                                for k in range(1, R1):
                                    pe.reg_mov(before[k], now[k])
                            if within(t, NT1):
                                pe.load(now, tei[0:1, bass.ds(t, R1)])
                        if within(t, NT1):
                            pe.wait_ge(M1.xs_in[u], 16 * (i + 1))
                            need(pe, M1.xt_evac, t - 1)
                            nc.tensor.transpose(pj_bank[q][:, 0:P], xs[u][:, 0, :], ident[:, :]).then_inc(M1.xt_full, 1)
                        if within(t - 1, NT1):
                            e = expert_of(u - 1)
                            pe.wait_ge(M1.xt_evac, t)
                            need(pe, M1.h_done, t - 2)
                            nc.tensor.matmul(s_bank[1 - q][:, :], xsT[1 - q][:, 0, :], gu[:, bass.ds(e, 1), :].squeeze(1),
                                             start=True, stop=True).then_inc(M1.h_full, 1)
                        if within(t - 2, NT1):
                            pe.wait_ge(M1.h_done, t - 1)
                            need(pe, M1.ht_evac, t - 3)
                            for f in range(2):
                                last = nc.tensor.transpose(st_bank[q][:, f * P:(f + 1) * P], hid[q][:, f * P:(f + 1) * P],
                                                           ident[:, :])
                            last.then_inc(M1.ht_full, 1)
                        if within(t - 3, NT1):
                            e = expert_of(u - 3)
                            pe.wait_ge(M1.ht_evac, t - 2)
                            need(pe, M1.y_evac, t - 3)
                            for f in range(2):
                                last = nc.tensor.matmul(o_bank[:, 0:DM], hT[1 - q][:, f, 0:P],
                                                        dn[:, bass.ds(e, 1), f, :].squeeze(1),
                                                        start=(f == 0), stop=(f == 1))
                            last.then_inc(M1.y_full, 1)
                    over_tiles1(pe, body, 3)

            @block.scalar
            def _(act):
                def attention(L, fill, layer):
                    D = (D0, D1)[layer]

                    def take(i, off, name, ahead):
                        b, p = 2 * i + off + ahead, (off + ahead) % 2
                        if not inside(b):
                            return
                        bk, k = fill(i, off, name)
                        act.wait_ge(L.pj_full[bk], k + 1)
                        ps, what, half = pj_bank[bk], name[0], int(name[-1] == "1")
                        if name == "xT":
                            if inside(b - 2):
                                bq, kq = fill(i, off - 2, "q") if layer == 0 else fill(i, off - 1, "q1")
                                need(act, L.pj_full[bq], kq + 1)
                            nc.scalar.copy(xnT[p][:, :], ps[:, 0:P]).then_inc(L.pj_free[bk], 1)
                        elif name == "q":
                            need(act, L.qpad_done, NQ * (b - 1))
                            nc.scalar.copy(qT[p][:, :], ps[:, 0:P]).then_inc(L.pj_free[bk], 1)
                        elif what == "q":
                            need(act, L.st_full, NQ * (b - 1))
                            for r in range(2):
                                rows = slice(D1 * r, D1 * (r + 1))
                                dst = qpad[p][rows, :, :].rearrange("p (c r) n -> p c r n", r=2)
                                last = nc.scalar.copy(dst[:, 4 * half:4 * half + 4, r, :],
                                                      ps[rows, :].rearrange("p (c n) -> p c n", c=4))
                            last.then_inc(L.pj_free[bk], 1)
                        elif what == "k":
                            need(act, L.st_full, NQ * (b - 1))
                            n = 4 if layer else 1
                            if layer == 0:
                                need(act, L.s_full, NQ * (b - 1))
                                nc.scalar.copy(kTb[p][:, 0, :], ps[:, 0:P])
                            nc.scalar.copy(kT[p][:, 4 * half:4 * half + n, :], ps[:, 0:n * P])\
                                .then_inc(L.pj_free[bk], 1)
                        elif what == "v":
                            need(act, L.pv_full, NQ * (b - 1))
                            n = NH // 2 if layer else NH
                            nc.scalar.copy((va0, va1)[layer][p][0][:, n * half:n * half + n, 0:D],
                                           ps[:, 0:n * D].rearrange("p (h d) -> p h d", d=D)).then_inc(L.vh_done, 1)
                        else:
                            need(act, L.y_full, b)
                            nc.scalar.copy(oT[:, 4 * half:4 * half + 4, :], ps[:, :]).then_inc(L.pj_free[bk], 1)

                    def body(i, off):
                        b = 2 * i + off
                        pn = (off + 1) % 2
                        for g in range(NQ):
                            Q = NQ * b + g
                            fills = FILLS[layer][g]
                            for name, ahead in fills[:layer]:
                                take(i, off, name, ahead)
                            if inside(b + (g + 1) // NQ):
                                act.wait_ge(L.c_full, Q + 2)
                                need(act, L.st_full, Q)
                                nc.scalar.copy(cT[(g + 1) % 2][:, :], cbank[0:QH, 0:P]).then_inc(L.c_free, 1)
                            if layer == 0:
                                bq, gq = (b, 3) if g == 0 else (b + 1, g - 1)
                                pq = off % 2 if g == 0 else pn
                                if inside(bq):
                                    act.wait_ge(L.qpad_done, NQ * bq + gq + 1)
                                    need(act, L.s_full, NQ * (bq - 2) + gq + 1)
                                    hs = slice(QH * gq, QH * gq + QH)
                                    nc.scalar.copy(qpadb[pq][:, hs, :], qpad[pq][:, hs, :]).then_inc(L.cast_done, 1)
                            if inside(b):
                                act.wait_ge(L.st_full, Q + 1)
                                need(act, L.pl_done, Q - 1)
                                nc.scalar.activation(pT[g % 2][:, :, :], st_bank[g % 2][:, :], ACT.Exp, scale=D ** -0.5)\
                                    .then_inc(L.exp_done, 1)
                                if layer == 0:
                                    need(act, L.pv_full, Q - 3)
                                    nc.scalar.activation(ph[g][:, :, :], st_bank[g % 2][:, :], ACT.Exp,
                                                         scale=D ** -0.5).then_inc(L.ph_done, 1)
                            for name, ahead in fills[layer:]:
                                take(i, off, name, ahead)
                    over_batches(act, body)
                attention(L0, fill0, 0)

                def route(M, n):
                    def body(i, u):
                        b = 2 * i + u
                        if within(b, NB):
                            act.wait_ge(M.t_full, b + 1)
                            need(act, M.lg_done, b - 1)
                            nc.scalar.copy(xnT[u][:, :], pj_bank[u][:, 0:P]).then_inc(M.t_evac, 1)
                        if n == 1 and within(b - 1, NB):
                            act.wait_ge(M.lg_done, b)
                            need(act, M.sh_done, b - 2)
                            nc.scalar.activation(sg[1 - u][:, :, :], s_bank[1 - u][:, 0:2 * P], ACT.Silu)\
                                .then_inc(M.sg_done, 1)
                    over_pairs(act, body)

                if stage >= 1:
                    route(M0, 0)
                    act.wait_ge(exp_in, 1)
                    nc.scalar.activation(pr[:, 0:E0, :], wk[:, 0:E0, :], ACT.Exp).then_inc(exp_out, 1)

                    def body(i, j):
                        q, t = j % 2, 2 * PER * i + j
                        if within(t, NT0):
                            act.wait_ge(M0.xt_full, t + 1)
                            need(act, M0.h_full, t - 1)
                            nc.scalar.copy(xsT[q][:, :, :], pj_bank[q][:, 0:2 * P]).then_inc(M0.xt_evac, 1)
                        if within(t - 1, NT0):
                            u = (j - 1) % (2 * PER) // PER
                            act.wait_ge(M0.h_full, t)
                            need(act, M0.y_full, t - 2)
                            for f in range(2):
                                last = nc.scalar.activation(hT[1 - q][:, f, :], s_bank[1 - q][:, 2 * f * P:2 * (f + 1) * P],
                                                            ACT.Gelu, bias=b1s[u][:, f:f + 1])
                            last.then_inc(M0.h_done, 1)
                    over_tiles0(act, body)
                if stage >= 2:
                    act.wait_ge(qpad_zero, 2)
                    attention(L1, fill1, 1)
                if stage >= 3:
                    route(M1, 1)
                    act.wait_ge(exp_in, 2)
                    nc.scalar.activation(v2[:, :], v1[:, :], ACT.Exp, scale=-1.0).then_inc(exp_out, 1)

                    def body(i, u):
                        t, q = R1 * i + u, u % 2
                        if within(t, NT1):
                            act.wait_ge(M1.xt_full, t + 1)
                            need(act, M1.h_full, t - 1)
                            nc.scalar.copy(xsT[q][:, 0, :], pj_bank[q][:, 0:P]).then_inc(M1.xt_evac, 1)
                        if within(t - 1, NT1):
                            act.wait_ge(M1.h_full, t)
                            need(act, M1.h_done, t - 2)
                            nc.scalar.activation(sg[1 - q][:, :, :], s_bank[1 - q][:, 0:2 * P], ACT.Silu)\
                                .then_inc(M1.h_act, 1)
                        if within(t - 2, NT1):
                            act.wait_ge(M1.ht_full, t - 1)
                            need(act, M1.y_full, t - 4 + 1)
                            nc.scalar.copy(hT[q][:, :, 0:P], st_bank[q][:, 0:2 * P]).then_inc(M1.ht_evac, 1)
                    over_tiles1(act, body, 2)

            @block.vector
            def _(dve):
                dve.wait_ge(loaded, NLOAD)

                def stat(b):
                    nc.vector.bn_stats(stats[:, b, :], x[:, b, :]).then_inc(stat_done, 1)
                with dve.Fori(0, NB) as b:
                    stat(b)
                dve.wait_ge(rstd_done, 1)
                dve.wait_ge(masked, 1)
                nc.vector.tensor_tensor(rstd[:, :], rstd[:, :], mask[:, :], ALU.mult).then_inc(masked, 1)
                dve.wait_ge(masked, 2)

                def attention(L, fill, layer):
                    D = (D0, D1)[layer]

                    def normed(b, p):
                        nc.vector.tensor_scalar(xn[p][:, :], x[:, b, :], mean[:, bass.ds(b, 1)], rstd[:, bass.ds(b, 1)],
                                                ALU.subtract, ALU.mult).then_inc(L.xn_ready, 1)

                    def evacuated(i, off, name):
                        bk, k = fill(i, off, name)
                        dve.wait_ge(L.pj_free[bk], k + 1)

                    def low_values(i, off, name, ahead):
                        b, p = 2 * i + off + ahead, (off + ahead) % 2
                        if not inside(b):
                            return
                        bk, k = fill(i, off, name)
                        n = 2 if layer else 1
                        half, nh = int(name == "v1"), NH // n
                        va = (va0, va1)[layer][p]
                        dve.wait_ge(L.vh_done, n * b + half + 1)
                        need(dve, L.pv_full, NQ * (b - 1))
                        nc.vector.tensor_tensor(va[1][:, nh * half:nh * half + nh, 0:D],
                                                pj_bank[bk][:, 0:nh * D].rearrange("p (h d) -> p h d", d=D),
                                                va[0][:, nh * half:nh * half + nh, 0:D], ALU.subtract)\
                            .then_inc(L.pj_free[bk], 1)

                    def body(i, off):
                        b = 2 * i + off
                        p, pn = off % 2, (off + 1) % 2
                        for g in range(NQ):
                            Q = NQ * b + g
                            if layer == 0:
                                bq, gq = (b, 3) if g == 0 else (b + 1, g - 1)
                                pq = p if g == 0 else pn
                                if inside(bq):
                                    if gq == 0:
                                        evacuated(i, off - 1, "q")
                                    need(dve, L.st_full, NQ * (bq - 2) + gq + 1)
                                    hs = slice(QH * gq, QH * gq + QH)
                                    nc.vector.tensor_tensor(qpad[pq][:, hs, :],
                                                            qT[pq][:, :].unsqueeze(1).broadcast_to([P, QH, P]),
                                                            hmask[:, hs].unsqueeze(2).broadcast_to([P, QH, P]),
                                                            ALU.mult).then_inc(L.qpad_done, 1)
                            elif g < 2 and inside(b + 1):
                                need(dve, L.s_full, NQ * b)
                                hs, cs = slice(8 * g, 8 * g + 8), slice(4 * g, 4 * g + 4)
                                evacuated(i, off, f"q{g}")
                                nc.vector.tensor_copy(qpadb[pn][:, hs, :], qpad[pn][:, hs, :]).then_inc(L.cast_done, 1)
                                evacuated(i, off, f"k{g}")
                                nc.vector.tensor_copy(kTb[pn][:, cs, :], kT[pn][:, cs, :]).then_inc(L.cast_done, 1)
                            if layer == 0 and g == 2 and inside(b - 1):
                                dve.wait_ge(L.pv_free, NQ * b)
                                need(dve, L.o_done, b - 1)
                                nc.vector.reciprocal(rden0[:, :], oraw[:, :, D]).then_inc(L.rden_done, 1)
                            if layer == 0 and g == 3 and inside(b - 1):
                                dve.wait_ge(L.o_done, b)
                                nc.vector.tensor_tensor(x[:, b - 1, :], x[:, b - 1, :],
                                                        o0[:, :, :].rearrange("p h d -> p (h d)"), ALU.add)\
                                    .then_inc(L.x_done, 1)
                            if layer == 0 and g == 0 and inside(b - 2):
                                dve.wait_ge(L.x_done, b - 1)
                                stat(b - 2)
                            if g == 1 + layer and inside(b + 2):
                                if inside(b):
                                    bx, kx = fill(i, off - 2, "xT")
                                    need(dve, L.pj_full[bx], kx + 1)
                                normed(b + 2, p)
                            if layer == 0 and g == 2:
                                low_values(i, off, "v", 1)
                            for name, ahead in FILLS[layer][g]:
                                if layer == 1 and name[0] == "v":
                                    low_values(i, off, name, ahead)
                            if layer == 1 and inside(b):
                                dve.wait_ge(L.exp_done, Q + 1)
                                need(dve, L.pv_full, Q - 3)
                                nc.vector.tensor_copy(ph[g][:, :, :], pT[g % 2][:, :, :]).then_inc(L.ph_done, 1)
                            if layer == 0 and g == 2 and inside(b - 1):
                                dve.wait_ge(L.rden_done, b)
                                need(dve, L.x_done, b - 1)
                                nc.vector.tensor_tensor(o0[:, :, :], oraw[:, :, 0:D],
                                                        rden0[:, :].unsqueeze(2).broadcast_to([P, NH, D]), ALU.mult)\
                                    .then_inc(L.o_done, 1)
                            if inside(b + (g + 2) // NQ):
                                dve.wait_ge(L.s_full, Q + 3)
                                need(dve, L.c_full, Q + 1)
                                nc.vector.reduce_max(cm[g % 2][:, :], s_bank[g % 2][:, :].rearrange("p (h k) -> p h k", h=QH),
                                                     AX.X).then_inc(L.max_done, 1)
                            if layer == 1 and g == 0 and inside(b - 2):
                                dve.wait_ge(L.y_full, b - 1)
                                nc.vector.tensor_tensor(ysum[:, :], o_bank[:, 0:DM], bo1[:, :], ALU.add)\
                                    .then_inc(L.y_free, 1)
                                dve.wait_ge(L.y_free, b - 1)
                                nc.vector.tensor_tensor(x[:, b - 2, :], x[:, b - 2, :], ysum[:, :], ALU.add)\
                                    .then_inc(L.x_done, 1)
                                dve.wait_ge(L.x_done, b - 1)
                                stat(b - 2)
                            bo, go = b + (g - 2) // NQ, (g - 2) % NQ
                            po = p if g > 1 else pn
                            if layer == 0 and inside(bo):
                                dve.wait_ge(L.pv_full, Q - 1)
                                if go == 0:
                                    need(dve, L.o_done, bo)
                                nc.vector.tensor_copy(oraw[:, QH * go:QH * (go + 1), :], o_bank[:, 0:QH * (D + 1)])\
                                    .then_inc(L.pv_free, 1)
                            elif inside(bo):
                                dve.wait_ge(L.pv_full, Q - 1)
                                ov = o_bank[:, 0:QH * (D + 1)].rearrange("p (h d) -> p h d", d=D + 1)
                                nc.vector.reciprocal(rden[:, :], ov[:, :, D]).then_inc(L.rden_done, 1)
                                dve.wait_ge(L.rden_done, Q - 1)
                                nc.vector.tensor_tensor(o1[po][:, QH * go:QH * (go + 1), :], ov[:, :, 0:D],
                                                        rden[:, :].unsqueeze(2).broadcast_to([P, QH, D]), ALU.mult)\
                                    .then_inc(L.pv_free, 1)
                    over_batches(dve, body)
                attention(L0, fill0, 0)

                chain = [0]

                def link(ins):
                    chain[0] += 1
                    ins.then_inc(rt, 1)
                    dve.wait_ge(rt, chain[0])

                def route(M, n, base):
                    dve.wait_ge(rstd_done, base)

                    def body(i, u):
                        b = 2 * i + u
                        if within(b, NB):
                            need(dve, M.t_full, b - 1)
                            need(dve, M.xr_copied, b - 1)
                            nc.vector.tensor_scalar(xn[u][:, :], x[:, b, :], mean[:, bass.ds(b, 1)],
                                                    rstd[:, bass.ds(b, 1)], ALU.subtract, ALU.mult)\
                                .then_inc(M.xr_ready, 1)
                            if n == 1:
                                nc.vector.tensor_scalar(xna[:, b, :], x[:, b, :], mean[:, bass.ds(b, 1)],
                                                        rstd[:, bass.ds(b, 1)], ALU.subtract, ALU.mult)\
                                    .then_inc(M.xr_copied, 1)
                        if n == 1 and within(b - 1, NB):
                            dve.wait_ge(M.sg_done, b)
                            need(dve, M.sy_full, b - 2)
                            nc.vector.tensor_tensor(hT[1 - u][:, :, 0:P], sg[1 - u][:, :, :],
                                                    s_bank[1 - u][:, 2 * P:4 * P].rearrange("p (c n) -> p c n", c=2),
                                                    ALU.mult).then_inc(M.sh_done, 1)
                        if n == 1 and within(b - 2, NB):
                            dve.wait_ge(M.sy_full, b - 1)
                            nc.vector.tensor_tensor(x[:, b - 2, :], x[:, b - 2, :], st_bank[u][:, 0:DM], ALU.add)\
                                .then_inc(M.sy_done, 1)
                    over_pairs(dve, body)

                def top(E, src, oh, best):
                    tt = nc.vector.tensor_tensor
                    by_token = "p e b -> p b e"
                    link(nc.vector.reduce_max(best[:, :], src[:, 0:E, :].rearrange(by_token), AX.X))
                    link(tt(wk[:, 0:E, :], src[:, 0:E, :], best[:, :].unsqueeze(1).broadcast_to([P, E, NB]), ALU.is_equal))
                    link(tt(wk[:, 0:E, :], wk[:, 0:E, :], rev[:, 0:E].unsqueeze(2).broadcast_to([P, E, NB]), ALU.mult))
                    link(nc.vector.reduce_max(v3[:, :], wk[:, 0:E, :].rearrange(by_token), AX.X))
                    link(tt(oh[:, 0:E, :], rev[:, 0:E].unsqueeze(2).broadcast_to([P, E, NB]),
                            v3[:, :].unsqueeze(1).broadcast_to([P, E, NB]), ALU.is_equal))

                def rank(n, E):
                    tt = nc.vector.tensor_tensor
                    dve.wait_ge(rank_ready, n + 1)
                    fl = "p e b -> p (e b)"
                    cols = E * NB
                    link(nc.vector.tensor_tensor_scan(wk[:, 0:E, :].rearrange(fl), reset[:, 0:E, :].rearrange(fl),
                                                      s_bank[1][:, 0:cols], 0.0, ALU.mult, ALU.add))
                    link(tt(rk[:, 0:E, :].rearrange(fl), wk[:, 0:E, :].rearrange(fl), s_bank[1][:, 0:cols], ALU.subtract))
                    link(tt(rk[:, 0:E, :].rearrange(fl), rk[:, 0:E, :].rearrange(fl), s_bank[0][:, 0:cols], ALU.add))

                def to_slot(E, oh, k, add):
                    link(nc.vector.tensor_tensor(wk[:, 0:E, :], oh[:, 0:E, :], rk[:, 0:E, :], ALU.mult))
                    link(nc.vector.reduce_sum(v4[:, :], wk[:, 0:E, :].rearrange("p e b -> p b e"), AX.X))
                    nc.vector.tensor_scalar(slot[k][:, :], v4[:, :], float(add), None, ALU.add).then_inc(slots_ready, 1)

                def add_gathered(n0, ks, weights, stats_too):
                    n = n0
                    for b in range(NB):
                        for k in ks:
                            dve.wait_ge(g_in[n % RING], 16 * (n // RING + 1))
                            g = gb[n % RING]
                            if weights:
                                nc.vector.scalar_tensor_tensor(x[:, b, :], g[:, :], wt[k][:, b:b + 1], x[:, b, :],
                                                               ALU.mult, ALU.add).then_inc(g_used, 1)
                            else:
                                nc.vector.tensor_tensor(x[:, b, :], x[:, b, :], g[:, :], ALU.add).then_inc(g_used, 1)
                            n += 1
                            dve.wait_ge(g_used, n)
                        if stats_too:
                            stat(b)

                tt, ts = nc.vector.tensor_tensor, nc.vector.tensor_scalar
                if stage >= 1:
                    route(M0, 0, 2)
                    dve.wait_ge(M0.lg_done, NB)
                    E = E0
                    r = slice(0, E)
                    link(tt(lg[:, r, :], o_bank[:, 0:E * NB].rearrange("p (b e) -> p e b", e=E),
                            rb0[:, :].unsqueeze(2).broadcast_to([P, E, NB]), ALU.add))
                    link(nc.vector.reduce_max(v1[:, :], lg[:, r, :].rearrange("p e b -> p b e"), AX.X))
                    tt(wk[:, r, :], lg[:, r, :], v1[:, :].unsqueeze(1).broadcast_to([P, E, NB]), ALU.subtract)\
                        .then_inc(exp_in, 1)
                    dve.wait_ge(exp_out, 1)
                    link(nc.vector.reduce_sum(v2[:, :], pr[:, r, :].rearrange("p e b -> p b e"), AX.X))
                    link(nc.vector.reciprocal(v3[:, :], v2[:, :]))
                    link(tt(pr[:, r, :], pr[:, r, :], v3[:, :].unsqueeze(1).broadcast_to([P, E, NB]), ALU.mult))
                    top(E, pr, oh1, v1)
                    link(nc.vector.scalar_tensor_tensor(pr[:, r, :], oh1[:, r, :], -2.0, pr[:, r, :], ALU.mult, ALU.add))
                    top(E, pr, oh2, v2)
                    tt(selb[:, r, :], oh1[:, r, :], oh2[:, r, :], ALU.add).then_inc(sel_ready, 1)
                    link(tt(v3[:, :], v1[:, :], v2[:, :], ALU.add))
                    link(ts(v4[:, :], v3[:, :], 1e-9, None, ALU.max))
                    link(nc.vector.reciprocal(v3[:, :], v4[:, :]))
                    link(tt(wt[0][:, :], v1[:, :], v3[:, :], ALU.mult))
                    link(tt(wt[1][:, :], v2[:, :], v3[:, :], ALU.mult))
                    rank(0, E)
                    link(ts(wk[:, r, :], rk[:, r, :], float(CAP), None, ALU.is_lt))
                    link(tt(rk[:, r, :], rk[:, r, :], base0[:, :].unsqueeze(2).broadcast_to([P, E, NB]), ALU.add))
                    link(tt(rk[:, r, :], rk[:, r, :], wk[:, r, :], ALU.mult))
                    to_slot(E, oh1, 0, ZROW)
                    to_slot(E, oh2, 1, ZROW)

                    def body(i, j):
                        q, t = j % 2, 2 * PER * i + j
                        if within(t - 2, NT0):
                            u = (j - 2) % (2 * PER) // PER
                            dve.wait_ge(M0.y_full, t - 1)
                            r = (j - 2) % R0
                            if within(t - 2 - R0, NT0):
                                dve.wait_ge(M0.y_out[r], 16 * (2 * PER // R0 * i + (j - 2) // R0))
                            nc.vector.tensor_tensor(ysb[r][:, :, :], st_bank[q][:, 0:2 * DM].rearrange("p (h d) -> p h d", h=2),
                                                    b2s[u][:, :].unsqueeze(1).broadcast_to([P, 2, DM]), ALU.add)\
                                .then_inc(M0.y_evac, 1)
                    over_tiles0(dve, body)
                    add_gathered(0, (0, 1), True, stage >= 2)
                if stage >= 2:
                    dve.wait_ge(rstd_done, 3)
                    attention(L1, fill1, 1)
                if stage >= 3:
                    route(M1, 1, 4)
                    E = E1
                    link(tt(lg[:, :, :], o_bank[:, 0:E * NB].rearrange("p (b e) -> p e b", e=E),
                            reset[:, :, 1:2].broadcast_to([P, E, NB]), ALU.mult))
                    top(E, lg, oh1, v1)
                    link(ts(selb[:, :, :], oh1[:, :, :], 1.0, None, ALU.mult))
                    nc.vector.sem_inc(sel_ready, 1)
                    nc.vector.sem_inc(exp_in, 1)
                    dve.wait_ge(exp_out, 2)
                    link(ts(v3[:, :], v2[:, :], 1.0, None, ALU.add))
                    link(nc.vector.reciprocal(v4[:, :], v3[:, :]))
                    link(tt(xna[:, :, :], xna[:, :, :], v4[:, :].unsqueeze(2).broadcast_to([P, NB, DM]), ALU.mult))
                    rank(1, E)
                    link(tt(oh2[:, :, :], wk[:, :, NB - 1:NB].broadcast_to([P, E, NB]),
                            k128[:, :].unsqueeze(1).broadcast_to([P, E, NB]), ALU.is_gt))
                    link(nc.vector.reduce_sum(ntile[:, :], oh2[:, :, :], AX.X))
                    link(nc.vector.tensor_tensor_scan(tcum[:, :], reset[:, :, 1:2].rearrange("p e b -> p (e b)"),
                                                      ntile[:, :], 0.0, ALU.mult, ALU.add))
                    link(tt(base1[:, :], tcum[:, :], ntile[:, :], ALU.subtract))
                    link(ts(base1[:, :], base1[:, :], float(P), None, ALU.mult))
                    link(tt(rk[:, :, :], rk[:, :, :], base1[:, :].unsqueeze(2).broadcast_to([P, E, NB]), ALU.add))
                    tw = tile_past
                    link(tt(tw, tiota[:, :].unsqueeze(2).broadcast_to([1, NT1, E]),
                            tcum[0:1, :].unsqueeze(1).broadcast_to([1, NT1, E]), ALU.is_ge))
                    link(nc.vector.reduce_sum(tef[:, :], tw, AX.X))
                    link(ts(tei[:, :], tef[:, :], float(E - 1), None, ALU.min))
                    to_slot(E, oh1, 2, 0)

                    def body(i, u):
                        t, q = R1 * i + u, u % 2
                        if within(t - 1, NT1):
                            dve.wait_ge(M1.h_act, t)
                            need(dve, M1.ht_full, t - 3 + 1)
                            nc.vector.tensor_tensor(hid[1 - q][:, :], sg[1 - q][:, :, :].rearrange("p c n -> p (c n)"),
                                                    s_bank[1 - q][:, 2 * P:4 * P], ALU.mult).then_inc(M1.h_done, 1)
                        if within(t - 3, NT1):
                            dve.wait_ge(M1.y_full, t - 2)
                            r = (u - 3) % R1
                            if within(t - 3 - R1, NT1):
                                dve.wait_ge(M1.y_out[r], 16 * (i + (u - 3) // R1))
                            nc.vector.tensor_copy(ysb[r][:, 0, :], o_bank[:, 0:DM]).then_inc(M1.y_evac, 1)
                    over_tiles1(dve, body, 3)
                    add_gathered(2 * NB, (2,), False, False)


def kernel(x, ctx_768, mask_BxS_bk0, L0_xattn_Wq, L0_xattn_Wkv, L0_ffn_router_w, L0_ffn_router_b, L0_ffn_w1,
           L0_ffn_b1, L0_ffn_w2, L0_ffn_b2, L1_xattn_w_q, L1_xattn_w_k, L1_xattn_w_v, L1_xattn_w_out,
           L1_xattn_b_out, L1_ffn_w_router, L1_ffn_gate_up_proj, L1_ffn_down_proj, L1_ffn_w_gate, L1_ffn_w_up,
           L1_ffn_w_down):
    import concourse.bacc as bacc
    from concourse.bass_utils import run_bass_kernel_spmd as run

    def lay(v):
        return np.ascontiguousarray(v)

    x = np.asarray(x)
    head = np.zeros((QH, QH, P), np.float32)
    for j in range(QH):
        head[j, j] = -1.0
    hm = np.zeros((P, NH), np.float32)
    for h in range(NH):
        hm[D0 * h:D0 * (h + 1), h] = 1.0
    arrays = {
        "x": lay(x.transpose(1, 0, 2)),
        "ctxT": lay(np.asarray(ctx_768).transpose(2, 0, 1).reshape(DC, NB * P)),
        "mask": lay(np.asarray(mask_BxS_bk0).T),
        "wq0": lay(np.asarray(L0_xattn_Wq).T),
        "wk0": lay(np.asarray(L0_xattn_Wkv)[:DM].T),
        "wv0": lay(np.asarray(L0_xattn_Wkv)[DM:].T),
        "wq1": lay(np.asarray(L1_xattn_w_q)),
        "wk1": lay(np.asarray(L1_xattn_w_k)),
        "wv1": lay(np.asarray(L1_xattn_w_v)),
        "wo1": lay(np.asarray(L1_xattn_w_out).reshape(NCH, P, DM).transpose(1, 0, 2)),
        "bo1": lay(np.broadcast_to(np.asarray(L1_xattn_b_out), (P, DM))),
        "ident": np.eye(P, dtype=np.float32),
        "sel": head,
        "hmask": hm,
        "mhalf": np.full((P, NB), -0.5, np.float32),
        "tri": np.triu(np.ones((P, P), np.float32), 1),
        "rw0": lay(np.asarray(L0_ffn_router_w)),
        "rw1": lay(np.asarray(L1_ffn_w_router).T),
        "rb0": lay(np.broadcast_to(np.asarray(L0_ffn_router_b), (P, E0))),
        "rev": lay(np.broadcast_to(E1 - np.arange(E1, dtype=np.float32), (P, E1))),
        "base0": lay(np.broadcast_to(CAP * np.arange(E0, dtype=np.float32) - ZROW, (P, E0))),
        "k128": lay(np.broadcast_to(P * np.arange(NB, dtype=np.float32), (P, NB))),
        "tiota": np.arange(NT1, dtype=np.float32)[None],
        "reset": lay(np.broadcast_to((np.arange(NB) > 0).astype(np.float32), (P, E1, NB))),
        "gu": lay(np.asarray(L1_ffn_gate_up_proj).transpose(1, 0, 2)),
        "dn": lay(np.asarray(L1_ffn_down_proj).reshape(E1, 2, P, DM).transpose(2, 0, 1, 3)),
        "wgu": lay(np.concatenate([np.asarray(L1_ffn_w_gate).T, np.asarray(L1_ffn_w_up).T], 1)),
        "wdn": lay(np.asarray(L1_ffn_w_down).T.reshape(2, P, DM).transpose(1, 0, 2)),
        "zero": np.zeros((P, ZR * DM), np.float32),
        "w1": lay(np.asarray(L0_ffn_w1)),
        "w2": lay(np.asarray(L0_ffn_w2).reshape(E0, 2, P, DM).transpose(0, 2, 1, 3)),
        "b1": lay(np.asarray(L0_ffn_b1).reshape(E0, 2, P).transpose(0, 2, 1)),
        "b2": lay(np.broadcast_to(np.asarray(L0_ffn_b2)[:, None], (E0, P, DM))),
    }
    nc = bacc.Bacc("TRN2", target_bir_lowering=False, num_devices=1)
    a = {n: nc.dram_tensor(f"in_{n}", v.shape, mybir.dt.from_np(v.dtype), kind="ExternalInput").ap()
         for n, v in arrays.items()}
    out = nc.dram_tensor("out", (P, NB, DM), F32, kind="ExternalOutput").ap()
    build(nc, a, out)
    r = run(nc, [{f"in_{n}": v for n, v in arrays.items()}], core_ids=[0])
    return r.results[0]["out"].transpose(1, 0, 2)
```

```python
import numpy as np
import concourse.bass as bass
from concourse import mybir
from contextlib import ExitStack

F32 = mybir.dt.float32
BF16 = mybir.dt.bfloat16
I32 = mybir.dt.int32
U8 = mybir.dt.uint8
ALU = mybir.AluOpType
ACT = mybir.ActivationFunctionType
AX = mybir.AxisListType

NB = 32
P = 128
DM = 128
DC = 96
NH = 16
QH = 4
NQ = NH // QH
D0, D1 = 8, 64
NCH = NH * D1 // P
E0, F0, CAP = 8, 256, 1280
E1, F1 = 16, 256
EPS = 1e-5
LAST = NB - 1


def need(eng, sem, value):
    if isinstance(value, int) and value <= 0:
        return
    eng.wait_ge(sem, value)


def over_batches(eng, body):
    for b in range(-3, 5):
        body((b + 1) // 2, b - 2 * ((b + 1) // 2))
    with eng.Fori(2, NB // 2 - 3) as i:
        body(i, 1)
        body(i, 2)
    for b in range(NB - 5, NB + 4):
        body((b - 1) // 2, 2 - b % 2)


def inside(b):
    return not isinstance(b, int) or 0 <= b <= LAST


NORM_LG = (-3, -4)

FILLS = (
    ((("k", 1),), (("rT", -3), ("v", 1)), (("xT", 2),), (("q", 2), ("lg", -3))),
    ((("q0", 1), ("k0", 1), ("y", -2)), (("q1", 1), ("k1", 1), ("rT", -4)), (("lg", -4), ("v0", 1), ("oT0", -1)),
     (("v1", 1), ("oT1", -1), ("xT", 2))),
)
FRONT = ((0, 0, 0, 0), (1, 2, 2, 2))


def number_fills(layer):
    numbers = {}
    for b in range(-3, NB + 4):
        for step in FILLS[layer]:
            for name, ahead in step:
                if 0 <= b + ahead <= LAST:
                    numbers[b, name] = len(numbers)
    return numbers


NUMBERS = (number_fills(0), number_fills(1))

NORM_AT = ({"stats": (0, -2), "aggr": (1, -2), "eps": (2, -2), "root": (3, -2), "normed": (0, -3)},
           {"stats": (2, -2), "aggr": (3, -2), "eps": (0, -3), "root": (1, -3), "normed": (2, -3)})


def fill_of(layer, i, off, name):
    if isinstance(i, int):
        f = NUMBERS[layer][2 * i + off, name]
        return f % 2, f // 2
    per = sum(len(step) for step in FILLS[layer])
    f = NUMBERS[layer][4 + off, name]
    return f % 2, f // 2 + per * (i - 2)


def fill0(i, off, name):
    return fill_of(0, i, off, name)


def fill1(i, off, name):
    return fill_of(1, i, off, name)


NT0, PER = E0 * CAP // (2 * P), CAP // (2 * P)
NT1 = NB + E1
ZROW = E0 * CAP
RING = 8
XPARTS = 4
XB = NB // XPARTS
OPARTS = 8
OB = NB // OPARTS
EPARTS = 4
ZR = 4
R0, R1 = 5, 4
LAG0, LAG1 = R0 + 3, R1 + 3


def over_pairs(eng, body, drain=2):
    for i in range(2):
        body(i, 0)
        body(i, 1)
    with eng.Fori(2, NB // 2) as i:
        body(i, 0)
        body(i, 1)
    for u in range(drain):
        body(NB // 2 + u // 2, u % 2)


def over_tiles0(eng, body, drain=2):
    for j in range(2 * PER):
        body(0, j)
    with eng.Fori(1, E0 // 2) as i:
        for j in range(2 * PER):
            body(i, j)
    for j in range(drain):
        body(E0 // 2, j)


def over_tiles1(eng, body, drain=2):
    for i in range(2):
        for u in range(R1):
            body(i, u)
    with eng.Fori(2, NT1 // R1) as i:
        for u in range(R1):
            body(i, u)
    for u in range(drain):
        body(NT1 // R1 + u // R1, u % R1)


def within(t, n):
    return not isinstance(t, int) or 0 <= t < n


def build(nc, a, out):
    ctx = ExitStack()
    with ctx:
        def sb(name, shape, dt=F32):
            return ctx.enter_context(nc.sbuf_tensor(name, shape, dt))

        def sem(name):
            return ctx.enter_context(nc.semaphore(name))

        x = sb("x", [P, NB, DM])
        ident = sb("ident", [P, P])
        identb = sb("identb", [P, P], BF16)
        sel = sb("sel", [QH, QH, P], BF16)
        hmask = sb("hmask", [P, NH])
        mask8 = sb("mask8", [P, NB], U8)
        mask = sb("mask", [P, NB])
        mhalf = sb("mhalf", [P, NB])
        stats = sb("stats", [P, NB, 6])
        mean = sb("mean", [P, NB])
        ln = [sb(f"ln{n}", [P, NB]) for n in range(4)]
        rstd = sb("rstd", [P, NB])
        st = [sb(f"st{p}", [P, 6]) for p in range(2)]
        mv = [sb(f"mv{p}", [P, 2]) for p in range(2)]
        ve = [sb(f"ve{p}", [P, 1]) for p in range(2)]
        rs = [sb(f"rs{p}", [P, 1]) for p in range(2)]
        stF = [sb(f"stF{p}", [P, 6]) for p in range(2)]
        mvF = [sb(f"mvF{p}", [P, 2]) for p in range(2)]
        veF = [sb(f"veF{p}", [P, 1]) for p in range(2)]
        rsF = [sb(f"rsF{p}", [P, 1]) for p in range(2)]
        xnF = [sb(f"xnF{p}", [P, DM]) for p in range(2)]
        xrT = [sb(f"xrT{p}", [DM, P]) for p in range(2)]
        gidx = [[sb(f"gidx{p}{k}", [P, 1], I32) for k in range(2)] for p in range(2)]
        wq0 = sb("wq0", [DM, DM])
        wk0 = sb("wk0", [DC, DM])
        wv0 = sb("wv0", [DC, DM])
        wq1 = sb("wq1", [DM, NH * D1])
        wk1 = sb("wk1", [DC, NH * D1])
        wv1 = sb("wv1", [DC, NH * D1])
        wo1 = sb("wo1", [P, NCH, DM])
        bo1 = sb("bo1", [P, DM])
        xn = [sb(f"xn{p}", [P, DM]) for p in range(2)]
        xnT = [sb(f"xnT{p}", [DM, P]) for p in range(2)]
        ctxT = [sb(f"ctxT{p}", [DC, P]) for p in range(2)]
        qpads = sb("qpads", [P, 2 * NH, P])
        qpad = [qpads[:, p * NH:(p + 1) * NH, :] for p in range(2)]
        kTs = sb("kTs", [P, 2 * NCH, P])
        kT = [kTs[:, p * NCH:(p + 1) * NCH, :] for p in range(2)]
        qT = [sb(f"qT{p}", [P, P]) for p in range(2)]
        qpadb = [sb(f"qpadb{p}", [P, NH, P], BF16) for p in range(2)]
        kTb = [sb(f"kTb{p}", [P, NCH, P], BF16) for p in range(2)]
        vv0 = [sb(f"vv0{p}", [P, NH, 2, D0 + 1], BF16) for p in range(2)]
        va0 = [[vv0[p][:, :, part, :] for part in range(2)] for p in range(2)]
        va1 = [[sb(f"va1{p}{n}", [P, NH, D1 + 1], BF16) for n in "hl"] for p in range(2)]
        cm = [sb(f"cm{p}", [P, QH], BF16) for p in range(2)]
        cT = [sb(f"cT{p}", [QH, P], BF16) for p in range(2)]
        pT = [sb(f"pT{p}", [P, QH, P]) for p in range(2)]
        ph = [sb(f"ph{g}", [P, QH, P], BF16) for g in range(NQ)]
        pl = [sb(f"pl{g}", [P, QH, P], BF16) for g in range(NQ)]
        rden = sb("rden", [P, QH])
        oraw = sb("oraw", [P, NH, 2, D0 + 1])
        osum = sb("osum", [P, NH, D0])
        rden0 = sb("rden0", [P, NH])
        o0 = sb("o0", [P, NH, D0])
        o1s = sb("o1s", [P, 2 * NH, D1])
        o1 = [o1s[:, p * NH:(p + 1) * NH, :] for p in range(2)]
        oT = sb("oT", [P, NCH, P])
        ysum = sb("ysum", [P, DM])

        xna = qpads
        tri = sb("tri", [P, P], BF16)
        ones = sb("ones", [P, P], BF16)
        rw = [sb("rw0", [DM, E0]), sb("rw1", [DM, E1])]
        rb0 = sb("rb0", [P, E0])
        rev = sb("rev", [P, E1])
        base0 = sb("base0", [P, E0])
        k128 = sb("k128", [P, NB])
        tiota = sb("tiota", [1, NT1])
        reset = sb("reset", [P, E1, NB])
        RT = [P, E1, NB]
        lg, pr, wk, oh1, oh2, rk = [sb(n, RT) for n in ("lg", "pr", "wk", "oh1", "oh2", "rk")]
        selb = sb("selb", RT, BF16)
        triw = wk[:, 0:P // NB, :].rearrange("p e b -> p (e b)")
        selw = rk[0:QH, :, :].rearrange("p e b -> p (e b)").rearrange("p (h n) -> p h n", h=QH)
        srstd = sb("srstd", [P, NB])
        v1, v2, v3, v4 = [sb(n, [P, NB]) for n in ("v1", "v2", "v3", "v4")]
        wt = [sb(f"wt{k}", [P, NB]) for k in range(2)]
        slot = [sb(f"slot{k}", [P, NB], I32) for k in range(3)]
        ntile, tcum, base1 = [sb(n, [P, E1]) for n in ("ntile", "tcum", "base1")]
        tile_past = qpadb[0][0:1, :, :].rearrange("p h n -> p (h n)").bitcast(F32)[:, 0:NT1 * E1]\
            .rearrange("p (t e) -> p t e", e=E1)
        tef = sb("tef", [1, NT1])
        tei = sb("tei", [1, NT1], I32)
        zero = sb("zero", [P, ZR * DM])
        w1s = [sb(f"w1s{p}", [DM, F0]) for p in range(2)]
        w2s = [sb(f"w2s{p}", [P, 2, DM]) for p in range(2)]
        b1s = [sb(f"b1s{p}", [P, 2]) for p in range(2)]
        b2s = [sb(f"b2s{p}", [P, DM]) for p in range(2)]
        xs = [qpads[:, 2 * r:2 * r + 2, :] for r in range(R0)]
        xsT = [sb(f"xsT{p}", [DM, 2, P]) for p in range(2)]
        hT = [sb(f"hT{p}", [P, 2, 2 * P]) for p in range(2)]
        sg = [sb(f"sg{p}", [P, 2, P]) for p in range(2)]
        ysb = [qpads[:, 2 * (R0 + r):2 * (R0 + r) + 2, :] for r in range(R0)]
        gb = [sb(f"gb{r}", [P, DM]) for r in range(RING)]
        gu = sb("gu", [DM, E1, 2 * F1])
        xna0 = gu[:, 0:NB * DM // (2 * F1), :].rearrange("p e f -> p (e f)").rearrange("p (b d) -> p b d", b=NB)
        dn = sb("dn", [P, E1, 2, DM])
        hid = [sb(f"hid{p}", [P, F1]) for p in range(2)]
        wgu = sb("wgu", [DM, 2 * F1])
        wdn = sb("wdn", [P, 2, DM])

        buf0 = nc.dram_tensor("buf0", (ZROW, DM), F32, kind="Internal").ap()
        eo0 = nc.dram_tensor("eo0", (ZROW + P, DM), F32, kind="Internal").ap()
        buf1 = nc.dram_tensor("buf1", (NT1 * P, DM), F32, kind="Internal").ap()
        eo1 = nc.dram_tensor("eo1", (NT1 * P, DM), F32, kind="Internal").ap()

        bank = [ctx.enter_context(nc.psum_tensor(f"bank{n}", [P, 512], F32)) for n in range(7)]
        cbank = ctx.enter_context(nc.psum_tensor("cbank", [P, 1024], BF16))
        s_bank, st_bank, pj_bank, o_bank = bank[0:2], bank[2:4], bank[4:6], bank[6]

        x_in = [sem(f"x_in{n}") for n in range(XPARTS)]
        loaded, later_loaded, experts_loaded = sem("loaded"), sem("later_loaded"), sem("experts_loaded")
        masked = sem("masked")
        stat_done = sem("stat_done")
        ln_step = sem("ln_step")
        rstd_done = sem("rstd_done")
        const_done = sem("const_done")
        stored = sem("stored")
        zeroed = [sem(f"zeroed{n}") for n in range(2)]
        zero_loaded = sem("zero_loaded")
        rt = sem("rt")
        exp_in, exp_out = sem("exp_in"), sem("exp_out")
        sel_ready, rank_ready = sem("sel_ready"), sem("rank_ready")
        slots_ready = sem("slots_ready")
        qpad_zero = sem("qpad_zero")
        g_in = [sem(f"g_in{r}") for r in range(RING)]
        g_used = sem("g_used")
        e_in = [[sem(f"e_in{p}{k}") for k in range(2)] for p in range(2)]
        e_used, idx_done = sem("e_used"), sem("idx_done")
        st_done, mv_done, ve_done, rs_done = sem("st_done"), sem("mv_done"), sem("ve_done"), sem("rs_done")

        class Moe:
            def __init__(self, n):
                self.scattered = sem(f"scattered_{n}")
                self.xs_in = [sem(f"xs_in{n}{p}") for p in range((R0, R1)[n])]
                self.xt_full = sem(f"xt_full_{n}")
                self.xt_evac = sem(f"xt_evac_{n}")
                self.h_full = sem(f"h_full_{n}")
                self.h_done = sem(f"h_done_{n}")
                self.y_full = sem(f"y_full_{n}")
                self.y_evac = sem(f"y_evac_{n}")
                self.y_out = [sem(f"y_out{n}{p}") for p in range((R0, R1)[n])]
                if n == 0:
                    self.w_in = [sem(f"w_in{p}") for p in range(2)]
                    return
                self.h_act = sem("h_act")
                self.ht_full = sem("ht_full")
                self.ht_evac = sem("ht_evac")
                self.xr_ready = sem("xr_ready")
                self.xr_copied = sem("xr_copied")
                self.t_full = sem("t_full")
                self.t_evac = sem("t_evac")
                self.g_full = sem("g_full")
                self.sg_done = sem("sg_done")
                self.sh_done = sem("sh_done")
                self.sy_full = sem("sy_full")
                self.sy_done = sem("sy_done")
        M0, M1 = Moe(0), Moe(1)

        class Layer:
            def __init__(self, n):
                self.ctx_in = [sem(f"ctx_in{n}{p}") for p in range(2)]
                self.xn_ready = sem(f"xn_ready{n}")
                self.pj_full = [sem(f"pj_full{n}{p}") for p in range(2)]
                self.pj_free = [sem(f"pj_free{n}{p}") for p in range(2)]
                self.s_full = sem(f"s_full{n}")
                self.max_done = sem(f"max_done{n}")
                self.qpad_done = sem(f"qpad_done{n}")
                self.cast_done = sem(f"cast_done{n}")
                self.vh_done = sem(f"vh_done{n}")
                self.ph_done = sem(f"ph_done{n}")
                self.pl_done = sem(f"pl_done{n}")
                self.c_full = sem(f"c_full{n}")
                self.c_free = sem(f"c_free{n}")
                self.st_full = sem(f"st_full{n}")
                self.exp_done = sem(f"exp_done{n}")
                self.pv_full = sem(f"pv_full{n}")
                self.rden_done = sem(f"rden_done{n}")
                self.o_done = sem(f"o_done{n}")
                self.pv_free = sem(f"pv_free{n}")
                self.x_done = sem(f"x_done{n}")
                self.part_done = {part: sem(f"{part}_done{n}") for part in ("stats", "aggr", "eps", "root", "normed")}
                self.kept = sem(f"kept{n}")
        L0, L1 = Layer(0), Layer(1)

        NZERO = (-(-ZROW // (ZR * P)) + 1, -(-NT1 // ZR))

        with nc.Block() as block:
            NLOAD, NLATER, NEXPERTS = 16 * 10, 16 * 12, 16 * (2 * EPARTS + 2)

            @block.sync
            def _(sp):
                for n in range(XPARTS):
                    bs = slice(n * XB, (n + 1) * XB)
                    sp.dma_start(x[:, bs, :], a["x"][:, bs, :]).then_inc(x_in[n], 16)

                def load(pairs, done):
                    for dst, name in pairs:
                        sp.dma_start(dst[(slice(None),) * len(dst.shape)], a[name]).then_inc(done, 16)
                weights = ((wq1, "wq1"), (wk1, "wk1"), (wv1, "wv1"), (wo1, "wo1"))
                late = ((bo1, "bo1"), (rw[1], "rw1"), (rb0, "rb0"), (rev, "rev"), (base0, "base0"), (k128, "k128"),
                        (tiota, "tiota"), (reset, "reset"))
                zeros = [[(buf, r, min(ZR * P, rows - r) // P) for r in range(0, rows, ZR * P)]
                         for buf, rows in ((buf0, ZROW), (buf1, NT1 * P))]
                zeros[0].append((eo0, ZROW, 1))
                assert len(zeros[0]) == NZERO[0] and len(zeros[1]) == NZERO[1] and len(late) + 4 == NLATER // 16
                at_batches = ((1, 2, 3, 4, NB - 5, NB - 4, NB - 3), (-1, 0, 1, 2, 3, 4))

                def background(layer, b):
                    if layer == 0 and b == -1:
                        load(((zero, "zero"),), zero_loaded)
                    if layer == 0 and b == 0:
                        load(late, later_loaded)
                        sp.wait_ge(zero_loaded, 16)
                    if layer == 0 and 1 <= b <= len(weights):
                        load(weights[b - 1:b], later_loaded)
                    if layer == 1 and 0 <= b < EPARTS:
                        es = slice(b * E1 // EPARTS, (b + 1) * E1 // EPARTS)
                        sp.dma_start(gu[:, es, :], a["gu"][:, es, :]).then_inc(experts_loaded, 16)
                        sp.dma_start(dn[:, es, :, :], a["dn"][:, es, :, :]).then_inc(experts_loaded, 16)
                    if layer == 1 and b == EPARTS:
                        load(((wgu, "wgu"), (wdn, "wdn")), experts_loaded)
                    places = at_batches[layer]
                    if b in places:
                        for buf, r, m in zeros[layer][places.index(b)::len(places)]:
                            sp.dma_start(buf[r:r + m * P, :].rearrange("(p m) d -> p (m d)", p=P), zero[:, 0:m * DM])\
                                .then_inc(zeroed[layer], 16)

                def attention(L, fill, lastv):
                    def body(i, off):
                        b = 2 * i + off
                        if isinstance(b, int) and b < -1 or not inside(b + 1):
                            return
                        at = (b + 1) * P
                        if not isinstance(at, int):
                            at = sp.snap(at)
                        if inside(b - 1):
                            bk, k = fill(i, off - 2, lastv)
                            need(sp, L.pj_full[bk], k + 1)
                        sp.dma_start(ctxT[(off + 1) % 2][:, :], a["ctxT"][:, bass.ds(at, P)])\
                            .then_inc(L.ctx_in[(off + 1) % 2], 16)
                        if isinstance(b, int):
                            background(int(lastv == "v1"), b)
                    over_batches(sp, body)
                attention(L0, fill0, "v")
                sp.wait_ge(M0.scattered, 16 * 2 * NB)
                def body(i, j):
                    u, q, t = j // PER % 2, j % 2, 2 * PER * i + j
                    if j % PER == 0 and within(t, NT0):
                        need(sp, M0.y_evac, t - PER)
                        e = 2 * i + u
                        for dst, name in ((w1s, "w1"), (w2s, "w2"), (b1s, "b1"), (b2s, "b2")):
                            src = a[name][e] if isinstance(e, int) else a[name][bass.ds(e, 1)]
                            if not isinstance(e, int):
                                src = src.squeeze(0)
                            sp.dma_start(dst[u][:], src).then_inc(M0.w_in[u], 16)
                    r, rs = j % R0, (j - LAG0) % R0
                    if within(t, NT0):
                        need(sp, M0.xt_full, t - R0 + 1)
                        sp.dma_start(xs[r][:, :, :], buf0[bass.ds(t * 2 * P, 2 * P), :]
                                     .rearrange("(h p) d -> p h d", p=P)).then_inc(M0.xs_in[r], 16)
                    if within(t - LAG0, NT0):
                        sp.wait_ge(M0.y_evac, t - LAG0 + 1)
                        sp.dma_start(eo0[bass.ds((t - LAG0) * 2 * P, 2 * P), :].rearrange("(h p) d -> p h d", p=P),
                                     ysb[rs][:, :, :]).then_inc(M0.y_out[rs], 16)
                over_tiles0(sp, body, LAG0)
                attention(L1, fill1, "v1")
                sp.wait_ge(M1.scattered, 16 * NB)

                def body(i, u):
                    t, us = R1 * i + u, (u - LAG1) % R1
                    if within(t, NT1):
                        need(sp, M1.xt_full, t - R1 + 1)
                        sp.dma_start(xs[u][:, 0, :], buf1[bass.ds(t * P, P), :]).then_inc(M1.xs_in[u], 16)
                    if within(t - LAG1, NT1):
                        sp.wait_ge(M1.y_evac, t - LAG1 + 1)
                        sp.dma_start(eo1[bass.ds((t - LAG1) * P, P), :], ysb[us][:, 0, :]).then_inc(M1.y_out[us], 16)
                over_tiles1(sp, body, LAG1)
                for n in range(OPARTS):
                    sp.wait_ge(g_used, (n + 1) * OB)
                    bs = slice(n * OB, (n + 1) * OB)
                    sp.dma_start(out[:, bs, :], x[:, bs, :]).then_inc(stored, 16)
                sp.wait_ge(stored, 16 * OPARTS)

            @block.gpsimd
            def _(pool):
                for p in range(2):
                    for part in range(2):
                        nc.gpsimd.memset(va0[p][part][:, :, D0:D0 + 1], 1.0 - part).then_inc(const_done, 1)
                        nc.gpsimd.memset(va1[p][part][:, :, D1:D1 + 1], 1.0 - part).then_inc(const_done, 1)
                pool.wait_ge(loaded, NLOAD)
                nc.gpsimd.tensor_copy(mask[:, :], mask8[:, :]).then_inc(masked, 1)

                def norm(n):
                    even, odd, c = 1, 4, slice(n * XB, (n + 1) * XB)
                    steps = [0]

                    def step(ins):
                        steps[0] += 1
                        ins.then_inc(ln_step, 1)
                        pool.wait_ge(ln_step, 10 * n + steps[0])
                    tt, ts = nc.gpsimd.tensor_tensor, nc.gpsimd.tensor_scalar
                    pool.wait_ge(stat_done, XB * (n + 1))
                    step(tt(ln[0][:, c], stats[:, c, even], stats[:, c, odd], ALU.add))
                    step(ts(mean[:, c], ln[0][:, c], 0.5, None, ALU.mult))
                    step(tt(ln[1][:, c], stats[:, c, even], stats[:, c, odd], ALU.subtract))
                    step(tt(ln[2][:, c], ln[1][:, c], ln[1][:, c], ALU.mult))
                    step(ts(ln[3][:, c], ln[2][:, c], 0.25, EPS, ALU.mult, ALU.add))
                    step(tt(ln[0][:, c], stats[:, c, even + 1], stats[:, c, odd + 1], ALU.add))
                    step(ts(ln[1][:, c], ln[0][:, c], 1.0 / DM, None, ALU.mult))
                    step(tt(ln[2][:, c], ln[1][:, c], ln[3][:, c], ALU.add))
                    step(tt(ln[0][:, c], ln[2][:, c], mhalf[:, c], ALU.pow))
                    step(tt(rstd[:, c], ln[0][:, c], mask[:, c], ALU.mult))
                    nc.gpsimd.sem_inc(rstd_done, 1)
                pool.wait_ge(masked, 1)
                norm(0)
                nc.gpsimd.tensor_copy(identb[:, :], ident[:, :]).then_inc(const_done, 1)
                nc.gpsimd.tensor_copy(sel[:, :, :], selw[:, :, :]).then_inc(const_done, 1)
                nc.gpsimd.tensor_copy(tri[:, :], triw[:, :]).then_inc(const_done, 1)
                nc.gpsimd.memset(ones[:, :], 1.0).then_inc(const_done, 1)

                def indices(t, p):
                    for k in range(2):
                        nc.gpsimd.tensor_copy(gidx[p][k][:, :], slot[k][:, bass.ds(t, 1)]).then_inc(idx_done, 1)

                def fetch(p):
                    for k in range(2):
                        nc.gpsimd.indirect_dma_start(
                            out=gb[2 * p + k][:, :], out_offset=None, in_=eo0[:, :],
                            in_offset=bass.IndirectOffsetOnAxis(ap=gidx[p][k][:, 0:1], axis=0)).then_inc(e_in[p][k], 16)

                def attention(L, fill, layer):
                    def body(i, off):
                        b = 2 * i + off
                        t, pt = b + 4, off % 2
                        if layer == 0 and isinstance(b, int) and 1 <= b < XPARTS:
                            norm(b)
                        for g in range(NQ):
                            Q = NQ * b + g
                            if layer == 1 and g == 0 and inside(t):
                                need(pool, e_used, 2 * (t - 1))
                            if layer == 1 and g == 1 and inside(t):
                                pool.wait_ge(idx_done, 2 * (t + 1))
                            if layer == 1 and g == 1 and inside(b + 2):
                                pool.wait_ge(ve_done, b + 3)
                                need(pool, L.xn_ready, b + 1)
                                nc.gpsimd.tensor_tensor(rs[pt][:, :], ve[pt][:, :], mhalf[:, 0:1], ALU.pow)\
                                    .then_inc(rs_done, 1)
                            gr, ahead = NORM_AT[layer]["root"]
                            if g == gr and inside(b + ahead):
                                n, pr_ = b + ahead, (off + ahead) % 2
                                pool.wait_ge(L.part_done["eps"], n + 1)
                                need(pool, L.part_done["normed"], n - 1)
                                if layer == 1:
                                    need(pool, L.kept, n - 1)
                                nc.gpsimd.tensor_tensor(rsF[pr_][:, :], veF[pr_][:, :], mhalf[:, 0:1], ALU.pow)\
                                    .then_inc(L.part_done["root"], 1)
                            if layer == 0 and g == 1 and inside(b - 3):
                                pool.wait_ge(L.part_done["normed"], b - 2)
                                nc.gpsimd.tensor_copy(xna0[:, b - 3, :], xnF[(off - 3) % 2][:, :]).then_inc(L.kept, 1)
                            if inside(b):
                                pool.wait_ge(L.exp_done, Q + 1)
                                pool.wait_ge(L.ph_done, Q + 1)
                                need(pool, L.pv_full, Q - 3)
                                nc.gpsimd.tensor_tensor(pl[g][:, :, :], pT[g % 2][:, :, :], ph[g][:, :, :],
                                                        ALU.subtract).then_inc(L.pl_done, 1)
                            if layer == 1 and g == 0 and inside(t):
                                indices(t, pt)
                            if layer == 1 and g == 1 and inside(t):
                                fetch(pt)
                    over_batches(pool, body)
                attention(L0, fill0, 0)

                def scatter(M, ks, src, buf, bound):
                    for k in ks:
                        pool.wait_ge(slots_ready, k + 1)
                        for b in range(NB):
                            if src is xna:
                                pool.wait_ge(M.xr_copied, b + 1)
                            nc.gpsimd.indirect_dma_start(
                                out=buf[:, :], out_offset=bass.IndirectOffsetOnAxis(ap=slot[k][:, b:b + 1], axis=0),
                                in_=src[:, b, :], in_offset=None, bounds_check=bound, oob_is_err=False)\
                                .then_inc(M.scattered, 16)

                def gather(k, src):
                    for b in range(NB):
                        if b >= RING:
                            pool.wait_ge(g_used, b - RING + 1)
                        nc.gpsimd.indirect_dma_start(
                            out=gb[b % RING][:, :], out_offset=None, in_=src[:, :],
                            in_offset=bass.IndirectOffsetOnAxis(ap=slot[k][:, b:b + 1], axis=0))\
                            .then_inc(g_in[b % RING], 16)
                pool.wait_ge(zeroed[0], 16 * NZERO[0])
                pool.wait_ge(L0.kept, NB)
                scatter(M0, (0, 1), xna0, buf0, ZROW - 1)
                for r in range(R0):
                    pool.wait_ge(M0.y_out[r], 16 * NT0 // R0)
                indices(0, 0)
                pool.wait_ge(idx_done, 2)
                fetch(0)
                pool.wait_ge(L0.st_full, NB * NQ)
                for p in range(2):
                    nc.gpsimd.memset(qpad[p][:, :, :], 0.0).then_inc(qpad_zero, 1)
                attention(L1, fill1, 1)
                pool.wait_ge(zeroed[1], 16 * NZERO[1])
                scatter(M1, (2,), xna, buf1, NT1 * P - 1)
                for u in range(R1):
                    pool.wait_ge(M1.y_out[u], 16 * NT1 // R1)
                gather(2, eo1)

            @block.tensor
            def _(pe):
                pe.wait_ge(loaded, NLOAD)

                def shifted(Q, g, j, last):
                    return nc.tensor.matmul(st_bank[g % 2][:, j * P:(j + 1) * P], sel[:, j, :], cT[g % 2][:, :],
                                            start=False, stop=last)

                def attention(L, fill, layer):
                    D = (D0, D1)[layer]

                    def evacuated(i, off, name):
                        bk, k = fill(i, off, name)
                        pe.wait_ge(L.pj_free[bk], k + 1)

                    def project(i, off, name, ahead):
                        b, p = 2 * i + off + ahead, (off + ahead) % 2
                        if not inside(b):
                            return
                        bk, k = fill(i, off, name)
                        need(pe, L.pj_free[bk], k)
                        ps = pj_bank[bk]
                        what, half = name[0], int(name[-1] == "1")
                        if name == "xT":
                            pe.wait_ge(L.xn_ready, b + 1)
                            last = nc.tensor.transpose(ps[:, 0:P], xn[p][:, :], ident[:, :])
                        elif what == "o":
                            pe.wait_ge(L.pv_free, NQ * b + 2 * half + 2)
                            for c in range(4):
                                last = nc.tensor.transpose(ps[:, c * P:(c + 1) * P],
                                                           o1[p][:, 8 * half + 2 * c:8 * half + 2 * c + 2, :], ident[:, :])
                        elif name == "rT":
                            pe.wait_ge(L.part_done["normed"], b + 1)
                            last = nc.tensor.transpose(ps[:, 0:P], xnF[p][:, :], ident[:, :])
                        elif name == "lg":
                            evacuated(i, off, "rT")
                            last = nc.tensor.matmul(ps[:, 0:(E0, E1)[layer]], xrT[p][:, :], rw[layer][:, :],
                                                    start=True, stop=True)
                        elif name == "y":
                            evacuated(i, off - 1, "oT1")
                            for c in range(NCH):
                                last = nc.tensor.matmul(ps[:, 0:DM], oT[:, c, :], wo1[:, c, :],
                                                        start=(c == 0), stop=(c == NCH - 1))
                        else:
                            if name in ("q", "q0"):
                                evacuated(i, off - layer, "xT")
                            if name in ("k", "k0"):
                                pe.wait_ge(L.ctx_in[p], 16 * (i + (off + 1) // 2 + 1))
                            if layer == 0 and what == "v":
                                last = nc.tensor.matmul(ps[:, 0:P], ctxT[p][:, :], wv0[:, :], start=True, stop=True)
                            elif what == "v":
                                last = nc.tensor.matmul(ps[:, :], ctxT[p][:, :], wv1[:, 512 * half:512 * (half + 1)],
                                                        start=True, stop=True)
                            else:
                                w = ((wq0, wk0), (wq1, wk1))[layer][what == "k"]
                                rhs = xnT[p] if what == "q" else ctxT[p]
                                for c in range(4 if layer else 1):
                                    n = 4 * half + c
                                    last = nc.tensor.matmul(ps[:, c * P:(c + 1) * P], w[:, n * P:(n + 1) * P],
                                                            rhs[:, :], start=True, stop=True)
                        last.then_inc(L.pj_full[bk], 1)

                    def body(i, off):
                        b = 2 * i + off
                        p, pn = off % 2, (off + 1) % 2
                        if layer == 0 and isinstance(b, int) and b == -1:
                            pe.wait_ge(const_done, 12)
                        for g in range(NQ):
                            Q = NQ * b + g
                            fills = FILLS[layer][g]
                            for name, ahead in fills[:FRONT[layer][g]]:
                                project(i, off, name, ahead)

                            st = st_bank[g % 2]
                            if inside(b):
                                need(pe, L.exp_done, Q - 1)
                                if layer == 0:
                                    need(pe, L.ph_done, Q - 1)
                                    nc.tensor.matmul(st[:, :], kT[p][:, 0, :], qpad[p][:, QH * g:QH * (g + 1), :],
                                                     start=True, stop=False)
                                else:
                                    for c in range(2):
                                        nc.tensor.matmul(st[:, 2 * c * P:2 * (c + 1) * P], kT[p][:, 2 * g + c, :],
                                                         qpad[p][:, QH * g + 2 * c:QH * g + 2 * c + 2, :],
                                                         start=(c == 0), stop=False)

                            if inside(b + (g + 1) // NQ):
                                pe.wait_ge(L.max_done, Q + 2)
                                need(pe, L.c_free, Q + 1)
                                nc.tensor.transpose(cbank[0:QH, 0:P], cm[(g + 1) % 2][:, :], identb[:, :])\
                                    .then_inc(L.c_full, 1)

                            if inside(b):
                                pe.wait_ge(L.c_free, Q + 1)
                                for j in range(QH):
                                    last = nc.tensor.matmul(st[:, j * P:(j + 1) * P], sel[:, j, :], cT[g % 2][:, :],
                                                            start=False, stop=(j == QH - 1))
                                last.then_inc(L.st_full, 1)

                            bs, gs = b + (g + 2) // NQ, (g + 2) % NQ
                            ps_ = p if g < 2 else pn
                            if inside(bs):
                                if layer == 0:
                                    pe.wait_ge(L.cast_done, NQ * bs + gs + 1)
                                    if gs == 0:
                                        evacuated(i, off, "k")
                                elif gs % 2 == 0:
                                    pe.wait_ge(L.cast_done, 4 * bs + gs + 2)
                                need(pe, L.max_done, Q + 1)
                                for j in range(QH):
                                    h = QH * gs + j
                                    last = nc.tensor.matmul(s_bank[g % 2][:, j * P:(j + 1) * P], qpadb[ps_][:, h, :],
                                                            kTb[ps_][:, h // 2 if layer else 0, :], start=True, stop=True)
                                last.then_inc(L.s_full, 1)

                            for name, ahead in fills[FRONT[layer][g]:]:
                                project(i, off, name, ahead)

                            bo, go = b + (g - 2) // NQ, (g - 2) % NQ
                            po = p if g > 1 else pn
                            if inside(bo):
                                pe.wait_ge(L.pl_done, Q - 1)
                                if go == 0:
                                    evacuated(i, off - 1, "v" if layer == 0 else "v1")
                                need(pe, L.pv_free, Q - 2)
                                for j in range(QH):
                                    if layer == 0:
                                        w = 2 * (D + 1)
                                        for n, pp in enumerate((ph, pl)):
                                            last = nc.tensor.matmul(o_bank[:, j * w:(j + 1) * w], pp[go][:, j, :],
                                                                    vv0[po][:, QH * go + j, :, :],
                                                                    start=(n == 0), stop=(n == 1))
                                        continue
                                    for n, (pp, part) in enumerate(((ph, 0), (ph, 1), (pl, 0), (pl, 1))):
                                        last = nc.tensor.matmul(o_bank[:, j * (D + 1):(j + 1) * (D + 1)],
                                                                pp[go][:, j, :], va1[po][part][:, QH * go + j, :],
                                                                start=(n == 0), stop=(n == 3))
                                last.then_inc(L.pv_full, 1)
                    over_batches(pe, body)
                attention(L0, fill0, 0)

                def shared(M):
                    def body(i, u):
                        b = 2 * i + u
                        if within(b, NB):
                            pe.wait_ge(M.xr_ready, b + 1)
                            need(pe, M.t_evac, b - 1)
                            nc.tensor.transpose(pj_bank[u][:, 0:P], xn[u][:, :], ident[:, :]).then_inc(M.t_full, 1)
                        if within(b - 1, NB):
                            pe.wait_ge(M.t_evac, b)
                            need(pe, M.sh_done, b - 2)
                            for c in range(4):
                                last = nc.tensor.matmul(s_bank[1 - u][:, c * P:(c + 1) * P], wgu[:, c * P:(c + 1) * P],
                                                        xnT[1 - u][:, :], start=True, stop=True)
                            last.then_inc(M.g_full, 1)
                        if within(b - 2, NB):
                            pe.wait_ge(M.sh_done, b - 1)
                            need(pe, M.sy_done, b - 3)
                            for c in range(2):
                                last = nc.tensor.matmul(st_bank[u][:, 0:DM], hT[u][:, c, 0:P], wdn[:, c, :],
                                                        start=(c == 0), stop=(c == 1))
                            last.then_inc(M.sy_full, 1)
                    over_pairs(pe, body)

                def ranks(n):
                    cols = (E0, E1)[n] * NB
                    flat = selb[:, 0:(E0, E1)[n], :].rearrange("p e b -> p (e b)")
                    pe.wait_ge(sel_ready, n + 1)
                    nc.tensor.matmul(s_bank[0][:, 0:cols], tri[:, :], flat, start=True, stop=True)
                    nc.tensor.matmul(s_bank[1][:, 0:cols], ones[:, :], flat, start=True, stop=True)\
                        .then_inc(rank_ready, 1)

                ranks(0)

                def body(i, j):
                    q, t = j % 2, 2 * PER * i + j
                    if within(t, NT0):
                        r = j % R0
                        pe.wait_ge(M0.xs_in[r], 16 * (2 * PER // R0 * i + j // R0 + 1))
                        need(pe, M0.xt_evac, t - 1)
                        for h in range(2):
                            last = nc.tensor.transpose(pj_bank[q][:, h * P:(h + 1) * P], xs[r][:, h, :], ident[:, :])
                        last.then_inc(M0.xt_full, 1)
                    if within(t - 1, NT0):
                        jj, ii = (j - 1) % (2 * PER), i if j else i - 1
                        u = jj // PER
                        pe.wait_ge(M0.w_in[u], 64 * (ii + 1))
                        pe.wait_ge(M0.xt_evac, t)
                        need(pe, M0.h_done, t - 2)
                        for f in range(2):
                            last = nc.tensor.matmul(s_bank[1 - q][:, 2 * f * P:2 * (f + 1) * P],
                                                    w1s[u][:, f * P:(f + 1) * P], xsT[1 - q][:, :, :],
                                                    start=True, stop=True)
                        last.then_inc(M0.h_full, 1)
                    if within(t - 2, NT0):
                        u = (j - 2) % (2 * PER) // PER
                        pe.wait_ge(M0.h_done, t - 1)
                        need(pe, M0.y_evac, t - 3)
                        for h in range(2):
                            for f in range(2):
                                last = nc.tensor.matmul(st_bank[q][:, h * DM:(h + 1) * DM],
                                                        hT[q][:, f, h * P:(h + 1) * P], w2s[u][:, f, :],
                                                        start=(f == 0), stop=(f == 1))
                        last.then_inc(M0.y_full, 1)
                over_tiles0(pe, body)
                pe.wait_ge(qpad_zero, 2)
                pe.wait_ge(later_loaded, NLATER)
                attention(L1, fill1, 1)
                ranks(1)
                pe.wait_ge(experts_loaded, NEXPERTS)
                shared(M1)
                pe.wait_ge(slots_ready, 3)

                now = [pe.alloc_register(f"expert{u}") for u in range(R1)]
                before = [pe.alloc_register(f"expert_before{u}") for u in range(R1)]

                def expert_of(u):
                    return pe.snap((now[u] if u >= 0 else before[u + R1]), min_val=0, max_val=E1 - 1)

                def body(i, u):
                    t, q = R1 * i + u, u % 2
                    if u == 0:
                        if within(t - 1, NT1):
                            for k in range(1, R1):
                                pe.reg_mov(before[k], now[k])
                        if within(t, NT1):
                            pe.load(now, tei[0:1, bass.ds(t, R1)])
                    if within(t, NT1):
                        pe.wait_ge(M1.xs_in[u], 16 * (i + 1))
                        need(pe, M1.xt_evac, t - 1)
                        nc.tensor.transpose(pj_bank[q][:, 0:P], xs[u][:, 0, :], ident[:, :]).then_inc(M1.xt_full, 1)
                    if within(t - 1, NT1):
                        e = expert_of(u - 1)
                        pe.wait_ge(M1.xt_evac, t)
                        need(pe, M1.h_done, t - 2)
                        nc.tensor.matmul(s_bank[1 - q][:, :], xsT[1 - q][:, 0, :], gu[:, bass.ds(e, 1), :].squeeze(1),
                                         start=True, stop=True).then_inc(M1.h_full, 1)
                    if within(t - 2, NT1):
                        pe.wait_ge(M1.h_done, t - 1)
                        need(pe, M1.ht_evac, t - 3)
                        for f in range(2):
                            last = nc.tensor.transpose(st_bank[q][:, f * P:(f + 1) * P], hid[q][:, f * P:(f + 1) * P],
                                                       ident[:, :])
                        last.then_inc(M1.ht_full, 1)
                    if within(t - 3, NT1):
                        e = expert_of(u - 3)
                        pe.wait_ge(M1.ht_evac, t - 2)
                        need(pe, M1.y_evac, t - 3)
                        for f in range(2):
                            last = nc.tensor.matmul(o_bank[:, 0:DM], hT[1 - q][:, f, 0:P],
                                                    dn[:, bass.ds(e, 1), f, :].squeeze(1),
                                                    start=(f == 0), stop=(f == 1))
                        last.then_inc(M1.y_full, 1)
                over_tiles1(pe, body, 3)

            @block.scalar
            def _(act):
                for dst, name in ((ident, "ident"), (mask8, "mask"), (mhalf, "mhalf"), (wq0, "wq0"), (wk0, "wk0"),
                                  (wv0, "wv0"), (hmask, "hmask"), (selw, "sel"), (triw, "tri"), (rw[0], "rw0")):
                    act.dma_start(dst[(slice(None),) * len(dst.shape)], a[name]).then_inc(loaded, 16)

                def attention(L, fill, layer):
                    D = (D0, D1)[layer]

                    def take(i, off, name, ahead):
                        b, p = 2 * i + off + ahead, (off + ahead) % 2
                        if name == "y" or not inside(b):
                            return
                        bk, k = fill(i, off, name)
                        act.wait_ge(L.pj_full[bk], k + 1)
                        ps, what, half = pj_bank[bk], name[0], int(name[-1] == "1")
                        if name == "xT":
                            if inside(b - 2):
                                bq, kq = fill(i, off - 2, "q") if layer == 0 else fill(i, off - 1, "q1")
                                need(act, L.pj_full[bq], kq + 1)
                            nc.scalar.copy(xnT[p][:, :], ps[:, 0:P]).then_inc(L.pj_free[bk], 1)
                        elif name == "rT":
                            nc.scalar.copy(xrT[p][:, :], ps[:, 0:P]).then_inc(L.pj_free[bk], 1)
                        elif name == "lg":
                            E = (E0, E1)[layer]
                            nc.scalar.copy(lg[:, 0:E, bass.ds(b, 1)].squeeze(2), ps[:, 0:E]).then_inc(L.pj_free[bk], 1)
                        elif name == "q":
                            need(act, L.qpad_done, NQ * (b - 1))
                            nc.scalar.copy(qT[p][:, :], ps[:, 0:P]).then_inc(L.pj_free[bk], 1)
                        elif what == "q":
                            need(act, L.st_full, NQ * (b - 1))
                            for r in range(2):
                                rows = slice(D1 * r, D1 * (r + 1))
                                dst = qpad[p][rows, :, :].rearrange("p (c r) n -> p c r n", r=2)
                                last = nc.scalar.copy(dst[:, 4 * half:4 * half + 4, r, :],
                                                      ps[rows, :].rearrange("p (c n) -> p c n", c=4))
                            last.then_inc(L.pj_free[bk], 1)
                        elif what == "k":
                            need(act, L.st_full, NQ * (b - 1))
                            n = 4 if layer else 1
                            if layer == 0:
                                need(act, L.s_full, NQ * (b - 1))
                                nc.scalar.copy(kTb[p][:, 0, :], ps[:, 0:P])
                            nc.scalar.copy(kT[p][:, 4 * half:4 * half + n, :], ps[:, 0:n * P])\
                                .then_inc(L.pj_free[bk], 1)
                        elif what == "v":
                            need(act, L.pv_full, NQ * (b - 1))
                            n = NH // 2 if layer else NH
                            nc.scalar.copy((va0, va1)[layer][p][0][:, n * half:n * half + n, 0:D],
                                           ps[:, 0:n * D].rearrange("p (h d) -> p h d", d=D)).then_inc(L.vh_done, 1)
                        else:
                            if inside(b - 1):
                                by, ky = fill(i, off, "y")
                                need(act, L.pj_full[by], ky + 1)
                            nc.scalar.copy(oT[:, 4 * half:4 * half + 4, :], ps[:, :]).then_inc(L.pj_free[bk], 1)

                    def body(i, off):
                        b = 2 * i + off
                        pn = (off + 1) % 2
                        for g in range(NQ):
                            Q = NQ * b + g
                            fills = FILLS[layer][g]
                            for name, ahead in fills[:FRONT[layer][g]]:
                                take(i, off, name, ahead)
                            if inside(b + (g + 1) // NQ):
                                act.wait_ge(L.c_full, Q + 2)
                                need(act, L.st_full, Q)
                                nc.scalar.copy(cT[(g + 1) % 2][:, :], cbank[0:QH, 0:P]).then_inc(L.c_free, 1)
                            if layer == 0:
                                bq, gq = (b, 3) if g == 0 else (b + 1, g - 1)
                                pq = off % 2 if g == 0 else pn
                                if inside(bq):
                                    act.wait_ge(L.qpad_done, NQ * bq + gq + 1)
                                    need(act, L.s_full, NQ * (bq - 2) + gq + 1)
                                    hs = slice(QH * gq, QH * gq + QH)
                                    nc.scalar.copy(qpadb[pq][:, hs, :], qpad[pq][:, hs, :]).then_inc(L.cast_done, 1)
                            if inside(b):
                                act.wait_ge(L.st_full, Q + 1)
                                need(act, L.pl_done, Q - 1)
                                nc.scalar.activation(pT[g % 2][:, :, :], st_bank[g % 2][:, :], ACT.Exp, scale=D ** -0.5)\
                                    .then_inc(L.exp_done, 1)
                                if layer == 0:
                                    need(act, L.pv_full, Q - 3)
                                    nc.scalar.activation(ph[g][:, :, :], st_bank[g % 2][:, :], ACT.Exp,
                                                         scale=D ** -0.5).then_inc(L.ph_done, 1)
                            for name, ahead in fills[FRONT[layer][g]:]:
                                take(i, off, name, ahead)
                    over_batches(act, body)
                attention(L0, fill0, 0)

                def shared(M):
                    def body(i, u):
                        b = 2 * i + u
                        if within(b, NB):
                            act.wait_ge(M.t_full, b + 1)
                            need(act, M.g_full, b - 1)
                            nc.scalar.copy(xnT[u][:, :], pj_bank[u][:, 0:P]).then_inc(M.t_evac, 1)
                        if within(b - 1, NB):
                            act.wait_ge(M.g_full, b)
                            need(act, M.sh_done, b - 2)
                            nc.scalar.activation(sg[1 - u][:, :, :], s_bank[1 - u][:, 0:2 * P], ACT.Silu)\
                                .then_inc(M.sg_done, 1)
                    over_pairs(act, body)

                act.wait_ge(exp_in, 1)
                nc.scalar.activation(pr[:, 0:E0, :], wk[:, 0:E0, :], ACT.Exp).then_inc(exp_out, 1)

                def body(i, j):
                    q, t = j % 2, 2 * PER * i + j
                    if within(t, NT0):
                        act.wait_ge(M0.xt_full, t + 1)
                        need(act, M0.h_full, t - 1)
                        nc.scalar.copy(xsT[q][:, :, :], pj_bank[q][:, 0:2 * P]).then_inc(M0.xt_evac, 1)
                    if within(t - 1, NT0):
                        u = (j - 1) % (2 * PER) // PER
                        act.wait_ge(M0.h_full, t)
                        need(act, M0.y_full, t - 2)
                        for f in range(2):
                            last = nc.scalar.activation(hT[1 - q][:, f, :], s_bank[1 - q][:, 2 * f * P:2 * (f + 1) * P],
                                                        ACT.Gelu, bias=b1s[u][:, f:f + 1])
                        last.then_inc(M0.h_done, 1)
                over_tiles0(act, body)
                act.wait_ge(qpad_zero, 2)
                attention(L1, fill1, 1)
                act.wait_ge(exp_in, 2)
                nc.scalar.activation(v2[:, :], v1[:, :], ACT.Exp, scale=-1.0).then_inc(exp_out, 1)
                shared(M1)

                def body(i, u):
                    t, q = R1 * i + u, u % 2
                    if within(t, NT1):
                        act.wait_ge(M1.xt_full, t + 1)
                        need(act, M1.h_full, t - 1)
                        nc.scalar.copy(xsT[q][:, 0, :], pj_bank[q][:, 0:P]).then_inc(M1.xt_evac, 1)
                    if within(t - 1, NT1):
                        act.wait_ge(M1.h_full, t)
                        need(act, M1.h_done, t - 2)
                        nc.scalar.activation(sg[1 - q][:, :, :], s_bank[1 - q][:, 0:2 * P], ACT.Silu)\
                            .then_inc(M1.h_act, 1)
                    if within(t - 2, NT1):
                        act.wait_ge(M1.ht_full, t - 1)
                        need(act, M1.y_full, t - 4 + 1)
                        nc.scalar.copy(hT[q][:, :, 0:P], st_bank[q][:, 0:2 * P]).then_inc(M1.ht_evac, 1)
                over_tiles1(act, body, 2)

            @block.vector
            def _(dve):
                def stat(b):
                    nc.vector.bn_stats(stats[:, b, :], x[:, b, :]).then_inc(stat_done, 1)
                def part_stats(n):
                    dve.wait_ge(x_in[n], 16)
                    for b in range(n * XB, (n + 1) * XB):
                        stat(b)
                part_stats(0)
                dve.wait_ge(loaded, NLOAD)
                dve.wait_ge(rstd_done, 1)

                def attention(L, fill, layer):
                    D = (D0, D1)[layer]

                    def normed(b, p):
                        if layer == 1:
                            dve.wait_ge(rs_done, b + 1)
                        m = mv[p][:, 0:1] if layer else mean[:, bass.ds(b, 1)]
                        r = rs[p][:, :] if layer else rstd[:, bass.ds(b, 1)]
                        nc.vector.tensor_scalar(xn[p][:, :], x[:, b, :], m, r,
                                                ALU.subtract, ALU.mult).then_inc(L.xn_ready, 1)

                    def moe_waits(i, off, g):
                        t, p, turn = 2 * i + off + 3, (off + 3) % 2, i + (off + 3) // 2
                        if inside(t):
                            if g < 2:
                                dve.wait_ge(e_in[p][g], 16 * (turn + 1))
                            if g == 1 or g == 2:
                                dve.wait_ge(e_used, 2 * t + g)
                            if g == 3:
                                dve.wait_ge(st_done, t + 1)
                        if g == 0 and inside(t - 1):
                            dve.wait_ge(mv_done, t)

                    def moe_added(i, off, g):
                        t, p = 2 * i + off + 3, (off + 3) % 2
                        if g < 2 and inside(t):
                            nc.vector.scalar_tensor_tensor(x[:, t, :], gb[2 * p + g][:, :], wt[g][:, bass.ds(t, 1)],
                                                           x[:, t, :], ALU.mult, ALU.add).then_inc(e_used, 1)
                        if g == 2 and inside(t):
                            nc.vector.bn_stats(st[p][:, :], x[:, t, :]).then_inc(st_done, 1)
                        if g == 3 and inside(t):
                            nc.vector.bn_aggr(mv[p][:, :], st[p][:, :]).then_inc(mv_done, 1)
                        if g == 0 and inside(t - 1):
                            nc.vector.tensor_scalar(ve[1 - p][:, :], mv[1 - p][:, 1:2], EPS, None, ALU.add)\
                                .then_inc(ve_done, 1)

                    def due(part, g, off, b):
                        at, ahead = NORM_AT[layer][part]
                        return (b + ahead, (off + ahead) % 2) if g == at and inside(b + ahead) else None

                    def norm_waits(i, g, off, b):
                        for part, before in (("stats", L.x_done), ("aggr", L.part_done["stats"]),
                                             ("eps", L.part_done["aggr"]), ("normed", L.part_done["root"])):
                            if due(part, g, off, b):
                                n, p = due(part, g, off, b)
                                dve.wait_ge(before, n + 1)
                                if part == "eps":
                                    need(dve, L.part_done["root"], n - 1)
                                if part == "normed" and inside(n - 2):
                                    bt, kt = fill(i, off - 2 + layer, "rT")
                                    need(dve, L.pj_full[bt], kt + 1)
                                    if layer == 0:
                                        need(dve, L.kept, n - 1)

                    def next_norm(g, off, b):
                        if due("stats", g, off, b):
                            n, p = due("stats", g, off, b)
                            nc.vector.bn_stats(stF[p][:, :], x[:, n, :]).then_inc(L.part_done["stats"], 1)
                        if due("aggr", g, off, b):
                            n, p = due("aggr", g, off, b)
                            nc.vector.bn_aggr(mvF[p][:, :], stF[p][:, :]).then_inc(L.part_done["aggr"], 1)
                        if due("eps", g, off, b):
                            n, p = due("eps", g, off, b)
                            nc.vector.tensor_scalar(veF[p][:, :], mvF[p][:, 1:2], EPS, None, ALU.add)\
                                .then_inc(L.part_done["eps"], 1)
                        if due("normed", g, off, b):
                            n, p = due("normed", g, off, b)
                            nc.vector.tensor_scalar(xnF[p][:, :], x[:, n, :], mvF[p][:, 0:1], rsF[p][:, :],
                                                    ALU.subtract, ALU.mult).then_inc(L.part_done["normed"], 1)
                            if layer == 1:
                                nc.vector.tensor_copy(mean[:, bass.ds(n, 1)], mvF[p][:, 0:1])
                                nc.vector.tensor_copy(rstd[:, bass.ds(n, 1)], rsF[p][:, :]).then_inc(L.kept, 1)

                    def evacuated(i, off, name):
                        bk, k = fill(i, off, name)
                        dve.wait_ge(L.pj_free[bk], k + 1)

                    def low_values(i, off, name, ahead):
                        b, p = 2 * i + off + ahead, (off + ahead) % 2
                        if not inside(b):
                            return
                        bk, k = fill(i, off, name)
                        n = 2 if layer else 1
                        half, nh = int(name == "v1"), NH // n
                        va = (va0, va1)[layer][p]
                        dve.wait_ge(L.vh_done, n * b + half + 1)
                        need(dve, L.pv_full, NQ * (b - 1))
                        nc.vector.tensor_tensor(va[1][:, nh * half:nh * half + nh, 0:D],
                                                pj_bank[bk][:, 0:nh * D].rearrange("p (h d) -> p h d", d=D),
                                                va[0][:, nh * half:nh * half + nh, 0:D], ALU.subtract)\
                            .then_inc(L.pj_free[bk], 1)

                    def body(i, off):
                        b = 2 * i + off
                        p, pn = off % 2, (off + 1) % 2
                        for g in range(NQ):
                            Q = NQ * b + g
                            if layer == 0:
                                bq, gq = (b, 3) if g == 0 else (b + 1, g - 1)
                                pq = p if g == 0 else pn
                                if inside(bq):
                                    if gq == 0:
                                        evacuated(i, off - 1, "q")
                                    need(dve, L.st_full, NQ * (bq - 2) + gq + 1)
                                    hs = slice(QH * gq, QH * gq + QH)
                                    nc.vector.tensor_tensor(qpad[pq][:, hs, :],
                                                            qT[pq][:, :].unsqueeze(1).broadcast_to([P, QH, P]),
                                                            hmask[:, hs].unsqueeze(2).broadcast_to([P, QH, P]),
                                                            ALU.mult).then_inc(L.qpad_done, 1)
                            elif g < 2 and inside(b + 1):
                                need(dve, L.s_full, NQ * b)
                                hs, cs = slice(8 * g, 8 * g + 8), slice(4 * g, 4 * g + 4)
                                evacuated(i, off, f"q{g}")
                                nc.vector.tensor_copy(qpadb[pn][:, hs, :], qpad[pn][:, hs, :]).then_inc(L.cast_done, 1)
                                evacuated(i, off, f"k{g}")
                                nc.vector.tensor_copy(kTb[pn][:, cs, :], kT[pn][:, cs, :]).then_inc(L.cast_done, 1)
                            if layer == 0 and g == 2 and inside(b - 1):
                                dve.wait_ge(L.pv_free, NQ * b)
                                need(dve, L.o_done, b - 1)
                                nc.vector.tensor_tensor(osum[:, :, :], oraw[:, :, 0, 0:D], oraw[:, :, 1, 0:D], ALU.add)
                                nc.vector.reciprocal(rden0[:, :], oraw[:, :, 0, D]).then_inc(L.rden_done, 1)
                            if layer == 0 and g == 3 and inside(b - 1):
                                dve.wait_ge(L.o_done, b)
                                nc.vector.tensor_tensor(x[:, b - 1, :], x[:, b - 1, :],
                                                        o0[:, :, :].rearrange("p h d -> p (h d)"), ALU.add)\
                                    .then_inc(L.x_done, 1)
                            if g == 1 + layer and inside(b + 2):
                                if inside(b):
                                    bx, kx = fill(i, off - 2, "xT")
                                    need(dve, L.pj_full[bx], kx + 1)
                                normed(b + 2, p)
                            if layer == 0 and g == 2:
                                low_values(i, off, "v", 1)
                            for name, ahead in FILLS[layer][g]:
                                if layer == 1 and name[0] == "v":
                                    low_values(i, off, name, ahead)
                            if layer == 1 and inside(b):
                                dve.wait_ge(L.exp_done, Q + 1)
                                need(dve, L.pv_full, Q - 3)
                                nc.vector.tensor_copy(ph[g][:, :, :], pT[g % 2][:, :, :]).then_inc(L.ph_done, 1)
                            if layer == 0 and g == 2 and inside(b - 1):
                                dve.wait_ge(L.rden_done, b)
                                need(dve, L.x_done, b - 1)
                                nc.vector.tensor_tensor(o0[:, :, :], osum[:, :, :],
                                                        rden0[:, :].unsqueeze(2).broadcast_to([P, NH, D]), ALU.mult)\
                                    .then_inc(L.o_done, 1)
                            norm_waits(i, g, off, b)
                            if layer == 1:
                                moe_waits(i, off, g)
                            if inside(b + (g + 2) // NQ):
                                dve.wait_ge(L.s_full, Q + 3)
                                need(dve, L.c_full, Q + 1)
                                nc.vector.reduce_max(cm[g % 2][:, :], s_bank[g % 2][:, :].rearrange("p (h k) -> p h k", h=QH),
                                                     AX.X).then_inc(L.max_done, 1)
                            next_norm(g, off, b)
                            if layer == 1:
                                moe_added(i, off, g)
                            if layer == 1 and g == 0 and inside(b - 2):
                                by, ky = fill(i, off, "y")
                                dve.wait_ge(L.pj_full[by], ky + 1)
                                nc.vector.tensor_tensor(ysum[:, :], pj_bank[by][:, 0:DM], bo1[:, :], ALU.add)\
                                    .then_inc(L.pj_free[by], 1)
                            if layer == 1 and g == 1 and inside(b - 2):
                                by, ky = fill(i, off, "y")
                                dve.wait_ge(L.pj_free[by], ky + 1)
                                nc.vector.tensor_tensor(x[:, b - 2, :], x[:, b - 2, :], ysum[:, :], ALU.add)\
                                    .then_inc(L.x_done, 1)
                            bo, go = b + (g - 2) // NQ, (g - 2) % NQ
                            po = p if g > 1 else pn
                            if layer == 0 and inside(bo):
                                dve.wait_ge(L.pv_full, Q - 1)
                                if go == 0:
                                    need(dve, L.o_done, bo)
                                nc.vector.tensor_copy(oraw[:, QH * go:QH * (go + 1), :, :], o_bank[:, 0:2 * QH * (D + 1)])\
                                    .then_inc(L.pv_free, 1)
                            elif inside(bo):
                                dve.wait_ge(L.pv_full, Q - 1)
                                ov = o_bank[:, 0:QH * (D + 1)].rearrange("p (h d) -> p h d", d=D + 1)
                                nc.vector.reciprocal(rden[:, :], ov[:, :, D]).then_inc(L.rden_done, 1)
                                dve.wait_ge(L.rden_done, Q - 1)
                                nc.vector.tensor_tensor(o1[po][:, QH * go:QH * (go + 1), :], ov[:, :, 0:D],
                                                        rden[:, :].unsqueeze(2).broadcast_to([P, QH, D]), ALU.mult)\
                                    .then_inc(L.pv_free, 1)
                            if layer == 0 and g == NQ - 1 and isinstance(b, int) and 0 <= b < XPARTS - 1:
                                part_stats(b + 1)
                            if layer == 0 and g == NQ - 1 and isinstance(b, int) and b == XPARTS:
                                dve.wait_ge(rstd_done, XPARTS)
                    over_batches(dve, body)
                attention(L0, fill0, 0)

                chain = [0]

                def link(ins):
                    chain[0] += 1
                    ins.then_inc(rt, 1)
                    dve.wait_ge(rt, chain[0])

                def logits_in(L, layer):
                    bk, k = fill_of(layer, (NB - 1) // 2, 1 - NORM_LG[layer], "lg")
                    dve.wait_ge(L.pj_free[bk], k + 1)

                def shared(M):
                    def body(i, u):
                        b = 2 * i + u
                        if within(b, NB):
                            nc.vector.tensor_scalar(xna[:, b, :], x[:, b, :], mean[:, bass.ds(b, 1)],
                                                    srstd[:, bass.ds(b, 1)], ALU.subtract, ALU.mult)\
                                .then_inc(M.xr_copied, 1)
                            need(dve, M.t_full, b - 1)
                            nc.vector.tensor_scalar(xn[u][:, :], x[:, b, :], mean[:, bass.ds(b, 1)],
                                                    rstd[:, bass.ds(b, 1)], ALU.subtract, ALU.mult)\
                                .then_inc(M.xr_ready, 1)
                        if within(b - 2, NB):
                            dve.wait_ge(M.sg_done, b - 1)
                            need(dve, M.sy_full, b - 3)
                            nc.vector.tensor_tensor(hT[u][:, :, 0:P], sg[u][:, :, :],
                                                    s_bank[u][:, 2 * P:4 * P].rearrange("p (c n) -> p c n", c=2),
                                                    ALU.mult).then_inc(M.sh_done, 1)
                        if within(b - 3, NB):
                            dve.wait_ge(M.sy_full, b - 2)
                            nc.vector.tensor_tensor(x[:, b - 3, :], x[:, b - 3, :], st_bank[1 - u][:, 0:DM], ALU.add)\
                                .then_inc(M.sy_done, 1)
                    over_pairs(dve, body, 3)

                def top(E, src, oh, best):
                    tt = nc.vector.tensor_tensor
                    by_token = "p e b -> p b e"
                    link(nc.vector.reduce_max(best[:, :], src[:, 0:E, :].rearrange(by_token), AX.X))
                    link(tt(wk[:, 0:E, :], src[:, 0:E, :], best[:, :].unsqueeze(1).broadcast_to([P, E, NB]), ALU.is_equal))
                    link(tt(wk[:, 0:E, :], wk[:, 0:E, :], rev[:, 0:E].unsqueeze(2).broadcast_to([P, E, NB]), ALU.mult))
                    link(nc.vector.reduce_max(v3[:, :], wk[:, 0:E, :].rearrange(by_token), AX.X))
                    link(tt(oh[:, 0:E, :], rev[:, 0:E].unsqueeze(2).broadcast_to([P, E, NB]),
                            v3[:, :].unsqueeze(1).broadcast_to([P, E, NB]), ALU.is_equal))

                def rank(n, E):
                    tt = nc.vector.tensor_tensor
                    dve.wait_ge(rank_ready, n + 1)
                    fl = "p e b -> p (e b)"
                    cols = E * NB
                    link(nc.vector.tensor_tensor_scan(wk[:, 0:E, :].rearrange(fl), reset[:, 0:E, :].rearrange(fl),
                                                      s_bank[1][:, 0:cols], 0.0, ALU.mult, ALU.add))
                    link(tt(rk[:, 0:E, :].rearrange(fl), wk[:, 0:E, :].rearrange(fl), s_bank[1][:, 0:cols], ALU.subtract))
                    link(tt(rk[:, 0:E, :].rearrange(fl), rk[:, 0:E, :].rearrange(fl), s_bank[0][:, 0:cols], ALU.add))

                def to_slot(E, oh, k, add):
                    link(nc.vector.tensor_tensor(wk[:, 0:E, :], oh[:, 0:E, :], rk[:, 0:E, :], ALU.mult))
                    link(nc.vector.reduce_sum(v4[:, :], wk[:, 0:E, :].rearrange("p e b -> p b e"), AX.X))
                    nc.vector.tensor_scalar(slot[k][:, :], v4[:, :], float(add), None, ALU.add).then_inc(slots_ready, 1)

                def add_gathered():
                    for b in range(NB):
                        dve.wait_ge(g_in[b % RING], 16 * (b // RING + 1))
                        nc.vector.tensor_tensor(x[:, b, :], x[:, b, :], gb[b % RING][:, :], ALU.add).then_inc(g_used, 1)

                tt, ts = nc.vector.tensor_tensor, nc.vector.tensor_scalar
                dve.wait_ge(later_loaded, NLATER)
                logits_in(L0, 0)
                E = E0
                r = slice(0, E)
                link(tt(lg[:, r, :], lg[:, r, :], rb0[:, :].unsqueeze(2).broadcast_to([P, E, NB]), ALU.add))
                link(nc.vector.reduce_max(v1[:, :], lg[:, r, :].rearrange("p e b -> p b e"), AX.X))
                tt(wk[:, r, :], lg[:, r, :], v1[:, :].unsqueeze(1).broadcast_to([P, E, NB]), ALU.subtract)\
                    .then_inc(exp_in, 1)
                dve.wait_ge(exp_out, 1)
                link(nc.vector.reduce_sum(v2[:, :], pr[:, r, :].rearrange("p e b -> p b e"), AX.X))
                link(nc.vector.reciprocal(v3[:, :], v2[:, :]))
                link(tt(pr[:, r, :], pr[:, r, :], v3[:, :].unsqueeze(1).broadcast_to([P, E, NB]), ALU.mult))
                top(E, pr, oh1, v1)
                link(nc.vector.scalar_tensor_tensor(pr[:, r, :], oh1[:, r, :], -2.0, pr[:, r, :], ALU.mult, ALU.add))
                top(E, pr, oh2, v2)
                tt(selb[:, r, :], oh1[:, r, :], oh2[:, r, :], ALU.add).then_inc(sel_ready, 1)
                rank(0, E)
                link(ts(wk[:, r, :], rk[:, r, :], float(CAP), None, ALU.is_lt))
                link(tt(rk[:, r, :], rk[:, r, :], base0[:, :].unsqueeze(2).broadcast_to([P, E, NB]), ALU.add))
                link(tt(rk[:, r, :], rk[:, r, :], wk[:, r, :], ALU.mult))
                to_slot(E, oh1, 0, ZROW)
                to_slot(E, oh2, 1, ZROW)
                dve.wait_ge(slots_ready, 2)
                link(tt(v3[:, :], v1[:, :], v2[:, :], ALU.add))
                link(ts(v4[:, :], v3[:, :], 1e-9, None, ALU.max))
                link(nc.vector.reciprocal(v3[:, :], v4[:, :]))
                link(tt(wt[0][:, :], v1[:, :], v3[:, :], ALU.mult))
                link(tt(wt[1][:, :], v2[:, :], v3[:, :], ALU.mult))

                def body(i, j):
                    q, t = j % 2, 2 * PER * i + j
                    if within(t - 2, NT0):
                        u = (j - 2) % (2 * PER) // PER
                        dve.wait_ge(M0.y_full, t - 1)
                        r = (j - 2) % R0
                        if within(t - 2 - R0, NT0):
                            dve.wait_ge(M0.y_out[r], 16 * (2 * PER // R0 * i + (j - 2) // R0))
                        nc.vector.tensor_tensor(ysb[r][:, :, :], st_bank[q][:, 0:2 * DM].rearrange("p (h d) -> p h d", h=2),
                                                b2s[u][:, :].unsqueeze(1).broadcast_to([P, 2, DM]), ALU.add)\
                            .then_inc(M0.y_evac, 1)
                over_tiles0(dve, body)
                attention(L1, fill1, 1)
                logits_in(L1, 1)
                E = E1
                top(E, lg, oh1, v1)
                link(ts(selb[:, :, :], oh1[:, :, :], 1.0, None, ALU.mult))
                nc.vector.sem_inc(sel_ready, 1)
                nc.vector.sem_inc(exp_in, 1)
                dve.wait_ge(exp_out, 2)
                link(ts(v3[:, :], v2[:, :], 1.0, None, ALU.add))
                link(nc.vector.reciprocal(v4[:, :], v3[:, :]))
                dve.wait_ge(L1.kept, NB)
                link(tt(srstd[:, :], rstd[:, :], v4[:, :], ALU.mult))
                rank(1, E)
                link(tt(oh2[:, :, :], wk[:, :, NB - 1:NB].broadcast_to([P, E, NB]),
                        k128[:, :].unsqueeze(1).broadcast_to([P, E, NB]), ALU.is_gt))
                link(nc.vector.reduce_sum(ntile[:, :], oh2[:, :, :], AX.X))
                link(nc.vector.tensor_tensor_scan(tcum[:, :], reset[:, :, 1:2].rearrange("p e b -> p (e b)"),
                                                  ntile[:, :], 0.0, ALU.mult, ALU.add))
                link(tt(base1[:, :], tcum[:, :], ntile[:, :], ALU.subtract))
                link(ts(base1[:, :], base1[:, :], float(P), None, ALU.mult))
                link(tt(rk[:, :, :], rk[:, :, :], base1[:, :].unsqueeze(2).broadcast_to([P, E, NB]), ALU.add))
                tw = tile_past
                link(tt(tw, tiota[:, :].unsqueeze(2).broadcast_to([1, NT1, E]),
                        tcum[0:1, :].unsqueeze(1).broadcast_to([1, NT1, E]), ALU.is_ge))
                link(nc.vector.reduce_sum(tef[:, :], tw, AX.X))
                link(ts(tei[:, :], tef[:, :], float(E - 1), None, ALU.min))
                to_slot(E, oh1, 2, 0)
                dve.wait_ge(slots_ready, 3)
                shared(M1)

                def body(i, u):
                    t, q = R1 * i + u, u % 2
                    if within(t - 1, NT1):
                        dve.wait_ge(M1.h_act, t)
                        need(dve, M1.ht_full, t - 3 + 1)
                        nc.vector.tensor_tensor(hid[1 - q][:, :], sg[1 - q][:, :, :].rearrange("p c n -> p (c n)"),
                                                s_bank[1 - q][:, 2 * P:4 * P], ALU.mult).then_inc(M1.h_done, 1)
                    if within(t - 3, NT1):
                        dve.wait_ge(M1.y_full, t - 2)
                        r = (u - 3) % R1
                        if within(t - 3 - R1, NT1):
                            dve.wait_ge(M1.y_out[r], 16 * (i + (u - 3) // R1))
                        nc.vector.tensor_copy(ysb[r][:, 0, :], o_bank[:, 0:DM]).then_inc(M1.y_evac, 1)
                over_tiles1(dve, body, 3)
                add_gathered()


def kernel(x, ctx_768, mask_BxS_bk0, L0_xattn_Wq, L0_xattn_Wkv, L0_ffn_router_w, L0_ffn_router_b, L0_ffn_w1,
           L0_ffn_b1, L0_ffn_w2, L0_ffn_b2, L1_xattn_w_q, L1_xattn_w_k, L1_xattn_w_v, L1_xattn_w_out,
           L1_xattn_b_out, L1_ffn_w_router, L1_ffn_gate_up_proj, L1_ffn_down_proj, L1_ffn_w_gate, L1_ffn_w_up,
           L1_ffn_w_down):
    import concourse.bacc as bacc
    from concourse.bass_utils import run_bass_kernel_spmd as run

    def lay(v):
        return np.ascontiguousarray(v)

    x = np.asarray(x)
    head = np.zeros((QH, QH, P), np.float32)
    for j in range(QH):
        head[j, j] = -1.0
    hm = np.zeros((P, NH), np.float32)
    for h in range(NH):
        hm[D0 * h:D0 * (h + 1), h] = 1.0
    arrays = {
        "x": lay(x.transpose(1, 0, 2)),
        "ctxT": lay(np.asarray(ctx_768).transpose(2, 0, 1).reshape(DC, NB * P)),
        "mask": lay(np.asarray(mask_BxS_bk0).T),
        "wq0": lay(np.asarray(L0_xattn_Wq).T),
        "wk0": lay(np.asarray(L0_xattn_Wkv)[:DM].T),
        "wv0": lay(np.asarray(L0_xattn_Wkv)[DM:].T),
        "wq1": lay(np.asarray(L1_xattn_w_q)),
        "wk1": lay(np.asarray(L1_xattn_w_k)),
        "wv1": lay(np.asarray(L1_xattn_w_v)),
        "wo1": lay(np.asarray(L1_xattn_w_out).reshape(NCH, P, DM).transpose(1, 0, 2)),
        "bo1": lay(np.broadcast_to(np.asarray(L1_xattn_b_out), (P, DM))),
        "ident": np.eye(P, dtype=np.float32),
        "sel": head,
        "hmask": hm,
        "mhalf": np.full((P, NB), -0.5, np.float32),
        "tri": np.triu(np.ones((P, P), np.float32), 1),
        "rw0": lay(np.asarray(L0_ffn_router_w)),
        "rw1": lay(np.asarray(L1_ffn_w_router).T),
        "rb0": lay(np.broadcast_to(np.asarray(L0_ffn_router_b), (P, E0))),
        "rev": lay(np.broadcast_to(E1 - np.arange(E1, dtype=np.float32), (P, E1))),
        "base0": lay(np.broadcast_to(CAP * np.arange(E0, dtype=np.float32) - ZROW, (P, E0))),
        "k128": lay(np.broadcast_to(P * np.arange(NB, dtype=np.float32), (P, NB))),
        "tiota": np.arange(NT1, dtype=np.float32)[None],
        "reset": lay(np.broadcast_to((np.arange(NB) > 0).astype(np.float32), (P, E1, NB))),
        "gu": lay(np.asarray(L1_ffn_gate_up_proj).transpose(1, 0, 2)),
        "dn": lay(np.asarray(L1_ffn_down_proj).reshape(E1, 2, P, DM).transpose(2, 0, 1, 3)),
        "wgu": lay(np.concatenate([np.asarray(L1_ffn_w_gate).T, np.asarray(L1_ffn_w_up).T], 1)),
        "wdn": lay(np.asarray(L1_ffn_w_down).T.reshape(2, P, DM).transpose(1, 0, 2)),
        "zero": np.zeros((P, ZR * DM), np.float32),
        "w1": lay(np.asarray(L0_ffn_w1)),
        "w2": lay(np.asarray(L0_ffn_w2).reshape(E0, 2, P, DM).transpose(0, 2, 1, 3)),
        "b1": lay(np.asarray(L0_ffn_b1).reshape(E0, 2, P).transpose(0, 2, 1)),
        "b2": lay(np.broadcast_to(np.asarray(L0_ffn_b2)[:, None], (E0, P, DM))),
    }
    nc = bacc.Bacc("TRN2", target_bir_lowering=False, num_devices=1)
    a = {n: nc.dram_tensor(f"in_{n}", v.shape, mybir.dt.from_np(v.dtype), kind="ExternalInput").ap()
         for n, v in arrays.items()}
    out = nc.dram_tensor("out", (P, NB, DM), F32, kind="ExternalOutput").ap()
    build(nc, a, out)
    r = run(nc, [{f"in_{n}": v for n, v in arrays.items()}], core_ids=[0])
    return r.results[0]["out"].transpose(1, 0, 2)
```
